# Optimizing a Trainium2 kernel written in Bass

```python
import numpy as np
import jax
import jax.numpy as jnp

def _softmax(x, axis=-1):
    return jax.nn.softmax(x, axis=axis)
def _gelu(x):
    return jax.nn.gelu(x, approximate=True)
def _silu(x):
    return jax.nn.silu(x)
def _sigmoid(x):
    return jax.nn.sigmoid(x)
def _layernorm(x, axis=-1, eps=1e-5):
    m = jnp.mean(x, axis=axis, keepdims=True)
    v = jnp.var(x, axis=axis, keepdims=True)
    return (x - m) / jnp.sqrt(v + eps)
def _scatter_add(tgt, idx, src, axis=0):
    return tgt.at[idx].add(src)
def _segment_sum(src, seg, n):
    return jax.ops.segment_sum(src, seg, n)

kernel_name = 'mk_conv_attn_hybrid_d4_conv_nchw128_1f9ecd'

def setup_inputs(seed: int = 0):
    np.random.seed(seed)
    _w = jnp.asarray
    def _rec_inputs():
        import jax
        import jax.numpy as jnp
        _gk = jax.random.key(seed)
        x = -0.0005207 + 1.001 * jax.random.normal(jax.random.fold_in(_gk, 1), (4, 128, 64, 64), jnp.float32)
        return x
    x = _rec_inputs()
    def _L0_conv_setup():
        import jax, jax.numpy as jnp
        import numpy as np
        from jax import lax
        B_, C_, H_, W_ = (4, 128, 64, 64)
        D_INNER, D_STATE, DT_RANK, D_CONV = (256, 16, 8, 4)

        def _mamba2d(x, proj_w, in_proj_w, conv_w, conv_b, x_proj_w, dt_proj_w, dt_proj_b, A_log, D, out_proj_w):
            b, c, h, w = x.shape
            L = h * w
            u = jnp.einsum('oc,bchw->bohw', proj_w, x).reshape(b, c, L).transpose(0, 2, 1)
            xz = u @ in_proj_w.T
            xs, zg = (xz[..., :D_INNER], xz[..., D_INNER:])
            xt = xs.transpose(0, 2, 1)
            xt = lax.conv_general_dilated(xt, conv_w, window_strides=(1,), padding=[(D_CONV - 1, 0)], feature_group_count=D_INNER)
            xc = jax.nn.silu(xt + conv_b[None, :, None]).transpose(0, 2, 1)
            x_dbl = xc @ x_proj_w.T
            dt_r = x_dbl[..., :DT_RANK]
            Bm = x_dbl[..., DT_RANK:DT_RANK + D_STATE]
            Cm = x_dbl[..., DT_RANK + D_STATE:]
            delta = jax.nn.softplus(dt_r @ dt_proj_w.T + dt_proj_b)
            A = -jnp.exp(A_log)

            def step(hprev, inp):
                dt_t, B_t, C_t, x_t = inp
                dA = jnp.exp(dt_t[:, :, None] * A)
                hn = dA * hprev + (dt_t * x_t)[:, :, None] * B_t[:, None, :]
                y = jnp.einsum('bdn,bn->bd', hn, C_t)
                return (hn, y)
            h0 = jnp.zeros((b, D_INNER, D_STATE), xc.dtype)
            _, ys = lax.scan(step, h0, (delta.transpose(1, 0, 2), Bm.transpose(1, 0, 2), Cm.transpose(1, 0, 2), xc.transpose(1, 0, 2)))
            y = ys.transpose(1, 0, 2) + xc * D
            y = y * jax.nn.silu(zg)
            out = y @ out_proj_w.T
            return out.transpose(0, 2, 1).reshape(b, c, h, w) + x
        ks = jax.random.split(jax.random.key(seed), 12)

        def rn(k, shape, fan_in):
            return jax.random.normal(k, shape, jnp.float32) * fan_in ** (-0.5)
        return {'x': jax.random.normal(ks[0], (B_, C_, H_, W_), jnp.float32), 'proj_w': rn(ks[1], (C_, C_), C_), 'in_proj_w': rn(ks[2], (2 * D_INNER, C_), C_), 'conv_w': rn(ks[3], (D_INNER, 1, D_CONV), D_CONV), 'conv_b': jax.random.normal(ks[4], (D_INNER,), jnp.float32) * 0.02, 'x_proj_w': rn(ks[5], (DT_RANK + 2 * D_STATE, D_INNER), D_INNER), 'dt_proj_w': rn(ks[6], (D_INNER, DT_RANK), DT_RANK), 'dt_proj_b': jax.random.normal(ks[7], (D_INNER,), jnp.float32) * 0.1, 'A_log': jax.random.uniform(ks[8], (D_INNER, D_STATE), jnp.float32), 'D': jax.random.normal(ks[9], (D_INNER,), jnp.float32), 'out_proj_w': rn(ks[10], (C_, D_INNER), D_INNER)}
    _L0_conv_all = _L0_conv_setup()
    _L0_conv_in = {k: v for k, v in _L0_conv_all.items() if k in ('proj_w', 'in_proj_w', 'conv_w', 'conv_b', 'x_proj_w', 'dt_proj_w', 'dt_proj_b', 'A_log', 'D', 'out_proj_w', )}
    del _L0_conv_all

    def _L1_conv_setup():
        import jax, jax.numpy as jnp
        import numpy as np
        THRESHOLD = 16.0
        BN_EPS = 1e-05
        key = jax.random.key(seed)
        k_x, k_w, k_b, k_g, k_be = jax.random.split(key, 5)
        B, C, H, W = (4, 128, 64, 64)
        C2 = 128
        x = jax.random.normal(k_x, (B, C, H, W), dtype=jnp.float32)
        W_fc = jax.random.normal(k_w, (C2, C), dtype=jnp.float32) * (1.0 / np.sqrt(C))
        b_fc = jax.random.normal(k_b, (C2,), dtype=jnp.float32) * 0.01
        gamma = jnp.ones((C2,), dtype=jnp.float32) + 0.1 * jax.random.normal(k_g, (C2,), dtype=jnp.float32)
        beta = 0.1 * jax.random.normal(k_be, (C2,), dtype=jnp.float32)
        return {'x': x, 'W_fc': W_fc, 'b_fc': b_fc, 'gamma': gamma, 'beta': beta}
    _L1_conv_all = _L1_conv_setup()
    _L1_conv_in = {k: v for k, v in _L1_conv_all.items() if k in ('W_fc', 'b_fc', 'gamma', 'beta', )}
    del _L1_conv_all

    def _L2_attn_setup():
        import jax, jax.numpy as jnp
        import numpy as np
        B, T, D = (4, 2048, 128)
        key = jax.random.key(seed)
        k1, k2, k3 = jax.random.split(key, 3)
        x = jax.random.normal(k1, (B, T, D), dtype=jnp.float32)
        lim = 1.0 / np.sqrt(D)
        W = jax.random.uniform(k2, (3 * D, D), dtype=jnp.float32, minval=-lim, maxval=lim)
        b = jax.random.uniform(k3, (3 * D,), dtype=jnp.float32, minval=-lim, maxval=lim)
        return {'x': x, 'W': W, 'b': b}
    _L2_attn_all = _L2_attn_setup()
    _L2_attn_in = {k: v for k, v in _L2_attn_all.items() if k in ('W', 'b', )}
    del _L2_attn_all

    def _L2_ffn_setup():
        import jax, jax.numpy as jnp
        import numpy as np
        B, S, D, E, H, O, K = (512, 2048, 128, 64, 512, 128, 8)
        key = jax.random.key(seed)
        k0, k1, k2, k3 = jax.random.split(key, 4)
        x = jax.random.normal(k0, (B, S, D), dtype=jnp.float32)
        gate_w = jax.random.normal(k1, (E, D), dtype=jnp.float32) * (1.0 / np.sqrt(D))
        gate_b = jnp.zeros((E,), dtype=jnp.float32)
        weight1 = jax.random.uniform(k2, (E, D + 1, H), dtype=jnp.float32, minval=-1.0, maxval=1.0) * (1.0 / np.sqrt(D + 1))
        weight2 = jax.random.uniform(k3, (E, H + 1, O), dtype=jnp.float32, minval=-1.0, maxval=1.0) * (1.0 / np.sqrt(H + 1))
        return {'x': x, 'gate_w': gate_w, 'gate_b': gate_b, 'weight1': weight1, 'weight2': weight2}
    _L2_ffn_all = _L2_ffn_setup()
    _L2_ffn_in = {k: v for k, v in _L2_ffn_all.items() if k in ('gate_w', 'gate_b', 'weight1', 'weight2', )}
    del _L2_ffn_all

    def _L3_attn_setup():
        import jax, jax.numpy as jnp
        import numpy as np
        INPUT_DIM = 128
        HIDDEN_DIM = 128
        WINDOW_SIZE = 256
        BLOCK_SIZE = 256
        BATCH = 8
        SEQ = 8192
        key = jax.random.key(seed)
        ks = jax.random.split(key, 7)
        s = 1.0 / np.sqrt(INPUT_DIM)
        return {'x': jax.random.normal(ks[0], (BATCH, SEQ, INPUT_DIM), dtype=jnp.float32), 'Wq': jax.random.normal(ks[1], (HIDDEN_DIM, INPUT_DIM), dtype=jnp.float32) * s, 'bq': jax.random.normal(ks[2], (HIDDEN_DIM,), dtype=jnp.float32) * s, 'Wk': jax.random.normal(ks[3], (HIDDEN_DIM, INPUT_DIM), dtype=jnp.float32) * s, 'bk': jax.random.normal(ks[4], (HIDDEN_DIM,), dtype=jnp.float32) * s, 'Wv': jax.random.normal(ks[5], (HIDDEN_DIM, INPUT_DIM), dtype=jnp.float32) * s, 'bv': jax.random.normal(ks[6], (HIDDEN_DIM,), dtype=jnp.float32) * s}
    _L3_attn_all = _L3_attn_setup()
    _L3_attn_in = {k: v for k, v in _L3_attn_all.items() if k in ('Wq', 'bq', 'Wk', 'bk', 'Wv', 'bv', )}
    del _L3_attn_all

    def _L3_ffn_setup():
        import jax, jax.numpy as jnp
        import numpy as np
        B, S, D, E, H, O, K = (512, 2048, 128, 64, 512, 128, 8)
        key = jax.random.key(seed)
        k0, k1, k2, k3 = jax.random.split(key, 4)
        x = jax.random.normal(k0, (B, S, D), dtype=jnp.float32)
        gate_w = jax.random.normal(k1, (E, D), dtype=jnp.float32) * (1.0 / np.sqrt(D))
        gate_b = jnp.zeros((E,), dtype=jnp.float32)
        weight1 = jax.random.uniform(k2, (E, D + 1, H), dtype=jnp.float32, minval=-1.0, maxval=1.0) * (1.0 / np.sqrt(D + 1))
        weight2 = jax.random.uniform(k3, (E, H + 1, O), dtype=jnp.float32, minval=-1.0, maxval=1.0) * (1.0 / np.sqrt(H + 1))
        return {'x': x, 'gate_w': gate_w, 'gate_b': gate_b, 'weight1': weight1, 'weight2': weight2}
    _L3_ffn_all = _L3_ffn_setup()
    _L3_ffn_in = {k: v for k, v in _L3_ffn_all.items() if k in ('gate_w', 'gate_b', 'weight1', 'weight2', )}
    del _L3_ffn_all

    return {
        "x": x,
        "L0_conv_proj_w": _L0_conv_in["proj_w"],
        "L0_conv_in_proj_w": _L0_conv_in["in_proj_w"],
        "L0_conv_conv_w": _L0_conv_in["conv_w"],
        "L0_conv_conv_b": _L0_conv_in["conv_b"],
        "L0_conv_x_proj_w": _L0_conv_in["x_proj_w"],
        "L0_conv_dt_proj_w": _L0_conv_in["dt_proj_w"],
        "L0_conv_dt_proj_b": _L0_conv_in["dt_proj_b"],
        "L0_conv_A_log": _L0_conv_in["A_log"],
        "L0_conv_D": _L0_conv_in["D"],
        "L0_conv_out_proj_w": _L0_conv_in["out_proj_w"],
        "L1_conv_W_fc": _L1_conv_in["W_fc"],
        "L1_conv_b_fc": _L1_conv_in["b_fc"],
        "L1_conv_gamma": _L1_conv_in["gamma"],
        "L1_conv_beta": _L1_conv_in["beta"],
        "L2_attn_W": _L2_attn_in["W"],
        "L2_attn_b": _L2_attn_in["b"],
        "L2_ffn_gate_w": _L2_ffn_in["gate_w"],
        "L2_ffn_gate_b": _L2_ffn_in["gate_b"],
        "L2_ffn_weight1": _L2_ffn_in["weight1"],
        "L2_ffn_weight2": _L2_ffn_in["weight2"],
        "L3_attn_Wq": _L3_attn_in["Wq"],
        "L3_attn_bq": _L3_attn_in["bq"],
        "L3_attn_Wk": _L3_attn_in["Wk"],
        "L3_attn_bk": _L3_attn_in["bk"],
        "L3_attn_Wv": _L3_attn_in["Wv"],
        "L3_attn_bv": _L3_attn_in["bv"],
        "L3_ffn_gate_w": _L3_ffn_in["gate_w"],
        "L3_ffn_gate_b": _L3_ffn_in["gate_b"],
        "L3_ffn_weight1": _L3_ffn_in["weight1"],
        "L3_ffn_weight2": _L3_ffn_in["weight2"],
    }

def reference(x, L0_conv_proj_w, L0_conv_in_proj_w, L0_conv_conv_w, L0_conv_conv_b, L0_conv_x_proj_w, L0_conv_dt_proj_w, L0_conv_dt_proj_b, L0_conv_A_log, L0_conv_D, L0_conv_out_proj_w, L1_conv_W_fc, L1_conv_b_fc, L1_conv_gamma, L1_conv_beta, L2_attn_W, L2_attn_b, L2_ffn_gate_w, L2_ffn_gate_b, L2_ffn_weight1, L2_ffn_weight2, L3_attn_Wq, L3_attn_bq, L3_attn_Wk, L3_attn_bk, L3_attn_Wv, L3_attn_bv, L3_ffn_gate_w, L3_ffn_gate_b, L3_ffn_weight1, L3_ffn_weight2):
    import jax
    import jax.numpy as jnp
    def _L0_conv_ref(x, proj_w, in_proj_w, conv_w, conv_b, x_proj_w, dt_proj_w, dt_proj_b, A_log, D, out_proj_w):
        import jax, jax.numpy as jnp
        import numpy as np
        from jax import lax
        B_, C_, H_, W_ = (4, 128, 64, 64)
        D_INNER, D_STATE, DT_RANK, D_CONV = (256, 16, 8, 4)

        def _mamba2d(x, proj_w, in_proj_w, conv_w, conv_b, x_proj_w, dt_proj_w, dt_proj_b, A_log, D, out_proj_w):
            b, c, h, w = x.shape
            L = h * w
            u = jnp.einsum('oc,bchw->bohw', proj_w, x).reshape(b, c, L).transpose(0, 2, 1)
            xz = u @ in_proj_w.T
            xs, zg = (xz[..., :D_INNER], xz[..., D_INNER:])
            xt = xs.transpose(0, 2, 1)
            xt = lax.conv_general_dilated(xt, conv_w, window_strides=(1,), padding=[(D_CONV - 1, 0)], feature_group_count=D_INNER)
            xc = jax.nn.silu(xt + conv_b[None, :, None]).transpose(0, 2, 1)
            x_dbl = xc @ x_proj_w.T
            dt_r = x_dbl[..., :DT_RANK]
            Bm = x_dbl[..., DT_RANK:DT_RANK + D_STATE]
            Cm = x_dbl[..., DT_RANK + D_STATE:]
            delta = jax.nn.softplus(dt_r @ dt_proj_w.T + dt_proj_b)
            A = -jnp.exp(A_log)

            def step(hprev, inp):
                dt_t, B_t, C_t, x_t = inp
                dA = jnp.exp(dt_t[:, :, None] * A)
                hn = dA * hprev + (dt_t * x_t)[:, :, None] * B_t[:, None, :]
                y = jnp.einsum('bdn,bn->bd', hn, C_t)
                return (hn, y)
            h0 = jnp.zeros((b, D_INNER, D_STATE), xc.dtype)
            _, ys = lax.scan(step, h0, (delta.transpose(1, 0, 2), Bm.transpose(1, 0, 2), Cm.transpose(1, 0, 2), xc.transpose(1, 0, 2)))
            y = ys.transpose(1, 0, 2) + xc * D
            y = y * jax.nn.silu(zg)
            out = y @ out_proj_w.T
            return out.transpose(0, 2, 1).reshape(b, c, h, w) + x
        return _mamba2d(x, proj_w, in_proj_w, conv_w, conv_b, x_proj_w, dt_proj_w, dt_proj_b, A_log, D, out_proj_w)

    def _L1_conv_ref(x, W_fc, b_fc, gamma, beta):
        import jax, jax.numpy as jnp
        import numpy as np
        THRESHOLD = 16.0
        BN_EPS = 1e-05
        b, c, h, w = x.shape
        xf = x.reshape(b, c, h * w).transpose(0, 2, 1)
        sq = jnp.sum(xf * xf, axis=-1)
        d2 = sq[:, :, None] + sq[:, None, :] - 2.0 * jnp.einsum('bic,bjc->bij', xf, xf)
        dist = jnp.sqrt(jnp.maximum(d2, 0.0))
        incidence = (dist < THRESHOLD).astype(x.dtype)
        xe = jnp.einsum('bnc,dc->bnd', xf, W_fc) + b_fc
        deg_e = jnp.sum(incidence, axis=1)
        edge = jnp.einsum('bve,bvc->bec', incidence, xe)
        edge = jnp.where(deg_e > 0, 1.0 / deg_e, 0.0)[:, :, None] * edge
        deg_v = jnp.sum(incidence, axis=2)
        vert = jnp.einsum('bve,bec->bvc', incidence, edge)
        vert = jnp.where(deg_v > 0, 1.0 / deg_v, 0.0)[:, :, None] * vert
        out = vert + xf
        out = out.transpose(0, 2, 1).reshape(b, -1, h, w)
        mean = jnp.mean(out, axis=(0, 2, 3))
        var = jnp.var(out, axis=(0, 2, 3))
        y = (out - mean[None, :, None, None]) * jax.lax.rsqrt(var[None, :, None, None] + BN_EPS)
        y = gamma[None, :, None, None] * y + beta[None, :, None, None]
        return y * jax.nn.sigmoid(y)

    def _L2_attn_ref(x, W, b):
        import jax, jax.numpy as jnp
        import numpy as np
        B, T, D = (4, 2048, 128)
        Bx, Tx, Dx = x.shape
        qkv = (x @ W.T + b).reshape(Bx, Tx, 3, Dx)
        q, k, v = (qkv[:, :, 0], qkv[:, :, 1], qkv[:, :, 2])
        q = jax.nn.elu(q) + 1.0
        k = jax.nn.elu(k) + 1.0
        kv = jnp.einsum('bti,btj->btij', k, v)
        kv_cum = jnp.cumsum(kv, axis=1)
        k_cum = jnp.cumsum(k, axis=1)
        num = jnp.einsum('bti,btij->btj', q, kv_cum)
        den = jnp.einsum('bti,bti->bt', q, k_cum)[..., None] + 1e-06
        return num / den

    def _L2_ffn_ref(x, gate_w, gate_b, weight1, weight2):
        import jax, jax.numpy as jnp
        import numpy as np
        B, S, D, E, H, O, K = (512, 2048, 128, 64, 512, 128, 8)
        Bn, Sn, Dn = x.shape
        logits = jnp.einsum('bsd,ed->bse', x, gate_w) + gate_b
        probs = jax.nn.softmax(logits, axis=1)
        vals, idx = jax.lax.top_k(probs.transpose(0, 2, 1), K)
        topv = vals.transpose(0, 2, 1)
        topi = idx.transpose(0, 2, 1)
        flat_idx = topi.reshape(Bn, K * E)
        gathered = jnp.take_along_axis(x, flat_idx[:, :, None], axis=1)
        gathered = gathered.reshape(Bn, K, E, Dn)
        pooled = jnp.einsum('bked,bke->bed', gathered, topv)
        ones = jnp.ones((E, Bn, 1), dtype=x.dtype)
        h = jnp.concatenate([pooled.transpose(1, 0, 2), ones], axis=-1)
        h = jax.nn.gelu(jnp.einsum('ebd,edh->ebh', h, weight1), approximate=False)
        h = jnp.concatenate([h, ones], axis=-1)
        out = jnp.einsum('ebh,eho->ebo', h, weight2)
        out = out.transpose(1, 0, 2)
        weighted = jnp.einsum('beo,bke->bkeo', out, topv).reshape(Bn, K * E, O)
        outputs = jnp.zeros((Bn, Sn, O), dtype=x.dtype)
        outputs = outputs.at[jnp.arange(Bn)[:, None], flat_idx].add(weighted)
        return outputs

    def _L3_attn_ref(x, Wq, bq, Wk, bk, Wv, bv):
        import jax, jax.numpy as jnp
        import numpy as np
        INPUT_DIM = 128
        HIDDEN_DIM = 128
        WINDOW_SIZE = 256
        BLOCK_SIZE = 256
        BATCH = 8
        SEQ = 8192
        B, S, D = x.shape
        bs, w = (BLOCK_SIZE, WINDOW_SIZE)
        nb = S // bs
        halo = w - 1
        W = bs + 2 * halo
        q = x @ Wq.T + bq
        k = x @ Wk.T + bk
        v = x @ Wv.T + bv
        k_pad = jnp.pad(k, ((0, 0), (halo, halo), (0, 0)))
        v_pad = jnp.pad(v, ((0, 0), (halo, halo), (0, 0)))
        starts = jnp.arange(nb) * bs
        idx = starts[:, None] + jnp.arange(W)[None, :]
        k_win = k_pad[:, idx, :]
        v_win = v_pad[:, idx, :]
        q_blk = q.reshape(B, nb, bs, -1)
        scale = 1.0 / jnp.sqrt(jnp.float32(D))
        attn = jnp.einsum('bnqh,bnkh->bnqk', q_blk, k_win) * scale
        out = jnp.einsum('bnqk,bnkh->bnqh', attn, v_win)
        return out.reshape(B, S, -1)

    def _L3_ffn_ref(x, gate_w, gate_b, weight1, weight2):
        import jax, jax.numpy as jnp
        import numpy as np
        B, S, D, E, H, O, K = (512, 2048, 128, 64, 512, 128, 8)
        Bn, Sn, Dn = x.shape
        logits = jnp.einsum('bsd,ed->bse', x, gate_w) + gate_b
        probs = jax.nn.softmax(logits, axis=1)
        vals, idx = jax.lax.top_k(probs.transpose(0, 2, 1), K)
        topv = vals.transpose(0, 2, 1)
        topi = idx.transpose(0, 2, 1)
        flat_idx = topi.reshape(Bn, K * E)
        gathered = jnp.take_along_axis(x, flat_idx[:, :, None], axis=1)
        gathered = gathered.reshape(Bn, K, E, Dn)
        pooled = jnp.einsum('bked,bke->bed', gathered, topv)
        ones = jnp.ones((E, Bn, 1), dtype=x.dtype)
        h = jnp.concatenate([pooled.transpose(1, 0, 2), ones], axis=-1)
        h = jax.nn.gelu(jnp.einsum('ebd,edh->ebh', h, weight1), approximate=False)
        h = jnp.concatenate([h, ones], axis=-1)
        out = jnp.einsum('ebh,eho->ebo', h, weight2)
        out = out.transpose(1, 0, 2)
        weighted = jnp.einsum('beo,bke->bkeo', out, topv).reshape(Bn, K * E, O)
        outputs = jnp.zeros((Bn, Sn, O), dtype=x.dtype)
        outputs = outputs.at[jnp.arange(Bn)[:, None], flat_idx].add(weighted)
        return outputs

    def _gn(v, G=32, eps=1e-5):
        B_, C_, H_, W_ = v.shape
        g = v.reshape(B_, G, C_ // G, H_, W_)
        m = jnp.mean(g, axis=(2, 3, 4), keepdims=True)
        s = jnp.var(g, axis=(2, 3, 4), keepdims=True)
        return ((g - m) / jnp.sqrt(s + eps)).reshape(v.shape)

    def _ln_c(v, eps=1e-6):
        m = jnp.mean(v, axis=1, keepdims=True)
        s = jnp.var(v, axis=1, keepdims=True)
        return (v - m) / jnp.sqrt(s + eps)

    def _ln_t(v, eps=1e-5):
        m = jnp.mean(v, axis=-1, keepdims=True)
        s = jnp.var(v, axis=-1, keepdims=True)
        return (v - m) / jnp.sqrt(s + eps)

    def _to_tokens(v):
        B_, C_, H_, W_ = v.shape
        return v.reshape(B_, C_, H_ * W_).transpose(0, 2, 1)
    def _from_tokens(t, like):
        B_, C_, H_, W_ = like.shape
        return t.transpose(0, 2, 1).reshape(B_, C_, H_, W_)

    x = _L0_conv_ref(x, L0_conv_proj_w, L0_conv_in_proj_w, L0_conv_conv_w, L0_conv_conv_b, L0_conv_x_proj_w, L0_conv_dt_proj_w, L0_conv_dt_proj_b, L0_conv_A_log, L0_conv_D, L0_conv_out_proj_w)
    x = x + _L1_conv_ref(_gn(x), L1_conv_W_fc, L1_conv_b_fc, L1_conv_gamma, L1_conv_beta)
    t = _to_tokens(x)
    t = t + _L2_attn_ref(_ln_t(t), L2_attn_W, L2_attn_b)
    t = t + _L2_ffn_ref(_ln_t(t), L2_ffn_gate_w, L2_ffn_gate_b, L2_ffn_weight1, L2_ffn_weight2)
    t = t + _L3_attn_ref(_ln_t(t), L3_attn_Wq, L3_attn_bq, L3_attn_Wk, L3_attn_bk, L3_attn_Wv, L3_attn_bv)
    t = t + _L3_ffn_ref(_ln_t(t), L3_ffn_gate_w, L3_ffn_gate_b, L3_ffn_weight1, L3_ffn_weight2)
    x = _from_tokens(t, x)
    return x


_drawn_inputs = setup_inputs


def setup_inputs(seed=0):
    import zlib

    import numpy as np

    out = dict(_drawn_inputs(seed))
    spreads = {'L2_ffn_gate_b': (0.0, 2.0), 'L3_ffn_gate_b': (0.0, 0.8)}
    factors = {'L0_conv_conv_b': 2.717,
     'L1_conv_b_fc': 64.0,
     'L2_ffn_gate_w': 8.0,
     'L2_ffn_weight1': 8.0,
     'L2_ffn_weight2': 8.0,
     'L3_ffn_gate_w': 29.765,
     'L3_ffn_weight1': 36.233,
     'L3_ffn_weight2': 29.918}
    for name, (base, spread) in spreads.items():
        noise = np.random.default_rng([zlib.crc32(name.encode()), seed]).standard_normal(out[name].shape)
        drawn = base * np.exp(spread * noise) if base else spread * noise
        out[name] = jnp.asarray(drawn.astype(out[name].dtype))
    for name, factor in factors.items():
        out[name] = (out[name] * factor).astype(out[name].dtype)
    return out
```

```python
from contextlib import ExitStack

import concourse.bass as bass
from concourse import mybir

ALU = mybir.AluOpType
ACT = mybir.ActivationFunctionType
F32 = mybir.dt.float32
BF16 = mybir.dt.bfloat16
F16 = mybir.dt.float16
F8 = mybir.dt.float8e4
AX_X = mybir.AxisListType.X

B = 4
C = 128
L = 4096
T = 512
CPB = L // T
NCH = B * CPB
DI, DS, DR, DK = 256, 16, 8, 4
HALO = DK - 1
TPC = T // 128

OFF = 8


def done(k):
    return OFF + k


class Semaphores:

    def __init__(self, nc, prefix):
        self.nc, self.prefix, self.handles = nc, prefix, []

    def __call__(self, name):
        s = self.nc.alloc_semaphore(self.prefix + name)
        self.handles.append(s)
        return s

    def clear(self):
        self.nc.clear_and_free_semaphores(self.handles)
        self.nc.all_engine_barrier()


def mamba(nc, a, x_in, x_out):
    U = 2 * DS
    R = 16
    GR = 8
    with ExitStack() as ctx:
        def sb(name, shape, dt=F32):
            return ctx.enter_context(nc.sbuf_tensor("m_" + name, shape, dt))

        def ps(name, shape):
            return ctx.enter_context(nc.psum_tensor("m_" + name, shape, F32))

        sem = Semaphores(nc, "m_")
        ctx.callback(sem.clear)

        xh = sb("xh", [C, NCH + 2, HALO + T])
        hs = sb("hs", [128, R, T])
        carry = sb("carry", [128, U])
        xc = sb("xc", [128, 2, T])
        sz = sb("sz", [128, 2, T])
        delta = sb("delta", [128, 2, 2, T])
        dtx = sb("dtx", [128, 2, 2, T])
        dtr = sb("dtr", [128, 2, T])
        parts = sb("parts", [96, 2, T], BF16)
        resid = sb("resid", [64, T])
        Bs = sb("Bs", [128, 4, T])
        dBx = sb("dBx", [128, 4, T])
        prod = sb("prod", [128, 4, T])
        sp_a = sb("sp_a", [128, 2, T])
        sp_r = sb("sp_r", [128, 2, T])
        ob = sb("ob", [128, T])
        ident = sb("ident", [128, 128])
        projw = dBx[:, 1, 0:C]
        inpT = dBx[:, 0, :]
        cwb = prod[:, 0:2, :].rearrange("p a (b d) -> p (a b) d", b=2)
        Wx = sb("Wx", [128, DK, DI])
        Wz = sb("Wz", [128, DI])
        xpT = sb("xpT", [128, 2, 104])
        dtT = sb("dtT", [128, DI])
        opT = sb("opT", [128, 2, C])
        diagD = sb("diagD", [128, 2, 128])
        E = sb("E", [96, 2, 32])
        Eb = sb("Eb", [96, 32], BF16)
        sel = sb("sel", [96, 32, 128], BF16)
        cb = sb("cb", [128, 2])
        dtb = sb("dtb", [128, 2])
        Dc = sb("Dc", [128, 2])
        Al = sb("Al", [128, 2, DS])
        Ae = sb("Ae", [128, 2, DS])
        An = sb("An", [128, 2, DS])
        tick = sb("tick", [128, 16])

        pdA = ps("pdA", [128, 2, T])
        pC = ps("pC", [128, 2, T])
        pB = ps("pB", [128, T])
        pY = ps("pY", [128, 2, T])
        pM = ps("pM", [128, T])

        s_w = sem("weights"); s_x0 = sem("x_first"); s_xr = sem("x_rest")
        s_wc = sem("w_product"); s_prep = sem("w_ready"); s_edge = sem("zeros")
        misc_full = sem("misc_full"); misc_free = sem("misc_free")
        xc_ready = sem("xc_ready"); sz_ready = sem("sz_ready"); D_done = sem("D_done")
        hi_ready = sem("hi_ready"); split_step = sem("split_step"); parts_ready = sem("parts_ready")
        act_step = sem("act_step"); sp_ready = sem("sp_ready")
        delta_ready = sem("delta_ready"); dtx_ready = sem("dtx_ready")
        B_full = sem("B_full"); Bs_ready = sem("Bs_ready"); C_full = sem("C_full")
        dA_ready = sem("dA_ready"); dBx_ready = sem("dBx_ready"); scan_done = sem("scan_done")
        carried = sem("carried"); h_zero = sem("h_zero")
        prod_ready = sem("prod_ready"); y_added = sem("y_added"); yg_ready = sem("yg_ready")
        stored = sem("stored"); started = sem("started")

        MP, MI = 5, 8
        M_OUT, M_Z, M_C, M_XD, M_DT = 0, 1, 3, 5, 6

        x_src = [x_in[b].rearrange("c (n t) -> c n t", t=T) for b in range(B)]

        def tile_of(i, lo, hi):
            return xh[:, bass.ds(i, 1), lo:hi].rearrange("c o t -> c (o t)")

        with nc.Block() as block:

            @block.sync
            def _(sp):
                def load(b, s):
                    sp.dma_start(xh[:, b * CPB + 1:(b + 1) * CPB + 1, HALO:], x_src[b]).then_inc(s, 16)
                    sp.dma_start(xh[:, b * CPB + 2:(b + 1) * CPB + 1, 0:HALO],
                                 x_src[b][:, 0:CPB - 1, T - HALO:T]).then_inc(s, 16)
                sp.dma_start(ident[:], a["ident"]).then_inc(s_w, 16)
                sp.dma_start(projw, a["L0_conv_proj_w"]).then_inc(s_w, 16)
                sp.dma_start(inpT, a["in_projT"]).then_inc(s_w, 16)
                sp.dma_start(cwb, a["conv_wT"].partition_broadcast(128)).then_inc(s_w, 16)
                load(0, s_x0)
                sp.dma_start(xpT[:], a["x_projT"].rearrange("(h p) m -> p h m", p=128)).then_inc(s_w, 16)
                sp.dma_start(dtT[96:104, :], a["dt_projT"]).then_inc(s_w, 16)
                sp.dma_start(opT[:], a["out_projT"].rearrange("(h p) m -> p h m", p=128)).then_inc(s_w, 16)
                sp.dma_start(cb[:], a["conv_b"]).then_inc(s_w, 16)
                sp.dma_start(dtb[:], a["dt_b"]).then_inc(s_w, 16)
                sp.dma_start(Dc[:], a["D"]).then_inc(s_w, 16)
                sp.dma_start(Al[:], a["A_log"].rearrange("(h p) n -> p h n", p=128)).then_inc(s_w, 16)
                for b in range(1, B):
                    load(b, s_xr)
                with sp.Fori(0, B) as b:
                    with sp.Fori(0, CPB) as c:
                        it = b * CPB + c
                        sp.wait_ge(misc_free, done((it + 1) * MI + MP + M_OUT + 1))
                        sp.dma_start(x_out[bass.ds(b, 1), :, bass.ds(c * T, T)].rearrange("o c t -> c (o t)"),
                                     ob[:]).then_inc(stored, 16)
                sp.wait_ge(stored, 16 * (NCH + 2))

            @block.tensor
            def _(pe):
                def misc(k, body):
                    pe.wait_ge(misc_free, done(k))
                    body().then_inc(misc_full, 1)

                def conv(k, q, half):
                    def body():
                        for tap in range(DK):
                            m = nc.tensor.matmul(pM[:], Wx[:, tap, half * 128:(half + 1) * 128],
                                                 tile_of(q + 1, tap, tap + T),
                                                 start=(tap == 0), stop=(tap == DK - 1))
                        return m
                    misc(k, body)

                def xdbl(k, q):
                    pe.wait_ge(xc_ready, q + 1)
                    def body():
                        for h in range(2):
                            m = nc.tensor.matmul(pM[0:104, :], xpT[:, h, :], xc[:, h, :],
                                                 start=(h == 0), stop=(h == 1))
                        return m
                    misc(k, body)

                def dt(k, q, par, half):
                    pe.wait_ge(hi_ready, 2 * q + 2)
                    misc(k, lambda: nc.tensor.matmul(pM[:], dtT[96:104, half * 128:(half + 1) * 128],
                                                     dtr[96:104, par, :], start=True, stop=True))

                def finish(k, i):
                    def body():
                        nc.tensor.matmul(pM[:], ident[:], tile_of(i, HALO, HALO + T), start=True, stop=False)
                        nc.tensor.matmul(pM[:], opT[:, 0, :], sz[:, 0, :], start=False, stop=False)
                        return nc.tensor.matmul(pM[:], opT[:, 1, :], sz[:, 1, :], start=False, stop=True)
                    misc(k, body)

                def spread_b(g, par, n):
                    nc.tensor.matmul(pB[:], sel[:, n, :], parts[:, par, :], start=True,
                                     stop=True).then_inc(B_full, 1)

                def spread_c(g, par, n):
                    nc.tensor.matmul(pC[:, n % 2, :], sel[:, DS + n, :], parts[:, par, :], start=True,
                                     stop=True).then_inc(C_full, 1)

                pe.wait_ge(s_w, 16 * 11)
                nc.tensor.matmul(pM[:], projw, inpT, start=True, stop=True).then_inc(s_wc, 1)
                pe.wait_ge(s_prep, 9)
                pe.wait_ge(started, 3)
                pe.wait_ge(s_edge, 4)
                for half in range(2):
                    nc.tensor.matmul(pY[:, half, :], ident[:], xh[:, 0, HALO:], start=True,
                                     stop=True).then_inc(y_added, OFF // 2)
                pe.wait_ge(s_x0, 32)
                for half in range(2):
                    conv(half, 0, half)
                xdbl(2, 0)
                for half in range(2):
                    dt(3 + half, 0, 0, half)
                pe.wait_ge(parts_ready, 1)
                spread_b(0, 0, 0)
                spread_c(0, 0, 0)
                pe.wait_ge(Bs_ready, 1)
                spread_b(1, 0, 1)
                with pe.Fori(0, B) as b:
                    with pe.Fori(0, CPB // 2) as c2:
                        for par in range(2):
                            it = b * CPB + c2 * 2 + par
                            k0 = it * MI + MP
                            g0 = it * U

                            def add(u):
                                pe.wait_ge(prod_ready, done(g0 + u + 1))
                                nc.tensor.matmul(pY[:, u % 2, :], ident[:], prod[:, u % 4, :],
                                                 start=False, stop=(u >= U - 2)).then_inc(y_added, 1)

                            for u in range(U):
                                n = u // 2
                                if u % 2 == 0:
                                    g = it * DS + n
                                    if n + 2 == DS:
                                        pe.wait_ge(parts_ready, it + 2)
                                    pe.wait_ge(Bs_ready, g + 2)
                                    spread_b(g + 2, par if n + 2 < DS else 1 - par, (n + 2) % DS)
                                    pe.wait_ge(prod_ready, done(2 * g))
                                    spread_c(g + 1, par if n + 1 < DS else 1 - par, (n + 1) % DS)
                                if u == 0:
                                    for half in range(2):
                                        pe.wait_ge(yg_ready, done(2 * it + 2))
                                        nc.tensor.matmul(pY[:, half, :], diagD[:, half, :], xc[:, half, :],
                                                         start=True, stop=False).then_inc(D_done, 1)
                                    finish(k0 + M_OUT, it)
                                if u == 16:
                                    pe.wait_ge(s_xr, 32 * (B - 1))
                                for half in range(2):
                                    if u == 2 + half:
                                        misc(k0 + M_Z + half, lambda: nc.tensor.matmul(
                                            pM[:], Wz[:, half * 128:(half + 1) * 128],
                                            tile_of(it + 1, HALO, HALO + T), start=True, stop=True))
                                    if u == 5 + half:
                                        conv(k0 + M_C + half, it + 1, half)
                                    if u == 17 + half:
                                        dt(k0 + M_DT + half, it + 1, 1 - par, half)
                                if u == 12:
                                    xdbl(k0 + M_XD, it + 1)
                                if u >= 1:
                                    add(u - 1)
                            add(U - 1)
                pe.wait_ge(yg_ready, done(2 * NCH + 2))
                finish(NCH * MI + MP + M_OUT, NCH)

            @block.scalar
            def _(act):
                def raw(k, out, bias=0.0):
                    act.wait_ge(misc_full, k + 1)
                    nc.scalar.activation(out, pM[:], ACT.Identity, bias=bias).then_inc(misc_free, 1)

                def conv(k, q, half):
                    act.wait_ge(D_done, 2 * q)
                    act.wait_ge(dtx_ready, 2 * q)
                    raw(k, xc[:, half, :], cb[:, half:half + 1])

                def xdbl(k, q, par):
                    act.wait_ge(misc_full, k + 1)
                    nc.scalar.copy(dtr[96:104, par, :], pM[96:104, :]).then_inc(hi_ready, 1)
                    nc.scalar.copy(parts[:, par, :], pM[0:96, :]).then_inc(hi_ready, 1)

                def softplus(k, q, half):
                    act.wait_ge(dtx_ready, 2 * q)
                    act.wait_ge(misc_full, k + 1)
                    t = sp_a[:, half, :]
                    nc.scalar.activation(t, pM[:], ACT.Abs, bias=dtb[:, half:half + 1]).then_inc(act_step, 1)
                    nc.scalar.activation(sp_r[:, half, :], pM[:], ACT.Relu,
                                         bias=dtb[:, half:half + 1]).then_inc(misc_free, 1)
                    act.wait_ge(act_step, 4 * q + 2 * half + 1)
                    nc.scalar.activation(t, t, ACT.Exp, scale=-1.0).then_inc(act_step, 1)

                def softplus_log(q):
                    act.wait_ge(act_step, 4 * q + 4)
                    t = sp_a[:].rearrange("p h t -> p (h t)")
                    nc.scalar.activation(t, t, ACT.Ln, bias=1.0).then_inc(sp_ready, 1)

                def silu(tile, k, ready):
                    act.wait_ge(misc_free, done(k + 2))
                    t = tile[:].rearrange("p h t -> p (h t)")
                    nc.scalar.activation(t, t, ACT.Silu).then_inc(ready, 1)

                def copy_b(g, n):
                    act.wait_ge(B_full, g + 1)
                    act.wait_ge(dBx_ready, done(2 * g - 6))
                    nc.scalar.copy(Bs[:, n % 4, :], pB[:]).then_inc(Bs_ready, 1)

                act.wait_ge(s_w, 16 * 11)
                nc.scalar.activation(Ae[:], Al[:], ACT.Exp).then_inc(s_wc, 1)
                act.wait_ge(s_prep, 9)
                for half in range(2):
                    raw(half, xc[:, half, :], cb[:, half:half + 1])
                silu(xc, 0, xc_ready)
                xdbl(2, 0, 0)
                for half in range(2):
                    softplus(3 + half, 0, half)
                softplus_log(0)
                copy_b(0, 0)
                with act.Fori(0, B) as b:
                    with act.Fori(0, CPB // 2) as c2:
                        for par in range(2):
                            it = b * CPB + c2 * 2 + par
                            k0 = it * MI + MP
                            g0 = it * U

                            def carry_on(group, u_end):
                                act.wait_ge(scan_done, done(g0 + u_end))
                                s0 = group * GR % R
                                nc.scalar.copy(carry[:, group * GR:(group + 1) * GR],
                                               hs[:, s0:s0 + GR, T - 1:T].rearrange("p a o -> p (a o)")
                                               ).then_inc(carried, 1)

                            for u in range(U):
                                n, half = u // 2, u % 2
                                if half == 0:
                                    copy_b(it * DS + n + 1, (n + 1) % DS)
                                act.wait_ge(delta_ready, 2 * it + 2)
                                act.wait_ge(scan_done, done(g0 + u - 1))
                                nc.scalar.activation(pdA[:, u % 2, :], delta[:, par, half, :], ACT.Exp,
                                                     scale=An[:, half, n:n + 1]).then_inc(dA_ready, 1)
                                if u == 2:
                                    act.wait_ge(h_zero, 2 * b + 2)
                                    carry_on(U // GR - 1, 0)
                                for group in range(U // GR - 1):
                                    if u == (group + 1) * GR + 2:
                                        carry_on(group, (group + 1) * GR)
                                if u == 3:
                                    act.wait_ge(stored, 16 * (it + 1))
                                    raw(k0 + M_OUT, ob[:])
                                for hf in range(2):
                                    if u == 4 + hf:
                                        raw(k0 + M_Z + hf, sz[:, hf, :])
                                    if u == 7 + hf:
                                        conv(k0 + M_C + hf, it + 1, hf)
                                    if u == 19 + hf:
                                        softplus(k0 + M_DT + hf, it + 1, hf)
                                if u == 9:
                                    silu(sz, k0 + M_Z, sz_ready)
                                    silu(xc, k0 + M_C, xc_ready)
                                if u == 14:
                                    xdbl(k0 + M_XD, it + 1, 1 - par)
                                if u == 21:
                                    softplus_log(it + 1)
                act.wait_ge(stored, 16 * (NCH + 1))
                raw(NCH * MI + MP + M_OUT, ob[:])

            @block.vector
            def _(dve):
                for k, s in enumerate((misc_free, scan_done, prod_ready, yg_ready, sz_ready, carried)):
                    nc.vector.memset(tick[:, 4 + k:5 + k], 0.0).then_inc(s, OFF)
                nc.vector.memset(tick[:, 10:11], 0.0).then_inc(stored, 32)
                nc.vector.memset(tick[:, 11:12], 0.0).then_inc(started, 1)
                nc.vector.memset(xh[:, 1:NCH + 1:CPB, 0:HALO], 0.0).then_inc(s_edge, 1)
                nc.vector.memset(xh[:, 0, :], 0.0).then_inc(s_edge, 1)
                nc.vector.memset(xh[:, NCH + 1, :], 0.0).then_inc(s_edge, 1)
                nc.vector.memset(sz[:], 0.0).then_inc(s_edge, 1)
                dve.wait_ge(s_w, 16 * 11)
                dve.wait_ge(s_wc, 2)
                for tap in range(DK):
                    nc.vector.tensor_tensor(Wx[:, tap, :], pM[:, 0:DI], cwb[:, tap, :],
                                            ALU.mult).then_inc(s_prep, 1)
                nc.vector.tensor_copy(Wz[:], pM[:, DI:2 * DI]).then_inc(s_prep, 1)
                nc.vector.tensor_scalar(An[:], Ae[:], -1.0, None, ALU.mult).then_inc(s_prep, 1)
                for half in range(2):
                    nc.vector.tensor_scalar(diagD[:, half, :], ident[:], Dc[:, half:half + 1], None,
                                            ALU.mult).then_inc(s_prep, 1)
                nc.vector.tensor_tensor(E[:, 0, :], ident[0:96, 0:32], ident[0:96, 32:64],
                                        ALU.add).then_inc(split_step, 1)
                dve.wait_ge(split_step, 1)
                nc.vector.tensor_tensor(Eb[:], E[:, 0, :], ident[0:96, 64:96], ALU.add).then_inc(split_step, 1)
                dve.wait_ge(split_step, 2)
                nc.vector.tensor_copy(sel[:], Eb[:].unsqueeze(2).to_broadcast([96, 32, 128])).then_inc(s_prep, 1)

                def split(k, q, par):
                    dve.wait_ge(hi_ready, 2 * q + 2)
                    nc.vector.tensor_tensor(resid[:], pM[0:64, :], parts[0:64, par, :],
                                            ALU.subtract).then_inc(misc_free, 1)
                    dve.wait_ge(misc_free, done(k + 1))
                    nc.vector.tensor_copy(parts[0:64, par, :], resid[:]).then_inc(split_step, 1)
                    dve.wait_ge(split_step, 2 + q + 1)
                    nc.vector.tensor_tensor(parts[0:32, par, :], resid[0:32, :], parts[0:32, par, :],
                                            ALU.subtract).then_inc(parts_ready, 1)

                def gate(it):
                    dve.wait_ge(sz_ready, done(it))
                    dve.wait_ge(y_added, done(it * U))
                    for half in range(2):
                        nc.vector.tensor_tensor(sz[:, half, :], pY[:, half, :], sz[:, half, :],
                                                ALU.mult).then_inc(yg_ready, 1)

                split(2, 0, 0)
                with dve.Fori(0, B) as b:
                    dve.wait_ge(prod_ready, done(b * (CPB * U)))
                    nc.vector.memset(hs[:, R - GR:R, T - 1:T], 0.0).then_inc(h_zero, 1)
                    dve.wait_ge(carried, done(b * (CPB * (U // GR))))
                    nc.vector.memset(carry[:, 0:U - GR], 0.0).then_inc(h_zero, 1)
                    with dve.Fori(0, CPB // 2) as c2:
                        for par in range(2):
                            it = b * CPB + c2 * 2 + par
                            k0 = it * MI + MP
                            g0 = it * U

                            def product(u):
                                n = u // 2
                                dve.wait_ge(C_full, it * DS + n + 1)
                                dve.wait_ge(scan_done, done(g0 + u + 1))
                                dve.wait_ge(y_added, done(g0 + u - 3))
                                nc.vector.tensor_tensor(prod[:, u % 4, :], hs[:, u % R, :], pC[:, n % 2, :],
                                                        ALU.mult).then_inc(prod_ready, 1)

                            for u in range(U):
                                if u == 0:
                                    dve.wait_ge(h_zero, 2 * b + 2)
                                if u % GR == 0:
                                    dve.wait_ge(carried, done(it * (U // GR) + u // GR))
                                    dve.wait_ge(prod_ready, done(g0 + u - 1))
                                dve.wait_ge(dA_ready, g0 + u + 1)
                                dve.wait_ge(dBx_ready, done(g0 + u + 1))
                                nc.vector.tensor_tensor_scan(hs[:, u % R, :], pdA[:, u % 2, :], dBx[:, u % 4, :],
                                                             carry[:, u:u + 1], ALU.mult, ALU.add).then_inc(scan_done, 1)
                                if u >= 1:
                                    product(u - 1)
                                if u == 0:
                                    gate(it)
                                if u == 16:
                                    split(k0 + M_XD, it + 1, 1 - par)
                            product(U - 1)
                gate(NCH)

            @block.gpsimd
            def _(pool):
                def dt_x(q, par, half, step):
                    if step == 0:
                        pool.wait_ge(sp_ready, q + 1)
                        nc.gpsimd.tensor_tensor(delta[:, par, half, :], sp_a[:, half, :], sp_r[:, half, :],
                                                ALU.add).then_inc(delta_ready, 1)
                    else:
                        pool.wait_ge(delta_ready, 2 * q + half + 1)
                        pool.wait_ge(xc_ready, q + 1)
                        nc.gpsimd.tensor_tensor(dtx[:, par, half, :], delta[:, par, half, :], xc[:, half, :],
                                                ALU.mult).then_inc(dtx_ready, 1)

                nc.gpsimd.memset(tick[:, 3:4], 0.0).then_inc(dBx_ready, OFF)
                nc.gpsimd.memset(tick[:, 2:3], 0.0).then_inc(started, 2)
                for half in range(2):
                    dt_x(0, 0, half, 0)
                    dt_x(0, 0, half, 1)
                with pool.Fori(0, B) as b:
                    with pool.Fori(0, CPB // 2) as c2:
                        for par in range(2):
                            it = b * CPB + c2 * 2 + par
                            g0 = it * U
                            for u in range(U):
                                n, half = u // 2, u % 2
                                pool.wait_ge(Bs_ready, it * DS + n + 1)
                                pool.wait_ge(dtx_ready, 2 * it + half + 1)
                                pool.wait_ge(scan_done, done(g0 + u - 3))
                                nc.gpsimd.tensor_tensor(dBx[:, u % 4, :], dtx[:, par, half, :], Bs[:, n % 4, :],
                                                        ALU.mult).then_inc(dBx_ready, 1)
                                if 22 <= u < 26:
                                    dt_x(it + 1, 1 - par, (u - 22) // 2, u % 2)


def hypergraph(nc, a, x_in, pre_out, bn_stats):
    NT = L // 128
    TPC = T // 128
    with ExitStack() as ctx:
        def sb(name, shape, dt=F32):
            return ctx.enter_context(nc.sbuf_tensor("h_" + name, shape, dt))

        def ps(name, shape):
            return ctx.enter_context(nc.psum_tensor("h_" + name, shape, F32))

        sem = Semaphores(nc, "h_")
        ctx.callback(sem.clear)

        inc = sb("inc", [128, NT, L], F8)
        xn = sb("xn", [128, CPB, T])
        parts = sb("parts", [128, 2, L], F16)
        inv_b = parts[:].rearrange("p a l -> p (a l)").bitcast(F32).rearrange("p (n t) -> p n t", t=T)
        rows = sb("rows", [128, 2, NT, 128], F16)
        sq = sb("sq", [128, CPB, T])
        tmp = sb("tmp", [128, 2, T])
        ob = sb("ob", [128, 2, T])
        ident = sb("ident", [128, 128])
        ident16 = sb("ident16", [128, 128], F16)
        ones = sb("ones", [128, 128])
        halves = sb("halves", [128, 128])
        gmean = sb("gmean", [128, 128])
        wfcT = sb("wfcT", [128, 128])
        bfc = sb("bfc", [128, 1])
        st = sb("st", [128, CPB, 6])
        mv = sb("mv", [128, 2])
        tick = sb("tick", [128, 16])
        sc = sb("sc", [128, 8])
        sd = sb("sd", [128, 2, NT])
        dg = sb("dg", [128, NT, CPB])
        inv = sb("inv", [128, 3, NT])
        pG = ps("pG", [128, 4, T])
        pE = ps("pE", [128, 2, T])
        pX = ps("pX", [128, 2, T])

        s_w = sem("weights"); w_ready = sem("w_ready"); started = sem("started")
        x_loaded = sem("x_loaded"); gn = sem("gn_step")
        hi_done = sem("hi_done"); lo_done = sem("lo_done"); square_done = sem("square_done")
        sq_full = sem("sq_full"); sq_done = sem("sq_done"); diag_step = sem("diag_step")
        turned = sem("turned"); rows_hi = sem("rows_hi"); rows_lo = sem("rows_lo")
        gram_full = sem("gram_full"); inc_done = sem("inc_done"); edge_full = sem("edge_full")
        edge_out = sem("edge_out"); deg_step = sem("deg_step"); dtile = sem("dtile")
        inv_full = sem("inv_full"); inv_done = sem("inv_done"); edge_scaled = sem("edge_scaled")
        eturn = sem("eturn"); ehi = sem("ehi"); elo = sem("elo")
        vert_full = sem("vert_full"); vert_out = sem("vert_out")
        w_full = sem("w_full"); ob_ready = sem("ob_ready"); bn_done = sem("bn_done"); stored = [sem("stored0"), sem("stored1")]

        pe_gate = sem("pe_gate"); dve_gate = sem("dve_gate")

        LAG = 3
        GN = 21
        x_src = x_in.rearrange("b c (n t) -> b c n t", t=T)

        with nc.Block() as block:

            @block.sync
            def _(sp):
                for dst, name in ((ident, "ident"), (gmean, "gmean"), (wfcT, "W_fcT"), (bfc, "b_fc")):
                    sp.dma_start(dst[:], a[name]).then_inc(s_w, 16)
                with sp.Fori(0, B) as b:
                    sp.wait_ge(bn_done, done(b * CPB))
                    sp.dma_start(xn[:], x_src[bass.ds(b, 1)].rearrange("o c n t -> c (o n) t")).then_inc(x_loaded, 16)
                    for j in range(CPB):
                        sp.wait_ge(ob_ready, done(b * CPB + j + 1))
                        sp.dma_start(pre_out[bass.ds(b, 1), :, j * T:(j + 1) * T].rearrange("o c t -> c (o t)"),
                                     ob[:, j % 2, :]).then_inc(stored[j % 2], 16)
                for par in range(2):
                    sp.wait_ge(stored[par], 16 * (NCH // 2 + 1))

            @block.tensor
            def _(pe):
                pe.wait_ge(s_w, 64)
                pe.wait_ge(w_ready, 3)
                pe.wait_ge(started, 1)
                with pe.Fori(0, B) as b:
                    def at(per, k):
                        return b * per + k
                    pe.wait_ge(gn, at(GN, 9))
                    nc.tensor.matmul(pX[:, 0, 0:1], gmean[:], mv[:, 0:1], start=True, stop=True).then_inc(gn, 1)
                    pe.wait_ge(gn, at(GN, 13))
                    nc.tensor.matmul(pX[:, 1, 0:1], gmean[:], sc[:, 1:2], start=True, stop=True).then_inc(gn, 1)
                    for j in range(CPB):
                        pe.wait_ge(square_done, at(CPB, j + 1))
                        pe.wait_ge(sq_done, done(at(CPB, j - 1)))
                        nc.tensor.matmul(pX[:, j % 2, :], halves[:], tmp[:, j % 2, :], start=True,
                                         stop=True).then_inc(sq_full, 1)
                        for part in range(2):
                            m = 2 * j + part
                            pe.wait_ge((hi_done, lo_done)[part], at(CPB, j + 1))
                            pe.wait_ge((rows_hi, rows_lo)[part], done(at(CPB, j - 1)))
                            dst = pG[:, m % 4, :].bitcast(F16)
                            for t in range(TPC):
                                i = j * TPC + t
                                m_ = nc.tensor.transpose(dst[:, t * 128:(t + 1) * 128],
                                                         parts[:, part, i * 128:(i + 1) * 128], ident16[:])
                            m_.then_inc(turned, 1)
                    pe.wait_ge(rows_hi, done(at(CPB, CPB)))
                    pe.wait_ge(rows_lo, done(at(CPB, CPB)))

                    def gram(k):
                        j, i = divmod(k, NT)
                        pe.wait_ge(inc_done, done(at(CPB * NT, k - 3)))
                        hi, lo = parts[:, 0, :], parts[:, 1, :]
                        me, them = slice(i * 128, (i + 1) * 128), slice(j * T, (j + 1) * T)
                        dst = pG[:, k % 4, :]
                        nc.tensor.matmul(dst, hi[:, me], hi[:, them], start=True, stop=False)
                        nc.tensor.matmul(dst, hi[:, me], lo[:, them], start=False, stop=False)
                        nc.tensor.matmul(dst, lo[:, me], hi[:, them], start=False, stop=True).then_inc(gram_full, 1)

                    def edge(k):
                        j, i = divmod(k, NT)
                        if i == 0:
                            pe.wait_ge(edge_out, done(at(CPB, j - 1)))
                        pe.wait_ge(inc_done, done(at(CPB * NT, k + 1)))
                        pe.sem_inc(pe_gate, 1)
                        for part in range(2):
                            m = nc.tensor.matmul(pE[:, j % 2, :], rows[:, part, i, :],
                                                 inc[:, i, j * T:(j + 1) * T],
                                                 start=(i == 0 and part == 0), stop=(i == NT - 1 and part == 1))
                        if i == NT - 1:
                            m.then_inc(edge_full, 1)

                    for k in range(LAG):
                        gram(k)
                    for k in range(CPB * NT):
                        if k + LAG < CPB * NT:
                            gram(k + LAG)
                        edge(k)

                    def spread_inv(j):
                        pe.wait_ge(dtile, at(CPB, j + 1))
                        pe.wait_ge(inv_done, done(at(CPB, j - 1)))
                        nc.tensor.matmul(pX[:, j % 2, :], ones[:], tmp[:, j % 2, :], start=True,
                                         stop=True).then_inc(inv_full, 1)

                    spread_inv(0)
                    for j in range(CPB):
                        if j + 1 < CPB:
                            spread_inv(j + 1)
                        pe.wait_ge(edge_scaled, at(CPB, j + 1))
                        pe.wait_ge(elo, done(at(CPB, j - 3)))
                        for t in range(TPC):
                            m = nc.tensor.transpose(pG[:, j % 4, t * 128:(t + 1) * 128],
                                                    sq[:, j, t * 128:(t + 1) * 128], ident[:])
                        m.then_inc(eturn, 1)
                    pe.wait_ge(elo, done(at(CPB, CPB)))

                    def fc(j):
                        pe.wait_ge(vert_out, done(at(CPB, j + 1)))
                        pe.wait_ge(ob_ready, done(at(CPB, j - 1)))
                        nc.tensor.matmul(pX[:, j % 2, :], wfcT[:], tmp[:, j % 2, :], start=True,
                                         stop=True).then_inc(w_full, 1)

                    for j in range(CPB):
                        pe.wait_ge(vert_out, done(at(CPB, j - 1)))
                        pe.sem_inc(pe_gate, 1)
                        for i in range(NT):
                            for part in range(2):
                                m = nc.tensor.matmul(pE[:, j % 2, :], rows[:, part, i, :],
                                                     inc[:, i, j * T:(j + 1) * T],
                                                     start=(i == 0 and part == 0),
                                                     stop=(i == NT - 1 and part == 1))
                        m.then_inc(vert_full, 1)
                        if j >= 1:
                            fc(j - 1)
                    fc(CPB - 1)

            @block.scalar
            def _(act):
                with act.Fori(0, B) as b:
                    def at(per, k):
                        return b * per + k
                    act.wait_ge(gn, at(GN, 15))
                    nc.scalar.activation(sc[:, 4:5], sc[:, 2:3], ACT.Ln).then_inc(gn, 1)
                    act.wait_ge(gn, at(GN, 16))
                    nc.scalar.activation(sc[:, 5:6], sc[:, 4:5], ACT.Exp, scale=-0.5).then_inc(gn, 1)
                    act.wait_ge(gn, at(GN, GN))
                    for j in range(CPB):
                        nc.scalar.copy(parts[:, 0, j * T:(j + 1) * T], xn[:, j, :]).then_inc(hi_done, 1)
                        act.wait_ge(sq_full, at(CPB, j + 1))
                        nc.scalar.copy(sq[:, j, :], pX[:, j % 2, :]).then_inc(sq_done, 1)
                        act.wait_ge(turned, at(2 * CPB, 2 * j + 1))
                        nc.scalar.copy(rows[:, 0, j * TPC:(j + 1) * TPC, :].rearrange("p a b -> p (a b)"),
                                       pG[:, (2 * j) % 4, :].bitcast(F16)[:, 0:T]).then_inc(rows_hi, 1)
                    for j in range(CPB):
                        act.wait_ge(edge_full, at(CPB, j + 1))
                        nc.scalar.copy(sq[:, j, :], pE[:, j % 2, :]).then_inc(edge_out, 1)
                    for j in range(CPB):
                        act.wait_ge(inv_full, at(CPB, j + 1))
                        nc.scalar.copy(inv_b[:, j, :], pX[:, j % 2, :]).then_inc(inv_done, 1)
                        act.wait_ge(eturn, at(CPB, j + 1))
                        nc.scalar.copy(rows[:, 0, j * TPC:(j + 1) * TPC, :].rearrange("p a b -> p (a b)"),
                                       pG[:, j % 4, :]).then_inc(ehi, 1)

            @block.vector
            def _(dve):
                nc.vector.memset(ones[:], 1.0).then_inc(w_ready, 1)
                nc.vector.memset(halves[:], 0.5).then_inc(w_ready, 1)
                nc.vector.memset(tick[:, 0:1], 0.0).then_inc(sq_done, OFF)
                nc.vector.memset(tick[:, 1:2], 0.0).then_inc(rows_hi, OFF)
                nc.vector.memset(tick[:, 2:3], 0.0).then_inc(rows_lo, OFF)
                nc.vector.memset(tick[:, 3:4], 0.0).then_inc(inc_done, OFF)
                nc.vector.memset(tick[:, 4:5], 0.0).then_inc(edge_out, OFF)
                nc.vector.memset(tick[:, 5:6], 0.0).then_inc(inv_done, OFF)
                nc.vector.memset(tick[:, 6:7], 0.0).then_inc(elo, OFF)
                nc.vector.memset(tick[:, 7:8], 0.0).then_inc(vert_out, OFF)
                nc.vector.memset(tick[:, 8:9], 0.0).then_inc(ob_ready, OFF)
                nc.vector.memset(tick[:, 9:10], 0.0).then_inc(bn_done, OFF)
                nc.vector.memset(tick[:, 10:11], 0.0).then_inc(stored[0], 16)
                nc.vector.memset(tick[:, 15:16], 0.0).then_inc(stored[1], 16)
                nc.vector.memset(tick[:, 11:12], 0.0).then_inc(started, 1)
                dve.wait_ge(s_w, 64)
                nc.vector.tensor_copy(ident16[:], ident[:]).then_inc(w_ready, 1)
                with dve.Fori(0, B) as b:
                    def at(per, k):
                        return b * per + k

                    def chain(k, op):
                        dve.wait_ge(gn, at(GN, k))
                        dve.sem_inc(dve_gate, 1)
                        op().then_inc(gn, 1)

                    dve.wait_ge(x_loaded, 16 * (b + 1))
                    for j in range(CPB):
                        nc.vector.bn_stats(st[:, j, :], xn[:, j, :]).then_inc(gn, 1)
                    chain(8, lambda: nc.vector.bn_aggr(mv[:], st[:].rearrange("p n s -> p (n s)")))
                    chain(10, lambda: nc.vector.tensor_tensor(sc[:, 0:1], pX[:, 0, 0:1], mv[:, 0:1], ALU.subtract))
                    chain(11, lambda: nc.vector.tensor_copy(sc[:, 3:4], pX[:, 0, 0:1]))
                    chain(12, lambda: nc.vector.scalar_tensor_tensor(
                        out=sc[:, 1:2], in0=sc[:, 0:1], scalar=sc[:, 0:1], in1=mv[:, 1:2],
                        op0=ALU.mult, op1=ALU.add))
                    chain(14, lambda: nc.vector.tensor_scalar(sc[:, 2:3], pX[:, 1, 0:1], 1e-5, None, ALU.add))
                    chain(17, lambda: nc.vector.tensor_tensor(sc[:, 6:7], sc[:, 5:6], sc[:, 5:6], ALU.mult))
                    chain(18, lambda: nc.vector.scalar_tensor_tensor(
                        out=sc[:, 6:7], in0=sc[:, 6:7], scalar=-0.5, in1=sc[:, 2:3],
                        op0=ALU.mult, op1=ALU.mult))
                    chain(19, lambda: nc.vector.scalar_tensor_tensor(
                        out=sc[:, 7:8], in0=sc[:, 6:7], scalar=1.5, in1=sc[:, 5:6],
                        op0=ALU.add, op1=ALU.mult))
                    chain(20, lambda: nc.vector.tensor_scalar(
                        xn[:].rearrange("p n t -> p (n t)"), xn[:].rearrange("p n t -> p (n t)"),
                        sc[:, 3:4], sc[:, 7:8], ALU.subtract, ALU.mult))
                    for j in range(CPB):
                        dve.wait_ge(hi_done, at(CPB, j + 1))
                        nc.vector.tensor_tensor(parts[:, 1, j * T:(j + 1) * T], xn[:, j, :],
                                                parts[:, 0, j * T:(j + 1) * T], ALU.subtract).then_inc(lo_done, 1)
                        dve.wait_ge(sq_done, done(at(CPB, j + 1)))
                        if j < 2:
                            dve.wait_ge(bn_done, done(at(CPB, 0)))
                            dve.wait_ge(stored[j], 16 * (b * (CPB // 2) + 1))
                        else:
                            dve.wait_ge(diag_step, at(2 * CPB + 1, 2 * j - 2))
                        nc.vector.tensor_tensor(ob[:, j % 2, :].rearrange("p (a b) -> p a b", b=128),
                                                sq[:, j, :].rearrange("p (a b) -> p a b", b=128),
                                                ident[:].unsqueeze(1).to_broadcast([128, TPC, 128]),
                                                ALU.mult).then_inc(diag_step, 1)
                        dve.wait_ge(diag_step, at(2 * CPB + 1, 2 * j + 1))
                        nc.vector.tensor_reduce(sd[:, 0, j * TPC:(j + 1) * TPC],
                                                ob[:, j % 2, :].rearrange("p (a b) -> p a b", b=128), AX_X,
                                                ALU.add).then_inc(diag_step, 1)
                        dve.wait_ge(turned, at(2 * CPB, 2 * j + 2))
                        nc.vector.tensor_copy(rows[:, 1, j * TPC:(j + 1) * TPC, :].rearrange("p a b -> p (a b)"),
                                              pG[:, (2 * j + 1) % 4, :].bitcast(F16)[:, 0:T]).then_inc(rows_lo, 1)
                    dve.wait_ge(diag_step, at(2 * CPB + 1, 2 * CPB))
                    nc.vector.tensor_scalar(sd[:, 1, :], sd[:, 0, :], -128.0, None, ALU.add).then_inc(diag_step, 1)
                    dve.wait_ge(diag_step, at(2 * CPB + 1, 2 * CPB + 1))
                    for k in range(CPB * NT):
                        j, i = divmod(k, NT)
                        dve.wait_ge(gram_full, at(CPB * NT, k + 1))
                        dve.sem_inc(dve_gate, 1)
                        nc.vector.scalar_tensor_tensor(
                            out=inc[:, i, j * T:(j + 1) * T], in0=pG[:, k % 4, :], scalar=sd[:, 1, i:i + 1],
                            in1=sq[:, j, :], op0=ALU.subtract, op1=ALU.is_gt,
                            accum_out=dg[:, i, j:j + 1], saturate=False).then_inc(inc_done, 1)
                    dve.wait_ge(inc_done, done(at(CPB * NT, CPB * NT)))
                    nc.vector.tensor_reduce(inv[:, 0, :], dg[:], AX_X, ALU.add).then_inc(deg_step, 1)
                    dve.wait_ge(deg_step, at(3, 1))
                    nc.vector.tensor_scalar(inv[:, 1, :], inv[:, 0, :], 1.0, None, ALU.max).then_inc(deg_step, 1)
                    dve.wait_ge(deg_step, at(3, 2))
                    nc.vector.reciprocal(inv[:, 2, :], inv[:, 1, :]).then_inc(deg_step, 1)
                    dve.wait_ge(deg_step, at(3, 3))

                    def diagonal(j):
                        if j >= 2:
                            dve.wait_ge(inv_full, at(CPB, j - 1))
                        for t in range(TPC):
                            i = j * TPC + t
                            d = nc.vector.tensor_scalar(tmp[:, j % 2, t * 128:(t + 1) * 128], ident[:],
                                                        inv[:, 2, i:i + 1], None, ALU.mult)
                        d.then_inc(dtile, 1)

                    diagonal(0)
                    for j in range(CPB):
                        if j + 1 < CPB:
                            diagonal(j + 1)
                        dve.wait_ge(inv_done, done(at(CPB, j + 1)))
                        dve.wait_ge(edge_out, done(at(CPB, j + 1)))
                        nc.vector.tensor_tensor(sq[:, j, :], sq[:, j, :], inv_b[:, j, :],
                                                ALU.mult).then_inc(edge_scaled, 1)
                        dve.wait_ge(ehi, at(CPB, j + 1))
                        nc.vector.tensor_tensor(rows[:, 1, j * TPC:(j + 1) * TPC, :].rearrange("p a b -> p (a b)"),
                                                pG[:, j % 4, :],
                                                rows[:, 0, j * TPC:(j + 1) * TPC, :].rearrange("p a b -> p (a b)"),
                                                ALU.subtract).then_inc(elo, 1)
                    for j in range(CPB):
                        dve.wait_ge(vert_full, at(CPB, j + 1))
                        if j >= 2:
                            dve.wait_ge(w_full, at(CPB, j - 1))
                        nc.vector.tensor_tensor(tmp[:, j % 2, :], pE[:, j % 2, :], inv_b[:, j, :],
                                                ALU.mult).then_inc(vert_out, 1)
                        dve.wait_ge(w_full, at(CPB, j + 1))
                        dve.wait_ge(stored[j % 2], 16 * (b * (CPB // 2) + j // 2 + 1))
                        nc.vector.scalar_tensor_tensor(out=ob[:, j % 2, :], in0=pX[:, j % 2, :],
                                                       scalar=bfc[:, 0:1], in1=xn[:, j, :],
                                                       op0=ALU.add, op1=ALU.add).then_inc(ob_ready, 1)
                        dve.wait_ge(ob_ready, done(at(CPB, j + 1)))
                        nc.vector.bn_stats(bn_stats[:, bass.ds(b * CPB + j, 1), :].rearrange("p o s -> p (o s)"),
                                           ob[:, j % 2, :]).then_inc(bn_done, 1)

            @block.gpsimd
            def _(pool):
                with pool.Fori(0, B) as b:
                    for j in range(CPB):
                        pool.wait_ge(gn, b * GN + GN)
                        if j >= 2:
                            pool.wait_ge(sq_full, b * CPB + j - 1)
                        nc.gpsimd.tensor_tensor(tmp[:, j % 2, :], xn[:, j, :], xn[:, j, :],
                                                ALU.mult).then_inc(square_done, 1)


class Banks:

    def __init__(self, nc, ctx, sem, prefix, names, n_banks):
        self.index = {name: k for k, name in enumerate(names)}
        assert len(names) % n_banks == 0
        self.per, self.n = len(names), n_banks
        self.psum = ctx.enter_context(nc.psum_tensor(prefix + "banks", [128, n_banks, T], F32))
        self.filled = sem(prefix + "filled")
        self.free = [sem(f"{prefix}free{k}") for k in range(n_banks)]

    def tile(self, use):
        return self.psum[:, self.index[use] % self.n, :]

    def count(self, use):
        return self.index[use] // self.n

    def wait_free(self, eng, it, use):
        k = self.index[use]
        eng.wait_ge(self.free[k % self.n], done(it * (self.per // self.n) + k // self.n))

    def wait_filled(self, eng, it, use):
        eng.wait_ge(self.filled, it * self.per + self.index[use] + 1)

    def wait_read(self, eng, it, use):
        k = self.index[use]
        eng.wait_ge(self.free[k % self.n], done(it * (self.per // self.n) + k // self.n + 1))

    def wait_to_fill(self, eng, it, use, inputs):
        for i in inputs:
            if (self.index[use] - self.index[i]) % self.n:
                self.wait_read(eng, it, i)
        self.wait_free(eng, it, use)

    def release(self, use):
        return self.free[self.index[use] % self.n]


class Norm:

    def __init__(self, nc, ctx, sem, prefix):
        def sb(name, shape):
            return ctx.enter_context(nc.sbuf_tensor(prefix + name, shape, F32))
        self.stats = sb("stats", [128, B, TPC, 6])
        self.mv = sb("mv", [128, B, TPC, 2])
        self.v = sb("v", [128, 4, B * TPC])
        self.rstd = sb("rstd", [128, B * TPC])
        self.step, self.gate = sem(prefix + "step"), sem(prefix + "gate")

    STEPS = 2 * B + 6

    def vector(self, nc, dve, banks, it, name, out):
        base = it * self.STEPS
        for b in range(B):
            banks.wait_filled(dve, it, (name, b))
            for t in range(TPC):
                i = nc.vector.bn_stats(self.stats[:, b, t, :], banks.tile((name, b))[:, t * 128:(t + 1) * 128])
            i.then_inc(self.step, 1)
        for b in range(B):
            dve.wait_ge(self.step, base + b + 1)
            dve.sem_inc(self.gate, 1)
            for t in range(TPC):
                i = nc.vector.bn_aggr(self.mv[:, b, t, :], self.stats[:, b, t, :])
            i.then_inc(self.step, 1)
        dve.wait_ge(self.step, base + 2 * B)
        nc.vector.tensor_scalar(self.v[:, 0, :], self.mv[:].rearrange("p b t s -> p (b t) s")[:, :, 1],
                                1e-5, None, ALU.add).then_inc(self.step, 1)
        dve.wait_ge(self.step, base + 2 * B + 3)
        nc.vector.tensor_tensor(self.v[:, 3, :], self.v[:, 2, :], self.v[:, 2, :], ALU.mult).then_inc(self.step, 1)
        dve.wait_ge(self.step, base + 2 * B + 4)
        nc.vector.scalar_tensor_tensor(out=self.v[:, 3, :], in0=self.v[:, 3, :], scalar=-0.5,
                                       in1=self.v[:, 0, :], op0=ALU.mult, op1=ALU.mult).then_inc(self.step, 1)
        dve.wait_ge(self.step, base + 2 * B + 5)
        nc.vector.scalar_tensor_tensor(out=self.rstd[:], in0=self.v[:, 3, :], scalar=1.5,
                                       in1=self.v[:, 2, :], op0=ALU.add, op1=ALU.mult).then_inc(self.step, 1)
        dve.wait_ge(self.step, base + 2 * B + 6)
        for b in range(B):
            for t in range(TPC):
                k = b * TPC + t
                i = nc.vector.tensor_scalar(out(b, t), banks.tile((name, b))[:, t * 128:(t + 1) * 128],
                                            self.mv[:, b, t, 0:1], self.rstd[:, k:k + 1],
                                            ALU.subtract, ALU.mult)
            i.then_inc(banks.release((name, b)), 1)

    def scalar(self, nc, act, it):
        base = it * self.STEPS + 2 * B
        act.wait_ge(self.step, base + 1)
        nc.scalar.activation(self.v[:, 1, :], self.v[:, 0, :], ACT.Ln).then_inc(self.step, 1)
        act.wait_ge(self.step, base + 2)
        nc.scalar.activation(self.v[:, 2, :], self.v[:, 1, :], ACT.Exp, scale=-0.5).then_inc(self.step, 1)


def turn(nc, dst, src, ident):
    for t in range(TPC):
        i = nc.tensor.transpose(dst[:, t * 128:(t + 1) * 128], src[:, t * 128:(t + 1) * 128], ident[:])
    return i


def linear_attention(nc, a, bn_stats, x_in, pre_in, x_out, xt_out, logits):
    names = ([("turn1", b) for b in range(B)] + [("back1", b) for b in range(B)]
             + [(w, b) for b in range(B) for w in ("q", "k")]
             + [("v", b) for b in range(B)] + [("kturn", b) for b in range(B)]
             + [("score", b) for b in range(B)]
             + [("kv", h, b) for h in range(2) for b in range(B)]
             + [("out", h, b) for h in range(2) for b in range(B)]
             + [("oturn", b) for b in range(B)] + [("turn2", b) for b in range(B)]
             + [("back2", b) for b in range(B)] + [("gate", b) for b in range(B)])
    with ExitStack() as ctx:
        def sb(name, shape, dt=F32):
            return ctx.enter_context(nc.sbuf_tensor("l_" + name, shape, dt))

        sem = Semaphores(nc, "l_")
        ctx.callback(sem.clear)

        banks = Banks(nc, ctx, sem, "l_", names, 6)
        norm1, norm2 = Norm(nc, ctx, sem, "l_n1"), Norm(nc, ctx, sem, "l_n2")
        xin, pin = sb("xin", [128, B, T]), sb("pin", [128, B, T])
        x2, x3 = sb("x2", [128, B, T]), sb("x3", [128, B, T])
        tok1, ch1 = sb("tok1", [128, B, T]), sb("ch1", [128, B, T])
        tok2, ch2 = sb("tok2", [128, B, T]), sb("ch2", [128, B, T])
        qk = sb("qk", [128, B, 2, T])
        relu = sb("relu", [128, B, 2, T])
        V = sb("V", [128, B, TPC, 129])
        kT = sb("kT", [128, B, T])
        sm = sb("sm", [128, B, T])
        o = sb("o", [128, B, T])
        S = sb("S", [128, B, TPC + 1, 129])
        rd = sb("rd", [128, 2, B, TPC])
        ident, mask = sb("ident", [128, 128]), sb("mask", [128, 128])
        wT = sb("wT", [128, 3 * C])
        bqk = sb("bqk", [128, 2])
        bv = sb("bv", [128, C])
        gwT = sb("gwT", [128, 64])
        gb = sb("gb", [128, 1])
        gamma_beta = sb("gamma_beta", [128, 2])
        mv = sb("bmv", [128, 2])
        bc = sb("bc", [128, 8])
        tick = sb("tick", [128, 32])

        s_w = sem("weights"); started = sem("started"); bn = sem("bn_step"); gate = sem("gate")
        loaded = [sem(f"loaded{b}") for b in range(B)]
        silu_done = sem("silu_done"); x2_ready = sem("x2_ready")
        exp_done = sem("exp_done"); qk_ready = sem("qk_ready"); S_step = sem("S_step")
        den_step = sem("den_step"); x_stored = [sem(f"x_stored{b}") for b in range(B)]
        t_stored = [sem(f"t_stored{b}") for b in range(B)]

        with nc.Block() as block:

            @block.sync
            def _(sp):
                for dst, name in ((ident, "ident"), (mask, "mask"), (wT, "attn2_wT"), (bqk, "attn2_bqk"),
                                  (gwT, "ffn2_gwT"), (gb, "ffn2_gb"), (gamma_beta, "gamma_beta")):
                    sp.dma_start(dst[:], a[name]).then_inc(s_w, 16)
                sp.dma_start(bv[:], a["attn2_bv"].partition_broadcast(128)).then_inc(s_w, 16)
                with sp.Fori(0, CPB) as c:
                    for b in range(B):
                        sp.wait_ge(x2_ready, done(c * B + b + 1 - B))
                        sp.dma_start(xin[:, b, :], x_in[b, :, bass.ds(c * T, T)]).then_inc(loaded[b], 16)
                        sp.dma_start(pin[:, b, :], pre_in[b, :, bass.ds(c * T, T)]).then_inc(loaded[b], 16)
                for b in range(B):
                    sp.wait_ge(loaded[b], 32 * CPB)

            @block.gpsimd
            def _(pool):
                pool.wait_ge(started, 1)
                with pool.Fori(0, CPB) as c:
                    for b in range(B):
                        pool.wait_ge(silu_done, c * B + b + 1)
                        pool.wait_ge(loaded[b], 32 * (c + 1))
                        banks.wait_read(pool, c - 1, ("oturn", b))
                        nc.gpsimd.tensor_tensor(x2[:, b, :], xin[:, b, :], pin[:, b, :],
                                                ALU.add).then_inc(x2_ready, 1)

            @block.tensor
            def _(pe):
                pe.wait_ge(started, 1)
                pe.wait_ge(s_w, 16 * 8)
                with pe.Fori(0, CPB) as c:
                    def fill(use, body, *inputs):
                        banks.wait_to_fill(pe, c, use, inputs)
                        body(banks.tile(use)).then_inc(banks.filled, 1)

                    for b in range(B):
                        pe.wait_ge(x2_ready, done(c * B + b + 1))
                        fill(("turn1", b), lambda p: turn(nc, p, x2[:, b, :], ident))
                    for b in range(B):
                        fill(("back1", b), lambda p: turn(nc, p, tok1[:, b, :], ident), ("turn1", b))
                    for b in range(B):
                        for w in range(2):
                            fill(("qk"[w], b), lambda p: nc.tensor.matmul(
                                p, wT[:, w * C:(w + 1) * C], ch1[:, b, :], start=True, stop=True), ("back1", b))
                    for b in range(B):
                        def values(p):
                            for t in range(TPC):
                                i = nc.tensor.matmul(p[:, t * 128:(t + 1) * 128], ch1[:, b, t * 128:(t + 1) * 128],
                                                     wT[:, 2 * C:], start=True, stop=True)
                            return i
                        fill(("v", b), values)
                    for b in range(B):
                        pe.wait_ge(qk_ready, c * 2 * B + 2 * b + 2)
                        fill(("kturn", b), lambda p: turn(nc, p, qk[:, b, 1, :], ident))
                    for b in range(B):
                        def scores(p):
                            for t in range(TPC):
                                s_ = slice(t * 128, (t + 1) * 128)
                                i = nc.tensor.matmul(p[:, s_], qk[:, b, 1, s_], qk[:, b, 0, s_],
                                                     start=True, stop=True)
                            return i
                        fill(("score", b), scores)
                    for h in range(2):
                        for b in range(B):
                            def state(p):
                                for t in range(2):
                                    tt = 2 * h + t
                                    i = nc.tensor.matmul(p[:, t * 129:(t + 1) * 129],
                                                         kT[:, b, tt * 128:(tt + 1) * 128],
                                                         V[:, b, tt, :], start=True, stop=True)
                                return i
                            fill(("kv", h, b), state, ("kturn", b), ("v", b))
                    for h in range(2):
                        for b in range(B):
                            def outs(p):
                                for t in range(2):
                                    tt = 2 * h + t
                                    s_ = slice(tt * 128, (tt + 1) * 128)
                                    nc.tensor.matmul(p[:, t * 129:(t + 1) * 129], sm[:, b, s_], V[:, b, tt, :],
                                                     start=True, stop=False)
                                    i = nc.tensor.matmul(p[:, t * 129:(t + 1) * 129], qk[:, b, 0, s_],
                                                         S[:, b, tt, :], start=False, stop=True)
                                return i
                            fill(("out", h, b), outs, ("score", b), ("kv", h, b))
                    for b in range(B):
                        fill(("oturn", b), lambda p: turn(nc, p, o[:, b, :], ident), ("out", 1, b))
                    for b in range(B):
                        fill(("turn2", b), lambda p: turn(nc, p, x3[:, b, :], ident), ("oturn", b))
                    for b in range(B):
                        fill(("back2", b), lambda p: turn(nc, p, tok2[:, b, :], ident), ("turn2", b))
                    for b in range(B):
                        r = 64 * (b % 2)
                        fill(("gate", b), lambda p: nc.tensor.matmul(p[r:r + 64, :], gwT[:], ch2[:, b, :],
                                                                     start=True, stop=True), ("back2", b))

            @block.scalar
            def _(act):
                act.wait_ge(bn, 3)
                nc.scalar.activation(bc[:, 1:2], bc[:, 0:1], ACT.Ln).then_inc(bn, 1)
                act.wait_ge(bn, 4)
                nc.scalar.activation(bc[:, 2:3], bc[:, 1:2], ACT.Exp, scale=-0.5).then_inc(bn, 1)
                act.wait_ge(bn, 10)
                with act.Fori(0, CPB) as c:
                    for b in range(B):
                        act.wait_ge(loaded[b], 32 * (c + 1))
                        nc.scalar.activation(pin[:, b, :], pin[:, b, :], ACT.Silu, bias=bc[:, 6:7],
                                             scale=bc[:, 4:5]).then_inc(silu_done, 1)
                    norm1.scalar(nc, act, c)
                    for b in range(B):
                        banks.wait_filled(act, c, ("back1", b))
                        nc.scalar.copy(ch1[:, b, :], banks.tile(("back1", b))).then_inc(banks.release(("back1", b)), 1)
                    for b in range(B):
                        for w in range(2):
                            use = ("qk"[w], b)
                            banks.wait_filled(act, c, use)
                            nc.scalar.activation(qk[:, b, w, :], banks.tile(use), ACT.Exp,
                                                 bias=bqk[:, w:w + 1]).then_inc(exp_done, 1)
                            nc.scalar.activation(relu[:, b, w, :], banks.tile(use), ACT.Relu,
                                                 bias=bqk[:, w:w + 1]).then_inc(banks.release(use), 1)
                    for b in range(B):
                        banks.wait_filled(act, c, ("kturn", b))
                        nc.scalar.copy(kT[:, b, :], banks.tile(("kturn", b))).then_inc(banks.release(("kturn", b)), 1)
                    for b in range(B):
                        banks.wait_read(act, c, ("oturn", b))
                        act.dma_start(x_out[b, :, bass.ds(c * T, T)], x3[:, b, :]).then_inc(x_stored[b], 16)
                    norm2.scalar(nc, act, c)
                    for b in range(B):
                        banks.wait_filled(act, c, ("back2", b))
                        nc.scalar.copy(ch2[:, b, :], banks.tile(("back2", b))).then_inc(banks.release(("back2", b)), 1)
                    for b in range(B):
                        r = 64 * (b % 2)
                        banks.wait_filled(act, c, ("gate", b))
                        nc.scalar.activation(logits[r:r + 64, b // 2, bass.ds(c * T, T)],
                                             banks.tile(("gate", b))[r:r + 64, :], ACT.Identity,
                                             bias=gb[r:r + 64, :]).then_inc(banks.release(("gate", b)), 1)
                    for b in range(B):
                        banks.wait_read(act, c, ("turn2", b))
                        act.dma_start(xt_out[b, bass.ds(c * T, T), :].rearrange("(t p) d -> p t d", p=128),
                                       tok2[:, b, :].rearrange("p (t d) -> p t d", d=C)).then_inc(t_stored[b], 16)
                for b in range(B):
                    act.wait_ge(x_stored[b], 16 * (CPB + 1))
                    act.wait_ge(t_stored[b], 16 * (CPB + 1))

            @block.vector
            def _(dve):
                k = 0
                for s in [x2_ready, S_step] + banks.free:
                    nc.vector.memset(tick[:, k:k + 1], 0.0).then_inc(s, OFF)
                    k += 1
                for s in x_stored + t_stored:
                    nc.vector.memset(tick[:, k:k + 1], 0.0).then_inc(s, 16)
                    k += 1
                nc.vector.memset(V[:, :, :, 128:129], 1.0).then_inc(S_step, 1)
                nc.vector.memset(S[:, :, TPC, :], 0.0).then_inc(S_step, 1)
                nc.vector.memset(tick[:, k:k + 1], 0.0).then_inc(started, 1)
                dve.wait_ge(s_w, 16 * 8)
                nc.vector.bn_aggr(mv[:], bn_stats[:].rearrange("p n s -> p (n s)")).then_inc(bn, 1)
                dve.wait_ge(bn, 1)
                nc.vector.tensor_scalar(bc[:, 0:1], mv[:, 1:2], 1e-5, None, ALU.add).then_inc(bn, 1)
                dve.wait_ge(bn, 2)
                nc.vector.tensor_scalar(bc[:, 7:8], mv[:, 0:1], -1.0, None, ALU.mult).then_inc(bn, 1)
                dve.wait_ge(bn, 5)
                nc.vector.tensor_tensor(bc[:, 3:4], bc[:, 2:3], bc[:, 2:3], ALU.mult).then_inc(bn, 1)
                dve.wait_ge(bn, 6)
                nc.vector.scalar_tensor_tensor(out=bc[:, 3:4], in0=bc[:, 3:4], scalar=-0.5, in1=bc[:, 0:1],
                                               op0=ALU.mult, op1=ALU.mult).then_inc(bn, 1)
                dve.wait_ge(bn, 7)
                nc.vector.scalar_tensor_tensor(out=bc[:, 5:6], in0=bc[:, 3:4], scalar=1.5, in1=bc[:, 2:3],
                                               op0=ALU.add, op1=ALU.mult).then_inc(bn, 1)
                dve.wait_ge(bn, 8)
                nc.vector.tensor_tensor(bc[:, 4:5], bc[:, 5:6], gamma_beta[:, 0:1], ALU.mult).then_inc(bn, 1)
                dve.wait_ge(bn, 9)
                nc.vector.scalar_tensor_tensor(out=bc[:, 6:7], in0=bc[:, 4:5], scalar=bc[:, 7:8],
                                               in1=gamma_beta[:, 1:2], op0=ALU.mult, op1=ALU.add).then_inc(bn, 1)
                with dve.Fori(0, CPB) as c:
                    SP_ = (TPC + 1) * B
                    for b in range(B):
                        dve.wait_ge(S_step, done(2 + c * SP_))
                        banks.wait_read(dve, c - 1, ("out", 1, b))
                        nc.vector.tensor_copy(S[:, b, 0, :], S[:, b, TPC, :]).then_inc(S_step, 1)
                    norm1.vector(nc, dve, banks, c, "turn1", lambda b, t: tok1[:, b, t * 128:(t + 1) * 128])
                    for b in range(B):
                        for w in range(2):
                            dve.wait_ge(exp_done, c * 2 * B + 2 * b + w + 1)
                            banks.wait_read(dve, c, ("qk"[w], b))
                            nc.vector.scalar_tensor_tensor(out=qk[:, b, w, :], in0=qk[:, b, w, :], scalar=1.0,
                                                           in1=relu[:, b, w, :], op0=ALU.min,
                                                           op1=ALU.add).then_inc(qk_ready, 1)
                    for b in range(B):
                        banks.wait_filled(dve, c, ("v", b))
                        nc.vector.tensor_tensor(V[:, b, :, 0:128],
                                                banks.tile(("v", b)).rearrange("p (t d) -> p t d", d=128),
                                                bv[:].unsqueeze(1).to_broadcast([128, TPC, 128]),
                                                ALU.add).then_inc(banks.release(("v", b)), 1)
                    for b in range(B):
                        banks.wait_filled(dve, c, ("score", b))
                        nc.vector.tensor_tensor(sm[:, b, :].rearrange("p (t d) -> p t d", d=128),
                                                banks.tile(("score", b)).rearrange("p (t d) -> p t d", d=128),
                                                mask[:].unsqueeze(1).to_broadcast([128, TPC, 128]),
                                                ALU.mult).then_inc(banks.release(("score", b)), 1)
                    for h in range(2):
                        for t in range(2):
                            tt = 2 * h + t
                            for b in range(B):
                                banks.wait_filled(dve, c, ("kv", h, b))
                                dve.wait_ge(S_step, done(2 + c * SP_ + tt * B + b + 1))
                                i = nc.vector.tensor_tensor(S[:, b, tt + 1, :],
                                                            banks.tile(("kv", h, b))[:, t * 129:(t + 1) * 129],
                                                            S[:, b, tt, :], ALU.add)
                                i.then_inc(S_step, 1)
                        for b in range(B):
                            dve.wait_ge(S_step, done(2 + c * SP_ + (2 * h + 2) * B + b + 1))
                            nc.vector.memset(tick[:, 20 + 4 * h + b:21 + 4 * h + b], 0.0).then_inc(
                                banks.release(("kv", h, b)), 1)
                    for h in range(2):
                        base = (c * 2 + h) * 2 * B
                        for b in range(B):
                            banks.wait_filled(dve, c, ("out", h, b))
                            nc.vector.tensor_scalar(
                                rd[:, 0, b, 0:2], banks.tile(("out", h, b))[:, 0:258].rearrange(
                                    "p (t d) -> p t d", d=129)[:, :, 128], 1e-6, None, ALU.add).then_inc(den_step, 1)
                        for b in range(B):
                            dve.wait_ge(den_step, base + b + 1)
                            nc.vector.reciprocal(rd[:, 1, b, 2 * h:2 * h + 2], rd[:, 0, b, 0:2]).then_inc(den_step, 1)
                        for b in range(B):
                            dve.wait_ge(den_step, base + B + b + 1)
                            for t in range(2):
                                tt = 2 * h + t
                                i = nc.vector.tensor_scalar(o[:, b, tt * 128:(tt + 1) * 128],
                                                            banks.tile(("out", h, b))[:, t * 129:t * 129 + 128],
                                                            rd[:, 1, b, tt:tt + 1], None, ALU.mult)
                            i.then_inc(banks.release(("out", h, b)), 1)
                    for b in range(B):
                        banks.wait_filled(dve, c, ("oturn", b))
                        dve.wait_ge(x_stored[b], 16 * (c + 1))
                        nc.vector.tensor_tensor(x3[:, b, :], banks.tile(("oturn", b)), x2[:, b, :],
                                                ALU.add).then_inc(banks.release(("oturn", b)), 1)
                    for b in range(B):
                        dve.wait_ge(t_stored[b], 16 * (c + 1))
                    norm2.vector(nc, dve, banks, c, "turn2", lambda b, t: tok2[:, b, t * 128:(t + 1) * 128])


def window_states(nc, a, x_in, q_out, states):
    names = ([("turn1", b) for b in range(B)] + [("back1", b) for b in range(B)]
             + [(w, b) for w in ("q", "k", "v") for b in range(B)]
             + [("kv", h, b) for h in range(2) for b in range(B)])
    with ExitStack() as ctx:
        def sb(name, shape, dt=F32):
            return ctx.enter_context(nc.sbuf_tensor("w_" + name, shape, dt))

        sem = Semaphores(nc, "w_")
        ctx.callback(sem.clear)

        banks = Banks(nc, ctx, sem, "w_", names, 7)
        norm = Norm(nc, ctx, sem, "w_n")
        xin = sb("xin", [128, B, T])
        tok1, ch1 = sb("tok1", [128, B, T]), sb("ch1", [128, B, T])
        q = sb("q", [128, B, T])
        k, kz, v = sb("k", [128, B, T]), sb("kz", [128, B, T]), sb("v", [128, B, T])
        ident = sb("ident", [128, 128])
        wT = sb("wT", [128, 3 * C])
        bq = sb("bq", [128, 2])
        bkv = sb("bkv", [128, 2, C])
        ends = sb("ends", [128, 2])
        tick = sb("tick", [128, 16])
        s_w = sem("weights"); started = sem("started"); prep = sem("prep")
        loaded = [sem(f"loaded{b}") for b in range(B)]
        pool_gate = sem("pool_gate"); q_ready = sem("q_ready"); kz_ready = sem("kz_ready")
        stored = [sem(f"stored{b}") for b in range(B)]

        with nc.Block() as block:

            @block.sync
            def _(sp):
                for dst, name in ((ident, "ident"), (wT, "attn3_wT"), (ends, "ends")):
                    sp.dma_start(dst[:], a[name]).then_inc(s_w, 16)
                sp.dma_start(bq[:, 0:1], a["attn3_bq"]).then_inc(s_w, 16)
                sp.dma_start(bkv[:], a["attn3_bkv"].partition_broadcast(128)).then_inc(s_w, 16)
                with sp.Fori(0, CPB) as c:
                    for b in range(B):
                        banks.wait_read(sp, c - 1, ("turn1", b))
                        sp.dma_start(xin[:, b, :], x_in[b, :, bass.ds(c * T, T)]).then_inc(loaded[b], 16)
                    for b in range(B):
                        sp.wait_ge(q_ready, c * B + b + 1)
                        sp.dma_start(q_out[b, :, bass.ds(c * T, T)], q[:, b, :]).then_inc(stored[b], 16)
                for b in range(B):
                    sp.wait_ge(stored[b], 16 * (CPB + 1))

            @block.gpsimd
            def _(pool):
                with pool.Fori(0, CPB) as c:
                    for b in range(B):
                        banks.wait_read(pool, c, ("k", b))
                        banks.wait_read(pool, c - 1, ("kv", 1, b))
                        pool.sem_inc(pool_gate, 1)
                        for e in range(2):
                            i = nc.gpsimd.tensor_scalar(
                                kz[:, b, :].rearrange("p (h e d) -> p h e d", e=2, d=128)[:, :, e, :],
                                k[:, b, :].rearrange("p (h e d) -> p h e d", e=2, d=128)[:, :, e, :],
                                ends[:, e:e + 1], None, ALU.mult)
                        i.then_inc(kz_ready, 1)

            @block.tensor
            def _(pe):
                pe.wait_ge(started, 1)
                pe.wait_ge(s_w, 16 * 5)
                with pe.Fori(0, CPB) as c:
                    def fill(use, body, *inputs):
                        banks.wait_to_fill(pe, c, use, inputs)
                        body(banks.tile(use)).then_inc(banks.filled, 1)

                    for b in range(B):
                        pe.wait_ge(loaded[b], 16 * (c + 1))
                        fill(("turn1", b), lambda p: turn(nc, p, xin[:, b, :], ident))
                    for b in range(B):
                        fill(("back1", b), lambda p: turn(nc, p, tok1[:, b, :], ident), ("turn1", b))
                    for b in range(B):
                        fill(("q", b), lambda p: nc.tensor.matmul(p, wT[:, 0:C], ch1[:, b, :], start=True,
                                                                  stop=True), ("back1", b))
                    for w in range(1, 3):
                        for b in range(B):
                            def by_token(p):
                                for t in range(TPC):
                                    s_ = slice(t * 128, (t + 1) * 128)
                                    i = nc.tensor.matmul(p[:, s_], ch1[:, b, s_], wT[:, w * C:(w + 1) * C],
                                                         start=True, stop=True)
                                return i
                            fill(("qkv"[w], b), by_token)
                    for h in range(2):
                        for b in range(B):
                            if h == 0:
                                pe.wait_ge(kz_ready, c * B + b + 1)
                            def state(p):
                                t0, t1 = (slice(t * 128, (t + 1) * 128) for t in (2 * h, 2 * h + 1))
                                for n, (ka, kb) in enumerate(((k, k), (kz, k), (k, kz))):
                                    dst = p[:, n * 128:(n + 1) * 128]
                                    nc.tensor.matmul(dst, ka[:, b, t0], v[:, b, t0], start=True, stop=False)
                                    i = nc.tensor.matmul(dst, kb[:, b, t1], v[:, b, t1], start=False, stop=True)
                                return i
                            fill(("kv", h, b), state, ("v", b))

            @block.scalar
            def _(act):
                act.wait_ge(prep, 1)
                with act.Fori(0, CPB) as c:
                    norm.scalar(nc, act, c)
                    for b in range(B):
                        banks.wait_filled(act, c, ("back1", b))
                        nc.scalar.copy(ch1[:, b, :], banks.tile(("back1", b))).then_inc(banks.release(("back1", b)), 1)
                    for b in range(B):
                        banks.wait_filled(act, c, ("q", b))
                        act.wait_ge(stored[b], 16 * (c + 1))
                        nc.scalar.activation(q[:, b, :], banks.tile(("q", b)), ACT.Identity, bias=bq[:, 1:2],
                                             scale=float(C) ** -0.5).then_inc(q_ready, 1)
                        act.wait_ge(q_ready, c * B + b + 1)
                        nc.scalar.copy(tick[:, 15:16], ident[:, 0:1]).then_inc(banks.release(("q", b)), 1)
                    for h in range(2):
                        for b in range(B):
                            banks.wait_filled(act, c, ("kv", h, b))
                            nc.scalar.copy(states[:, b, :, bass.ds(c * 2 + h + 1, 1), :].rearrange("p v o d -> p v (o d)"),
                                           banks.tile(("kv", h, b))[:, 0:384].rearrange("p (v d) -> p v d", d=128)
                                           ).then_inc(banks.release(("kv", h, b)), 1)

            @block.vector
            def _(dve):
                n = 0
                for s in banks.free:
                    nc.vector.memset(tick[:, n:n + 1], 0.0).then_inc(s, OFF)
                    n += 1
                for s in stored:
                    nc.vector.memset(tick[:, n:n + 1], 0.0).then_inc(s, 16)
                    n += 1
                nc.vector.memset(states[:, :, :, 0, :], 0.0).then_inc(started, 1)
                nc.vector.memset(states[:, :, :, 2 * CPB + 1, :], 0.0)
                dve.wait_ge(s_w, 16 * 5)
                nc.vector.tensor_scalar(bq[:, 1:2], bq[:, 0:1], float(C) ** -0.5, None, ALU.mult).then_inc(prep, 1)
                with dve.Fori(0, CPB) as c:
                    norm.vector(nc, dve, banks, c, "turn1", lambda b, t: tok1[:, b, t * 128:(t + 1) * 128])
                    for w, dst in ((0, k), (1, v)):
                        for b in range(B):
                            use = ("kv"[w], b)
                            banks.wait_filled(dve, c, use)
                            nc.vector.tensor_tensor(dst[:, b, :].rearrange("p (t d) -> p t d", d=128),
                                                    banks.tile(use).rearrange("p (t d) -> p t d", d=128),
                                                    bkv[:, w, :].unsqueeze(1).to_broadcast([128, TPC, 128]),
                                                    ALU.add).then_inc(banks.release(use), 1)


def window_attention(nc, a, x_in, q_in, states, x_out, xt_out, logits):
    names = ([("att", b) for b in range(B)] + [("turn2", b) for b in range(B)]
             + [("back2", b) for b in range(B)] + [("gate", b) for b in range(B)])
    with ExitStack() as ctx:
        def sb(name, shape, dt=F32):
            return ctx.enter_context(nc.sbuf_tensor("a_" + name, shape, dt))

        sem = Semaphores(nc, "a_")
        ctx.callback(sem.clear)

        banks = Banks(nc, ctx, sem, "a_", names, 8)
        norm = Norm(nc, ctx, sem, "a_n")
        xin, qin = sb("xin", [128, B, T]), sb("qin", [128, B, T])
        x5 = sb("x5", [128, B, T])
        tok2, ch2 = sb("tok2", [128, B, T]), sb("ch2", [128, B, T])
        W = sb("W", [128, B, 2, 2, 128])
        ident = sb("ident", [128, 128])
        gwT = sb("gwT", [128, 64])
        gb = sb("gb", [128, 1])
        tick = sb("tick", [128, 16])
        s_w = sem("weights"); started = sem("started"); W_step = sem("W_step")
        loaded = [sem(f"loaded{b}") for b in range(B)]
        x_stored = [sem(f"x_stored{b}") for b in range(B)]
        t_stored = [sem(f"t_stored{b}") for b in range(B)]

        with nc.Block() as block:

            @block.sync
            def _(sp):
                for dst, name in ((ident, "ident"), (gwT, "ffn3_gwT"), (gb, "ffn3_gb")):
                    sp.dma_start(dst[:], a[name]).then_inc(s_w, 16)
                with sp.Fori(0, CPB) as c:
                    for b in range(B):
                        banks.wait_read(sp, c - 1, ("att", b))
                        sp.dma_start(xin[:, b, :], x_in[b, :, bass.ds(c * T, T)]).then_inc(loaded[b], 16)
                        sp.dma_start(qin[:, b, :], q_in[b, :, bass.ds(c * T, T)]).then_inc(loaded[b], 16)

            @block.gpsimd
            def _(pool):
                pool.wait_ge(started, 1)
                with pool.Fori(0, CPB) as c:
                    def blocks(b, variant, first):
                        return states[:, b, variant, bass.ds(c * 2 + first, 2), :]
                    for b in range(B):
                        banks.wait_read(pool, c - 1, ("att", b))
                        nc.gpsimd.tensor_tensor(W[:, b, 0, :, :], blocks(b, 1, 0), blocks(b, 0, 1),
                                                ALU.add).then_inc(W_step, 1)
                        pool.wait_ge(W_step, (c * B + b) * 2 + 1)
                        nc.gpsimd.tensor_tensor(W[:, b, 1, :, :], W[:, b, 0, :, :], blocks(b, 2, 2),
                                                ALU.add).then_inc(W_step, 1)

            @block.tensor
            def _(pe):
                pe.wait_ge(started, 1)
                pe.wait_ge(s_w, 16 * 3)
                with pe.Fori(0, CPB) as c:
                    def fill(use, body, *inputs):
                        banks.wait_to_fill(pe, c, use, inputs)
                        body(banks.tile(use)).then_inc(banks.filled, 1)

                    for b in range(B):
                        pe.wait_ge(loaded[b], 32 * (c + 1))
                        pe.wait_ge(W_step, (c * B + b) * 2 + 2)
                        def att(p):
                            for h in range(2):
                                s_ = slice(h * 256, (h + 1) * 256)
                                i = nc.tensor.matmul(p[:, s_], W[:, b, 1, h, :], qin[:, b, s_], start=True, stop=True)
                            return i
                        fill(("att", b), att)
                    for b in range(B):
                        fill(("turn2", b), lambda p: turn(nc, p, x5[:, b, :], ident), ("att", b))
                    for b in range(B):
                        fill(("back2", b), lambda p: turn(nc, p, tok2[:, b, :], ident), ("turn2", b))
                    for b in range(B):
                        r = 64 * (b % 2)
                        fill(("gate", b), lambda p: nc.tensor.matmul(p[r:r + 64, :], gwT[:], ch2[:, b, :],
                                                                     start=True, stop=True), ("back2", b))

            @block.scalar
            def _(act):
                with act.Fori(0, CPB) as c:
                    for b in range(B):
                        banks.wait_read(act, c, ("att", b))
                        act.dma_start(x_out[b, :, bass.ds(c * T, T)], x5[:, b, :]).then_inc(x_stored[b], 16)
                    norm.scalar(nc, act, c)
                    for b in range(B):
                        banks.wait_filled(act, c, ("back2", b))
                        nc.scalar.copy(ch2[:, b, :], banks.tile(("back2", b))).then_inc(banks.release(("back2", b)), 1)
                    for b in range(B):
                        r = 64 * (b % 2)
                        banks.wait_filled(act, c, ("gate", b))
                        nc.scalar.activation(logits[r:r + 64, b // 2, bass.ds(c * T, T)],
                                             banks.tile(("gate", b))[r:r + 64, :], ACT.Identity,
                                             bias=gb[r:r + 64, :]).then_inc(banks.release(("gate", b)), 1)
                    for b in range(B):
                        banks.wait_read(act, c, ("turn2", b))
                        act.dma_start(xt_out[b, bass.ds(c * T, T), :].rearrange("(t p) d -> p t d", p=128),
                                      tok2[:, b, :].rearrange("p (t d) -> p t d", d=C)).then_inc(t_stored[b], 16)
                for b in range(B):
                    act.wait_ge(x_stored[b], 16 * (CPB + 1))
                    act.wait_ge(t_stored[b], 16 * (CPB + 1))

            @block.vector
            def _(dve):
                n = 0
                for s in banks.free:
                    nc.vector.memset(tick[:, n:n + 1], 0.0).then_inc(s, OFF)
                    n += 1
                for s in x_stored:
                    nc.vector.memset(tick[:, n:n + 1], 0.0).then_inc(s, 16)
                    n += 1
                for s in t_stored[:3]:
                    nc.vector.memset(tick[:, n:n + 1], 0.0).then_inc(s, 16)
                    n += 1
                nc.vector.memset(tick[:, n:n + 1], 0.0).then_inc(t_stored[3], 16)
                nc.vector.memset(x5[:, 0, 0:1], 0.0).then_inc(started, 1)
                dve.wait_ge(started, 1)
                with dve.Fori(0, CPB) as c:
                    for b in range(B):
                        banks.wait_filled(dve, c, ("att", b))
                        dve.wait_ge(x_stored[b], 16 * (c + 1))
                        nc.vector.tensor_tensor(x5[:, b, :], banks.tile(("att", b)), xin[:, b, :],
                                                ALU.add).then_inc(banks.release(("att", b)), 1)
                    for b in range(B):
                        dve.wait_ge(t_stored[b], 16 * (c + 1))
                    norm.vector(nc, dve, banks, c, "turn2", lambda b, t: tok2[:, b, t * 128:(t + 1) * 128])


def experts(nc, a, tag, x_in, xt, logits, x_out):
    NE, H = 64, 512
    G = 4
    NG = NE // G
    HT = H // 128
    P2 = B // 2
    w1, w2 = a[tag + "w1"], a[tag + "w2"]
    with ExitStack() as ctx:
        def sb(name, shape, dt=F32):
            return ctx.enter_context(nc.sbuf_tensor(tag + name, shape, dt))

        sem = Semaphores(nc, tag)
        ctx.callback(sem.clear)

        W1 = sb("W1", [128, 2, G, H])
        W2 = sb("W2", [128, 2, G, HT * C])
        b1 = sb("b1", [128, NE * HT])
        b2 = sb("b2", [128, NE])
        ident = sb("ident", [128, 128])
        acc = sb("acc", [128, P2, C])
        pT = sb("pT", [128, NE, B])
        oT = sb("oT", [128, B, NE])
        oE = sb("oE", [128, B, C])
        tick = sb("tick", [128, 32])
        s_w = sem("weights")
        w_loaded = [sem("w_loaded0"), sem("w_loaded1")]

        def load_group(sp, g, par):
            sp.dma_start(W1[:, par, :, :], w1[bass.ds(g * G, G), 0:C, :].rearrange("e d h -> d e h")
                         ).then_inc(w_loaded[par], 16)
            sp.dma_start(W2[:, par, :, :], w2[bass.ds(g * G, G), 0:H, :].rearrange("e (p m) o -> p e (m o)", m=HT)
                         ).then_inc(w_loaded[par], 16)

        names = [(w, par, p) for par in range(2) for w in ("mturn", "pool") for p in range(P2)]
        with ExitStack() as c1:
            def sb1(name, shape, dt=F32):
                return c1.enter_context(nc.sbuf_tensor(tag + name, shape, dt))

            banks = Banks(nc, c1, sem, tag + "s_", names, 8)
            rest = sb1("rest", [128, L])
            xtb = sb1("xtb", [128, 2, B, T])
            ms = sb1("ms", [128, 2, P2, T])
            mT = sb1("mT", [128, 2, P2, T])
            sc = sb1("sc", [128, P2, 8])
            top = sb1("top", [128, P2, 8])
            sel = sem("select_step"); started = sem("started"); ms_ready = sem("ms_ready")
            x_loaded = [sem("x_loaded0"), sem("x_loaded1")]
            with nc.Block() as block:

                @block.sync
                def _(sp):
                    sp.dma_start(ident[:], a["ident"]).then_inc(s_w, 16)
                    sp.dma_start(b1[:], a[tag + "b1"]).then_inc(s_w, 16)
                    sp.dma_start(b2[:], a[tag + "b2"]).then_inc(s_w, 16)
                    for par in range(2):
                        load_group(sp, par, par)
                    with sp.Fori(0, CPB // 2) as c2:
                        for par in range(2):
                            for p in range(P2):
                                banks.wait_read(sp, c2 - 1, ("pool", par, p))
                            for b in range(B):
                                sp.dma_start(xtb[:, par, b, :].rearrange("p (t d) -> p t d", d=C),
                                             xt[b, bass.ds((c2 * 2 + par) * T, T), :].rearrange(
                                                 "(t p) d -> p t d", p=128)).then_inc(x_loaded[par], 16)

                @block.vector
                def _(dve):
                    n = 0
                    for s in banks.free:
                        nc.vector.memset(tick[:, n:n + 1], 0.0).then_inc(s, OFF)
                        n += 1
                    nc.vector.memset(tick[:, n:n + 1], 0.0).then_inc(ms_ready, OFF)
                    nc.vector.memset(acc[:], 0.0).then_inc(sel, 1)
                    nc.vector.memset(tick[:, n + 1:n + 2], 0.0).then_inc(started, 1)
                    step = 1
                    for p in range(P2):
                        lg = logits[:, p, :]
                        def chain(op):
                            nonlocal step
                            dve.wait_ge(sel, step)
                            op().then_inc(sel, 1)
                            step += 1
                        chain(lambda: nc.vector.reduce_max(sc[:, p, 0:1], lg, AX_X))
                        chain(lambda: nc.vector.tensor_scalar(sc[:, p, 1:2], sc[:, p, 0:1], -1.0, None, ALU.mult))
                        step += 1
                        chain(lambda: nc.vector.reciprocal(sc[:, p, 3:4], sc[:, p, 2:3]))
                        chain(lambda: nc.vector.tensor_scalar(lg, lg, sc[:, p, 3:4], None, ALU.mult))
                        chain(lambda: nc.vector.max(top[:, p, :], lg))
                        chain(lambda: nc.vector.match_replace(rest[:], top[:, p, :], lg, 0.0))
                        chain(lambda: nc.vector.tensor_tensor(lg, lg, rest[:], ALU.subtract))
                    with dve.Fori(0, CPB // 2) as c2:
                        for par in range(2):
                            for p in range(P2):
                                banks.wait_filled(dve, c2, ("mturn", par, p))
                                nc.vector.tensor_copy(mT[:, par, p, :], banks.tile(("mturn", par, p))).then_inc(
                                    banks.release(("mturn", par, p)), 1)
                            for p in range(P2):
                                banks.wait_filled(dve, c2, ("pool", par, p))
                                banks.wait_read(dve, c2 - (par == 0), ("pool", 1 - par, p))
                                nc.vector.tensor_tensor(acc[:, p, :], acc[:, p, :],
                                                        banks.tile(("pool", par, p))[:, 0:C],
                                                        ALU.add).then_inc(banks.release(("pool", par, p)), 1)

                @block.scalar
                def _(act):
                    for p in range(P2):
                        act.wait_ge(sel, 1 + p * 8 + 2)
                        nc.scalar.activation(logits[:, p, :], logits[:, p, :], ACT.Exp, bias=sc[:, p, 1:2],
                                             accum_out=sc[:, p, 2:3]).then_inc(sel, 1)
                    act.wait_ge(sel, 1 + P2 * 8)
                    with act.Fori(0, CPB // 2) as c2:
                        for par in range(2):
                            for p in range(P2):
                                banks.wait_read(act, c2 - 1, ("mturn", par, p))
                                nc.scalar.copy(ms[:, par, p, :], logits[:, p, bass.ds((c2 * 2 + par) * T, T)]
                                               ).then_inc(ms_ready, 1)

                @block.tensor
                def _(pe):
                    pe.wait_ge(s_w, 48)
                    pe.wait_ge(started, 1)
                    with pe.Fori(0, CPB // 2) as c2:
                        for par in range(2):
                            for p in range(P2):
                                use = ("mturn", par, p)
                                pe.wait_ge(ms_ready, done((c2 * 2 + par) * P2 + p + 1))
                                banks.wait_free(pe, c2, use)
                                turn(nc, banks.tile(use), ms[:, par, p, :], ident).then_inc(banks.filled, 1)
                            pe.wait_ge(x_loaded[par], 16 * B * (c2 + 1))
                            for p in range(P2):
                                use = ("pool", par, p)
                                banks.wait_to_fill(pe, c2, use, [("mturn", par, p)])
                                for h in range(2):
                                    for t in range(TPC):
                                        i = nc.tensor.matmul(
                                            banks.tile(use)[64 * h:64 * h + 64, 0:C],
                                            mT[:, par, p, t * 128 + 64 * h:t * 128 + 64 * h + 64],
                                            xtb[:, par, 2 * p + h, t * 128:(t + 1) * 128],
                                            start=(t == 0), stop=(t == TPC - 1))
                                i.then_inc(banks.filled, 1)

        with ExitStack() as c1:
            def sb1(name, shape, dt=F32):
                return c1.enter_context(nc.sbuf_tensor(tag + name, shape, dt))

            pP = c1.enter_context(nc.psum_tensor(tag + "pP", [128, P2, C], F32))
            pH = c1.enter_context(nc.psum_tensor(tag + "pH", [128, 2, T], F32))
            pO = c1.enter_context(nc.psum_tensor(tag + "pO", [128, 2, T], F32))
            hb = sb1("hb", [128, 2, G * HT, B])
            hg = sb1("hg", [128, 2, G * HT, B])
            pt_full = sem("pt_full"); pt_ready = sem("pt_ready"); pt_free = sem("pt_free")
            h_full = sem("h_full"); hb_ready = sem("hb_ready"); hg_ready = sem("hg_ready")
            o_full = sem("o_full"); o_ready = sem("o_ready")
            ot_full = sem("ot_full"); oe_ready = sem("oe_ready"); zero = sem("oe_zero")
            with nc.Block() as block:

                @block.sync
                def _(sp):
                    with sp.Fori(1, NG // 2) as k:
                        for par in range(2):
                            sp.wait_ge(o_full, k * 2 + par - 1)
                            load_group(sp, k * 2 + par, par)

                @block.tensor
                def _(pe):
                    for p in range(P2):
                        i = nc.tensor.transpose(pP[:, p, :], acc[:, p, :], ident[:])
                    i.then_inc(pt_full, 1)
                    pe.wait_ge(pt_ready, 1)
                    with pe.Fori(0, NG // 2) as k:
                        for par in range(2):
                            pe.wait_ge(w_loaded[par], 32 * (k + 1))
                            pe.wait_ge(hb_ready, done(k * 2 + par - 1))
                            for e in range(G):
                                for m in range(HT):
                                    j = (e * HT + m) * B
                                    i = nc.tensor.matmul(
                                        pH[:, par, j:j + B], W1[:, par, e, m:H:HT],
                                        pT[:, bass.ds((k * 2 + par) * G + e, 1), :].rearrange("p o b -> p (o b)"),
                                        start=True, stop=True)
                            i.then_inc(h_full, 1)
                        for par in range(2):
                            pe.wait_ge(hg_ready, k * 2 + par + 1)
                            pe.wait_ge(o_ready, done(k * 2 + par - 1))
                            for e in range(G):
                                for m in range(HT):
                                    i = nc.tensor.matmul(pO[:, par, e * B:(e + 1) * B],
                                                         W2[:, par, e, m * C:(m + 1) * C],
                                                         hg[:, par, e * HT + m, :],
                                                         start=(m == 0), stop=(m == HT - 1))
                            i.then_inc(o_full, 1)
                    pe.wait_ge(o_ready, done(NG))
                    pe.wait_ge(pt_ready, 1)
                    for p in range(P2):
                        i = nc.tensor.transpose(pP[:, p, :], oT[:, 2 * p:2 * p + 2, :].rearrange("p b e -> p (b e)"),
                                                ident[:])
                    i.then_inc(ot_full, 1)

                @block.scalar
                def _(act):
                    with act.Fori(0, NG // 2) as k:
                        for par in range(2):
                            act.wait_ge(hb_ready, done(k * 2 + par + 1))
                            nc.scalar.activation(hg[:, par, :, :], hb[:, par, :, :], ACT.Gelu).then_inc(hg_ready, 1)

                @block.vector
                def _(dve):
                    nc.vector.memset(tick[:, 20:21], 0.0).then_inc(hb_ready, OFF)
                    nc.vector.memset(tick[:, 21:22], 0.0).then_inc(o_ready, OFF)
                    nc.vector.memset(oE[:], 0.0).then_inc(zero, 1)
                    dve.wait_ge(pt_full, 1)
                    nc.vector.tensor_copy(pT[:].rearrange("p e b -> p b e"),
                                          pP[:].rearrange("p a (b e) -> p (a b) e", e=NE)).then_inc(pt_ready, 1)
                    with dve.Fori(0, NG // 2) as k:
                        for par in range(2):
                            g = k * 2 + par
                            dve.wait_ge(h_full, g + 1)
                            nc.vector.tensor_tensor(hb[:, par, :, :],
                                                    pH[:, par, 0:G * HT * B].rearrange("p (j b) -> p j b", b=B),
                                                    b1[:, bass.ds(g * (G * HT), G * HT)].unsqueeze(2).to_broadcast(
                                                        [128, G * HT, B]), ALU.add).then_inc(hb_ready, 1)
                        for par in range(2):
                            g = k * 2 + par
                            dve.wait_ge(o_full, g + 1)
                            nc.vector.tensor_tensor(oT[:, :, bass.ds(g * G, G)],
                                                    pO[:, par, 0:G * B].rearrange("p (e b) -> p b e", b=B),
                                                    b2[:, bass.ds(g * G, G)].unsqueeze(1).to_broadcast([128, B, G]),
                                                    ALU.add).then_inc(o_ready, 1)
                    dve.wait_ge(ot_full, 1)
                    dve.wait_ge(zero, 1)
                    for b in range(B):
                        r = 64 * (b % 2)
                        nc.vector.tensor_copy(oE[r:r + 64, b, :], pP[r:r + 64, b // 2, :]).then_inc(oe_ready, 1)

        names = [("give", b) for b in range(B)] + [("give2", b) for b in range(B)]
        with ExitStack() as c1:
            banks = Banks(nc, c1, sem, tag + "g_", names, 8)
            xin = c1.enter_context(nc.sbuf_tensor(tag + "xin", [128, 2, B, T], F32))
            xo = c1.enter_context(nc.sbuf_tensor(tag + "xo", [128, 2, B, T], F32))
            loaded = [[sem(f"gl{p}{b}") for b in range(B)] for p in range(2)]
            stored = [[sem(f"gs{p}{b}") for b in range(B)] for p in range(2)]
            go = sem("go")
            WHICH = ("give", "give2")
            with nc.Block() as block:

                @block.sync
                def _(sp):
                    sp.wait_ge(go, 1)
                    with sp.Fori(0, CPB // 2) as c2:
                        for par in range(2):
                            for b in range(B):
                                banks.wait_read(sp, c2 - 1, (WHICH[par], b))
                                sp.dma_start(xin[:, par, b, :], x_in[b, :, bass.ds((c2 * 2 + par) * T, T)]
                                             ).then_inc(loaded[par][b], 16)

                @block.tensor
                def _(pe):
                    pe.wait_ge(go, 1)
                    with pe.Fori(0, CPB // 2) as c2:
                        for par in range(2):
                            for b in range(B):
                                use = (WHICH[par], b)
                                banks.wait_free(pe, c2, use)
                                nc.tensor.matmul(banks.tile(use), oE[:, b, :],
                                                 logits[:, b // 2, bass.ds((c2 * 2 + par) * T, T)],
                                                 start=True, stop=True).then_inc(banks.filled, 1)

                @block.vector
                def _(dve):
                    n = 0
                    for s in banks.free:
                        nc.vector.memset(tick[:, n:n + 1], 0.0).then_inc(s, OFF)
                        n += 1
                    for s in stored[0] + stored[1]:
                        nc.vector.memset(tick[:, n:n + 1], 0.0).then_inc(s, 16)
                        n += 1
                    nc.vector.memset(tick[:, n:n + 1], 0.0).then_inc(go, 1)
                    with dve.Fori(0, CPB // 2) as c2:
                        for par in range(2):
                            for b in range(B):
                                use = (WHICH[par], b)
                                banks.wait_filled(dve, c2, use)
                                dve.wait_ge(loaded[par][b], 16 * (c2 + 1))
                                dve.wait_ge(stored[par][b], 16 * (c2 + 1))
                                nc.vector.tensor_tensor(xo[:, par, b, :], banks.tile(use), xin[:, par, b, :],
                                                        ALU.add).then_inc(banks.release(use), 1)

                @block.scalar
                def _(act):
                    act.wait_ge(go, 1)
                    with act.Fori(0, CPB // 2) as c2:
                        for par in range(2):
                            for b in range(B):
                                banks.wait_read(act, c2, (WHICH[par], b))
                                act.dma_start(x_out[b, :, bass.ds((c2 * 2 + par) * T, T)], xo[:, par, b, :]
                                              ).then_inc(stored[par][b], 16)
                    for par in range(2):
                        for b in range(B):
                            act.wait_ge(stored[par][b], 16 * (CPB // 2 + 1))




def build_program(nc, a, out):
    def scratch(name, shape):
        return nc.dram_tensor(name, shape, F32, kind="Internal").ap()

    x1, pre, x3, x4, x5 = (scratch(n, (B, C, L)) for n in ("x1", "pre", "x3", "x4", "x5"))
    xt, q = scratch("xt", (B, L, C)), scratch("q", (B, C, L))
    mamba(nc, a, a["x"], x1)
    with nc.sbuf_tensor("bn_stats", [C, NCH, 6], F32) as bn_stats:
        hypergraph(nc, a, x1, pre, bn_stats)
        with nc.sbuf_tensor("logits2", [128, B // 2, L], F32) as logits:
            linear_attention(nc, a, bn_stats, x1, pre, x3, xt, logits)
            experts(nc, a, "ffn2_", x3, xt, logits, x4)
    with nc.sbuf_tensor("logits3", [128, B // 2, L], F32) as logits:
        with nc.sbuf_tensor("states", [128, B, 3, 2 * CPB + 2, 128], F32) as states:
            window_states(nc, a, x4, q, states)
            window_attention(nc, a, x4, q, states, x5, xt, logits)
        experts(nc, a, "ffn3_", x5, xt, logits, out)


def kernel(**inputs):
    import numpy as np
    import concourse.bacc as bacc
    from concourse.bass_utils import run_bass_kernel_spmd

    def t(name, shape=None):
        v = np.asarray(inputs[name])
        return np.ascontiguousarray(v if shape is None else shape(v))

    xp = np.asarray(inputs["L0_conv_x_proj_w"]).T
    bc = xp[:, DR:]
    arrays = {
        "x": t("x", lambda v: v.reshape(B, C, L)),
        "ident": np.eye(128, dtype=np.float32),
        "L0_conv_proj_w": t("L0_conv_proj_w"),
        "in_projT": t("L0_conv_in_proj_w", lambda v: v.T),
        "conv_wT": t("L0_conv_conv_w", lambda v: v.reshape(DI, DK).T),
        "x_projT": np.ascontiguousarray(np.concatenate([bc, bc, bc, xp[:, :DR]], axis=1)),
        "dt_projT": t("L0_conv_dt_proj_w", lambda v: v.T),
        "out_projT": t("L0_conv_out_proj_w", lambda v: v.T),
        "conv_b": t("L0_conv_conv_b", lambda v: v.reshape(2, 128).T),
        "dt_b": t("L0_conv_dt_proj_b", lambda v: v.reshape(2, 128).T),
        "D": t("L0_conv_D", lambda v: v.reshape(2, 128).T),
        "A_log": t("L0_conv_A_log"),
        "gmean": np.kron(np.eye(C // 4, dtype=np.float32), np.full((4, 4), 0.25, np.float32)),
        "W_fcT": t("L1_conv_W_fc", lambda v: v.T),
        "gamma_beta": np.ascontiguousarray(np.stack([inputs["L1_conv_gamma"], inputs["L1_conv_beta"]], axis=1)),
        "mask": np.triu(np.ones((128, 128), np.float32)),
        "attn2_wT": t("L2_attn_W", lambda v: v.T),
        "attn2_bqk": t("L2_attn_b", lambda v: v[:2 * C].reshape(2, C).T),
        "attn2_bv": t("L2_attn_b", lambda v: v[2 * C:]),
        "attn3_wT": np.ascontiguousarray(np.concatenate([np.asarray(inputs[f"L3_attn_W{w}"]).T for w in "qkv"], axis=1)),
        "attn3_bq": t("L3_attn_bq", lambda v: v.reshape(C, 1)),
        "attn3_bkv": np.ascontiguousarray(np.stack([inputs["L3_attn_bk"], inputs["L3_attn_bv"]])),
        "ends": np.stack([np.arange(128) > 0, np.arange(128) < 127], axis=1).astype(np.float32),
        "b_fc": t("L1_conv_b_fc", lambda v: v.reshape(C, 1)),
    }
    for n in (2, 3):
        f, g = f"L{n}_ffn_", f"ffn{n}_"
        arrays[g + "gwT"] = t(f + "gate_w", lambda v: v.T)
        arrays[g + "gb"] = t(f + "gate_b", lambda v: np.concatenate([v, v]).reshape(128, 1))
        arrays[g + "w1"] = t(f + "weight1")
        arrays[g + "w2"] = t(f + "weight2")
        arrays[g + "b1"] = t(f + "weight1", lambda v: v[:, C, :].reshape(64, 128, 4).transpose(1, 0, 2).reshape(128, 256))
        arrays[g + "b2"] = t(f + "weight2", lambda v: v[:, 512, :].T)
    nc = bacc.Bacc("TRN2", target_bir_lowering=False, num_devices=1)
    a = {k: nc.dram_tensor("in_" + k, v.shape, F32, kind="ExternalInput").ap() for k, v in arrays.items()}
    out = nc.dram_tensor("out_x", (B, C, L), F32, kind="ExternalOutput").ap()
    build_program(nc, a, out)
    r = run_bass_kernel_spmd(nc, [{"in_" + k: v for k, v in arrays.items()}], core_ids=[0])
    return r.results[0]["out_x"].reshape(B, C, 64, 64)
```

```python
from contextlib import ExitStack

import concourse.bass as bass
from concourse import mybir

ALU = mybir.AluOpType
ACT = mybir.ActivationFunctionType
F32 = mybir.dt.float32
BF16 = mybir.dt.bfloat16
F16 = mybir.dt.float16
F8 = mybir.dt.float8e4
AX_X = mybir.AxisListType.X

B = 4
C = 128
L = 4096
T = 512
CPB = L // T
NCH = B * CPB
DI, DS, DR, DK = 256, 16, 8, 4
HALO = DK - 1
TPC = T // 128

OFF = 8


def done(k):
    return OFF + k


class Semaphores:

    def __init__(self, nc, prefix):
        self.nc, self.prefix, self.handles = nc, prefix, []

    def __call__(self, name):
        s = self.nc.alloc_semaphore(self.prefix + name)
        self.handles.append(s)
        return s

    def clear(self):
        self.nc.clear_and_free_semaphores(self.handles)
        self.nc.all_engine_barrier()


def mamba(nc, a, x_in, x_out):
    U = 2 * DS
    R = 8
    GR = 4
    ND, NX, NP = 8, 8, 8
    LB, LS, NS = 6, 4, 8
    with ExitStack() as ctx:
        def sb(name, shape, dt=F32):
            return ctx.enter_context(nc.sbuf_tensor("m_" + name, shape, dt))

        def ps(name, shape):
            return ctx.enter_context(nc.psum_tensor("m_" + name, shape, F32))

        sem = Semaphores(nc, "m_")
        ctx.callback(sem.clear)

        xh = sb("xh", [C, NCH + 2, HALO + T])
        hs = sb("hs", [128, R, T])
        carry = sb("carry", [128, U])
        xc = sb("xc", [128, 2, T])
        sz = sb("sz", [128, 2, T])
        delta = sb("delta", [128, 2, 2, T])
        dtx = sb("dtx", [128, 2, 2, T])
        dtr = sb("dtr", [128, T])
        parts = sb("parts", [96, 2, T], BF16)
        resid = sb("resid", [64, T])
        Bs = sb("Bs", [128, NS, T])
        dA = sb("dA", [128, ND, T])
        dBx = sb("dBx", [128, NX, T])
        prod = sb("prod", [128, NP, T])
        sp_a = sb("sp_a", [128, 2, T])
        sp_r = sb("sp_r", [128, 2, T])
        ob = sb("ob", [128, T])
        ident = sb("ident", [128, 128])
        projw = dBx[:, 1, 0:C]
        inpT = dBx[:, 0, :]
        cwb = prod[:, 0:2, :].rearrange("p a (b d) -> p (a b) d", b=2)
        Wx = sb("Wx", [128, DK, DI])
        Wz = sb("Wz", [128, DI])
        xpT = sb("xpT", [128, 2, 104])
        dtT = sb("dtT", [128, DI])
        opT = sb("opT", [128, 2, C])
        diagD = sb("diagD", [128, 2, 128])
        E = sb("E", [96, 2, 32])
        Eb = sb("Eb", [96, 32], BF16)
        sel = sb("sel", [96, 32, 128], BF16)
        cb = sb("cb", [128, 2])
        dtb = sb("dtb", [128, 2])
        Dc = sb("Dc", [128, 2])
        Al = sb("Al", [128, 2, DS])
        Ae = sb("Ae", [128, 2, DS])
        An = sb("An", [128, 2, DS])
        tick = sb("tick", [128, 16])

        pC = ps("pC", [128, 2, T])
        pB = ps("pB", [128, 2, T])
        pY = ps("pY", [128, 2, T])
        pM = ps("pM", [128, 2, T])

        s_w = sem("weights"); s_x0 = sem("x_first"); s_xr = sem("x_rest")
        s_wc = sem("w_product"); s_prep = sem("w_ready"); s_edge = sem("zeros")
        misc_full = sem("misc_full"); misc_free = [sem("misc_free0"), sem("misc_free1")]
        xc_ready = sem("xc_ready"); sz_ready = sem("sz_ready"); D_done = sem("D_done")
        hi_ready = sem("hi_ready"); split_step = sem("split_step"); parts_ready = sem("parts_ready")
        act_step = sem("act_step"); sp_ready = sem("sp_ready")
        delta_ready = sem("delta_ready"); dtx_ready = sem("dtx_ready")
        B_full = sem("B_full"); Bs_ready = sem("Bs_ready"); C_full = sem("C_full")
        dA_ready = sem("dA_ready"); dBx_ready = sem("dBx_ready"); scan_done = sem("scan_done")
        carried = sem("carried"); h_zero = sem("h_zero")
        prod_ready = sem("prod_ready"); y_added = sem("y_added"); yg_ready = sem("yg_ready")
        stored = sem("stored"); started = sem("started"); out_ready = sem("out_ready")

        MP, MI = 5, 8
        M_C, M_OUT, M_Z, M_XD, M_DT = (0, 2), 1, (3, 4), 5, (6, 7)

        def bank(m):
            return (MP + m) % 2

        def number(it, m):
            return it * MI + MP + m, it * (MI // 2) + (MP + m) // 2

        x_src = [x_in[b].rearrange("c (n t) -> c n t", t=T) for b in range(B)]

        def tile_of(i, lo, hi):
            return xh[:, bass.ds(i, 1), lo:hi].rearrange("c o t -> c (o t)")

        with nc.Block() as block:

            @block.sync
            def _(sp):
                def load(b, s):
                    sp.dma_start(xh[:, b * CPB + 1:(b + 1) * CPB + 1, HALO:], x_src[b]).then_inc(s, 16)
                    sp.dma_start(xh[:, b * CPB + 2:(b + 1) * CPB + 1, 0:HALO],
                                 x_src[b][:, 0:CPB - 1, T - HALO:T]).then_inc(s, 16)
                sp.dma_start(ident[:], a["ident"]).then_inc(s_w, 16)
                sp.dma_start(projw, a["L0_conv_proj_w"]).then_inc(s_w, 16)
                sp.dma_start(inpT, a["in_projT"]).then_inc(s_w, 16)
                sp.dma_start(cwb, a["conv_wT"].partition_broadcast(128)).then_inc(s_w, 16)
                load(0, s_x0)
                sp.dma_start(xpT[:], a["x_projT"].rearrange("(h p) m -> p h m", p=128)).then_inc(s_w, 16)
                sp.dma_start(dtT[96:104, :], a["dt_projT"]).then_inc(s_w, 16)
                sp.dma_start(opT[:], a["out_projT"].rearrange("(h p) m -> p h m", p=128)).then_inc(s_w, 16)
                sp.dma_start(cb[:], a["conv_b"]).then_inc(s_w, 16)
                sp.dma_start(dtb[:], a["dt_b"]).then_inc(s_w, 16)
                sp.dma_start(Dc[:], a["D"]).then_inc(s_w, 16)
                sp.dma_start(Al[:], a["A_log"].rearrange("(h p) n -> p h n", p=128)).then_inc(s_w, 16)
                for b in range(1, B):
                    load(b, s_xr)
                with sp.Fori(0, B) as b:
                    with sp.Fori(0, CPB) as c:
                        it = b * CPB + c
                        sp.wait_ge(out_ready, it + 2)
                        sp.dma_start(x_out[bass.ds(b, 1), :, bass.ds(c * T, T)].rearrange("o c t -> c (o t)"),
                                     ob[:]).then_inc(stored, 16)
                sp.wait_ge(stored, 16 * (NCH + 2))

            @block.tensor
            def _(pe):
                def misc(it, m, body):
                    pe.wait_ge(misc_free[bank(m)], done(number(it, m)[1]))
                    body(pM[:, bank(m), :]).then_inc(misc_full, 1)

                def conv(it, m, q, half):
                    def body(out):
                        for tap in range(DK):
                            p = nc.tensor.matmul(out, Wx[:, tap, half * 128:(half + 1) * 128],
                                                 tile_of(q + 1, tap, tap + T),
                                                 start=(tap == 0), stop=(tap == DK - 1))
                        return p
                    misc(it, m, body)

                def xdbl(it, m, q):
                    pe.wait_ge(xc_ready, q + 1)
                    def body(out):
                        for h in range(2):
                            p = nc.tensor.matmul(out[0:104, :], xpT[:, h, :], xc[:, h, :],
                                                 start=(h == 0), stop=(h == 1))
                        return p
                    misc(it, m, body)

                def dt(it, m, q, half):
                    pe.wait_ge(hi_ready, 2 * q + 2)
                    misc(it, m, lambda out: nc.tensor.matmul(out, dtT[96:104, half * 128:(half + 1) * 128],
                                                             dtr[96:104, :], start=True, stop=True))

                def finish(it, m):
                    def body(out):
                        nc.tensor.matmul(out, opT[:, 0, :], sz[:, 0, :], start=True, stop=False)
                        return nc.tensor.matmul(out, opT[:, 1, :], sz[:, 1, :], start=False, stop=True)
                    misc(it, m, body)

                def spread_b(g, par, n):
                    nc.tensor.matmul(pB[:, n % 2, :], sel[:, n, :], parts[:, par, :], start=True,
                                     stop=True).then_inc(B_full, 1)

                def spread_c(g, par, n):
                    nc.tensor.matmul(pC[:, n % 2, :], sel[:, DS + n, :], parts[:, par, :], start=True,
                                     stop=True).then_inc(C_full, 1)

                pe.wait_ge(s_w, 16 * 11)
                nc.tensor.matmul(pM[:, 0, :], projw, inpT, start=True, stop=True).then_inc(s_wc, 1)
                pe.wait_ge(s_prep, 9)
                pe.wait_ge(started, 3)
                pe.wait_ge(s_edge, 4)
                for half in range(2):
                    nc.tensor.matmul(pY[:, half, :], ident[:], xh[:, 0, HALO:], start=True,
                                     stop=True).then_inc(y_added, OFF // 2)
                pe.wait_ge(s_x0, 32)
                for half in range(2):
                    conv(0, half - MP, 0, half)
                xdbl(0, 2 - MP, 0)
                for half in range(2):
                    dt(0, 3 + half - MP, 0, half)
                pe.wait_ge(parts_ready, 1)
                spread_c(0, 0, 0)
                for n in range(LB):
                    if n >= 2:
                        pe.wait_ge(Bs_ready, n - 1)
                    spread_b(n, 0, n)
                with pe.Fori(0, B) as b:
                    with pe.Fori(0, CPB // 2) as c2:
                        for par in range(2):
                            it = b * CPB + c2 * 2 + par
                            g0 = it * U

                            def add(u):
                                pe.wait_ge(prod_ready, done(g0 + u + 1))
                                nc.tensor.matmul(pY[:, u % 2, :], ident[:], prod[:, u % NP, :],
                                                 start=False, stop=(u >= U - 2)).then_inc(y_added, 1)

                            for u in range(U):
                                n = u // 2
                                if u % 2 == 0:
                                    g = it * DS + n
                                    if n + LB == DS:
                                        pe.wait_ge(parts_ready, it + 2)
                                    pe.wait_ge(Bs_ready, g + LB - 1)
                                    spread_b(g + LB, par if n + LB < DS else 1 - par, (n + LB) % DS)
                                    pe.wait_ge(prod_ready, done(2 * g))
                                    spread_c(g + 1, par if n + 1 < DS else 1 - par, (n + 1) % DS)
                                if u == 0:
                                    conv(it, M_C[0], it + 1, 0)
                                    for half in range(2):
                                        pe.wait_ge(yg_ready, done(2 * it + 2))
                                        nc.tensor.matmul(pY[:, half, :], diagD[:, half, :], xc[:, half, :],
                                                         start=True, stop=False).then_inc(D_done, 1)
                                if u == 2:
                                    finish(it, M_OUT)
                                if u == 4:
                                    conv(it, M_C[1], it + 1, 1)
                                if u == 16:
                                    pe.wait_ge(s_xr, 32 * (B - 1))
                                for half in range(2):
                                    if u == 6 + 2 * half:
                                        misc(it, M_Z[half], lambda out: nc.tensor.matmul(
                                            out, Wz[:, half * 128:(half + 1) * 128],
                                            tile_of(it + 1, HALO, HALO + T), start=True, stop=True))
                                    if u == 15 + half:
                                        dt(it, M_DT[half], it + 1, half)
                                if u == 12:
                                    xdbl(it, M_XD, it + 1)
                                if u >= 1:
                                    add(u - 1)
                            add(U - 1)
                pe.wait_ge(yg_ready, done(2 * NCH + 2))
                finish(NCH, 0)

            @block.scalar
            def _(act):
                def raw(it, m, out, bias=0.0):
                    act.wait_ge(misc_full, number(it, m)[0] + 1)
                    nc.scalar.activation(out, pM[:, bank(m), :], ACT.Identity,
                                         bias=bias).then_inc(misc_free[bank(m)], 1)

                def conv(it, m, q, half):
                    act.wait_ge(D_done, 2 * q)
                    act.wait_ge(dtx_ready, 2 * q)
                    raw(it, m, xc[:, half, :], cb[:, half:half + 1])

                def xdbl(it, m, q, par):
                    act.wait_ge(misc_full, number(it, m)[0] + 1)
                    nc.scalar.copy(dtr[96:104, :], pM[96:104, bank(m), :]).then_inc(hi_ready, 1)
                    nc.scalar.copy(parts[:, par, :], pM[0:96, bank(m), :]).then_inc(hi_ready, 1)

                def softplus(it, m, q, half):
                    act.wait_ge(dtx_ready, 2 * q)
                    act.wait_ge(misc_full, number(it, m)[0] + 1)
                    t = sp_a[:, half, :]
                    nc.scalar.activation(t, pM[:, bank(m), :], ACT.Abs,
                                         bias=dtb[:, half:half + 1]).then_inc(act_step, 1)
                    nc.scalar.activation(sp_r[:, half, :], pM[:, bank(m), :], ACT.Relu,
                                         bias=dtb[:, half:half + 1]).then_inc(misc_free[bank(m)], 1)
                    act.wait_ge(act_step, 4 * q + 2 * half + 1)
                    nc.scalar.activation(t, t, ACT.Exp, scale=-1.0).then_inc(act_step, 1)

                def softplus_log(q):
                    act.wait_ge(act_step, 4 * q + 4)
                    t = sp_a[:].rearrange("p h t -> p (h t)")
                    nc.scalar.activation(t, t, ACT.Ln, bias=1.0).then_inc(sp_ready, 1)

                def silu(tile, it, uses, ready):
                    for m in uses:
                        act.wait_ge(misc_free[bank(m)], done(number(it, m)[1] + 1))
                    t = tile[:].rearrange("p h t -> p (h t)")
                    nc.scalar.activation(t, t, ACT.Silu).then_inc(ready, 1)

                def copy_b(g, n):
                    act.wait_ge(B_full, g + 1)
                    nc.scalar.copy(Bs[:, n % NS, :], pB[:, n % 2, :]).then_inc(Bs_ready, 1)

                act.wait_ge(s_w, 16 * 11)
                nc.scalar.activation(Ae[:], Al[:], ACT.Exp).then_inc(s_wc, 1)
                act.wait_ge(s_prep, 9)
                for half in range(2):
                    raw(0, half - MP, xc[:, half, :], cb[:, half:half + 1])
                silu(xc, 0, (-MP, 1 - MP), xc_ready)
                xdbl(0, 2 - MP, 0, 0)
                for half in range(2):
                    softplus(0, 3 + half - MP, 0, half)
                softplus_log(0)
                for n in range(LS):
                    copy_b(n, n)
                with act.Fori(0, B) as b:
                    with act.Fori(0, CPB // 2) as c2:
                        for par in range(2):
                            it = b * CPB + c2 * 2 + par
                            g0 = it * U
                            for u in range(U):
                                n, half = u // 2, u % 2
                                if half == 1:
                                    act.wait_ge(dBx_ready, done(2 * (it * DS + n + LS - NS + 1)))
                                    copy_b(it * DS + n + LS, (n + LS) % DS)
                                act.wait_ge(delta_ready, 2 * it + 2)
                                act.wait_ge(scan_done, done(g0 + u - ND + 1))
                                nc.scalar.activation(dA[:, u % ND, :], delta[:, par, half, :], ACT.Exp,
                                                     scale=An[:, half, n:n + 1]).then_inc(dA_ready, 1)
                                for hf in range(2):
                                    if u == 7 + 2 * hf:
                                        conv(it, M_C[hf], it + 1, hf)
                                    if u == 11 + 2 * hf:
                                        raw(it, M_Z[hf], sz[:, hf, :])
                                    if u == 20 + hf:
                                        softplus(it, M_DT[hf], it + 1, hf)
                                if u == 8:
                                    act.wait_ge(stored, 16 * (it + 1))
                                    raw(it, M_OUT, ob[:])
                                if u == 14:
                                    silu(xc, it, M_C, xc_ready)
                                    silu(sz, it, M_Z, sz_ready)
                                if u == 17:
                                    xdbl(it, M_XD, it + 1, 1 - par)
                                if u == 22:
                                    softplus_log(it + 1)
                act.wait_ge(stored, 16 * (NCH + 1))
                raw(NCH, 0, ob[:])

            @block.vector
            def _(dve):
                for k, s in enumerate((*misc_free, scan_done, prod_ready, yg_ready, sz_ready, carried)):
                    nc.vector.memset(tick[:, 4 + k:5 + k], 0.0).then_inc(s, OFF)
                nc.vector.memset(tick[:, 12:13], 0.0).then_inc(stored, 32)
                nc.vector.memset(tick[:, 11:12], 0.0).then_inc(started, 1)
                nc.vector.memset(xh[:, 1:NCH + 1:CPB, 0:HALO], 0.0).then_inc(s_edge, 1)
                nc.vector.memset(xh[:, 0, :], 0.0).then_inc(s_edge, 1)
                nc.vector.memset(xh[:, NCH + 1, :], 0.0).then_inc(s_edge, 1)
                nc.vector.memset(sz[:], 0.0).then_inc(s_edge, 1)
                dve.wait_ge(s_w, 16 * 11)
                dve.wait_ge(s_wc, 2)
                for tap in range(DK):
                    nc.vector.tensor_tensor(Wx[:, tap, :], pM[:, 0, 0:DI], cwb[:, tap, :],
                                            ALU.mult).then_inc(s_prep, 1)
                nc.vector.tensor_copy(Wz[:], pM[:, 0, DI:2 * DI]).then_inc(s_prep, 1)
                nc.vector.tensor_scalar(An[:], Ae[:], -1.0, None, ALU.mult).then_inc(s_prep, 1)
                for half in range(2):
                    nc.vector.tensor_scalar(diagD[:, half, :], ident[:], Dc[:, half:half + 1], None,
                                            ALU.mult).then_inc(s_prep, 1)
                nc.vector.tensor_tensor(E[:, 0, :], ident[0:96, 0:32], ident[0:96, 32:64],
                                        ALU.add).then_inc(split_step, 1)
                dve.wait_ge(split_step, 1)
                nc.vector.tensor_tensor(Eb[:], E[:, 0, :], ident[0:96, 64:96], ALU.add).then_inc(split_step, 1)
                dve.wait_ge(split_step, 2)
                nc.vector.tensor_copy(sel[:], Eb[:].unsqueeze(2).to_broadcast([96, 32, 128])).then_inc(s_prep, 1)

                def split(it, m, q, par):
                    dve.wait_ge(hi_ready, 2 * q + 2)
                    nc.vector.tensor_tensor(resid[:], pM[0:64, bank(m), :], parts[0:64, par, :],
                                            ALU.subtract).then_inc(misc_free[bank(m)], 1)
                    dve.wait_ge(misc_free[bank(m)], done(number(it, m)[1] + 1))
                    nc.vector.tensor_copy(parts[0:64, par, :], resid[:]).then_inc(split_step, 1)
                    dve.wait_ge(split_step, 2 + q + 1)
                    nc.vector.tensor_tensor(parts[0:32, par, :], resid[0:32, :], parts[0:32, par, :],
                                            ALU.subtract).then_inc(parts_ready, 1)

                def gate(it):
                    dve.wait_ge(sz_ready, done(it))
                    dve.wait_ge(y_added, done(it * U))
                    for half in range(2):
                        nc.vector.tensor_tensor(sz[:, half, :], pY[:, half, :], sz[:, half, :],
                                                ALU.mult).then_inc(yg_ready, 1)

                split(0, 2 - MP, 0, 0)
                with dve.Fori(0, B) as b:
                    dve.wait_ge(prod_ready, done(b * (CPB * U)))
                    nc.vector.memset(hs[:, R - GR:R, T - 1:T], 0.0).then_inc(h_zero, 1)
                    dve.wait_ge(carried, done(b * (CPB * (U // GR))))
                    nc.vector.memset(carry[:, 0:U - GR], 0.0).then_inc(h_zero, 1)
                    with dve.Fori(0, CPB // 2) as c2:
                        for par in range(2):
                            it = b * CPB + c2 * 2 + par
                            g0 = it * U

                            def product(u):
                                n = u // 2
                                dve.wait_ge(C_full, it * DS + n + 1)
                                dve.wait_ge(scan_done, done(g0 + u + 1))
                                dve.wait_ge(y_added, done(g0 + u - NP + 1))
                                nc.vector.tensor_tensor(prod[:, u % NP, :], hs[:, u % R, :], pC[:, n % 2, :],
                                                        ALU.mult).then_inc(prod_ready, 1)

                            def carry_on(group, u_end):
                                dve.wait_ge(scan_done, done(g0 + u_end))
                                s0 = group * GR % R
                                nc.vector.tensor_copy(carry[:, group * GR:(group + 1) * GR],
                                                      hs[:, s0:s0 + GR, T - 1:T].rearrange("p a o -> p (a o)")
                                                      ).then_inc(carried, 1)

                            for u in range(U):
                                if u == 0:
                                    dve.wait_ge(h_zero, 2 * b + 2)
                                if u % GR == 0:
                                    dve.wait_ge(carried, done(it * (U // GR) + u // GR))
                                    dve.wait_ge(prod_ready, done(g0 + u - 1))
                                dve.wait_ge(dA_ready, g0 + u + 1)
                                dve.wait_ge(dBx_ready, done(g0 + u + 1))
                                nc.vector.tensor_tensor_scan(hs[:, u % R, :], dA[:, u % ND, :], dBx[:, u % NX, :],
                                                             carry[:, u:u + 1], ALU.mult, ALU.add).then_inc(scan_done, 1)
                                if u >= 1:
                                    product(u - 1)
                                if u == 1:
                                    gate(it)
                                if u == 2:
                                    carry_on(U // GR - 1, 0)
                                for group in range(U // GR - 1):
                                    if u == (group + 1) * GR + 2:
                                        carry_on(group, (group + 1) * GR)
                                if u == 15:
                                    split(it, M_XD, it + 1, 1 - par)
                            product(U - 1)
                gate(NCH)

            @block.gpsimd
            def _(pool):
                def dt_x(q, par, half, step):
                    if step == 0:
                        pool.wait_ge(sp_ready, q + 1)
                        nc.gpsimd.tensor_tensor(delta[:, par, half, :], sp_a[:, half, :], sp_r[:, half, :],
                                                ALU.add).then_inc(delta_ready, 1)
                    else:
                        pool.wait_ge(delta_ready, 2 * q + half + 1)
                        pool.wait_ge(xc_ready, q + 1)
                        nc.gpsimd.tensor_tensor(dtx[:, par, half, :], delta[:, par, half, :], xc[:, half, :],
                                                ALU.mult).then_inc(dtx_ready, 1)

                def add_x(it, m):
                    pool.wait_ge(misc_free[bank(m)], done(number(it, m)[1] + 1))
                    nc.gpsimd.tensor_tensor(ob[:], ob[:], tile_of(it, HALO, HALO + T),
                                            ALU.add).then_inc(out_ready, 1)

                nc.gpsimd.memset(tick[:, 3:4], 0.0).then_inc(dBx_ready, OFF)
                nc.gpsimd.memset(tick[:, 2:3], 0.0).then_inc(started, 2)
                for half in range(2):
                    dt_x(0, 0, half, 0)
                    dt_x(0, 0, half, 1)
                with pool.Fori(0, B) as b:
                    with pool.Fori(0, CPB // 2) as c2:
                        for par in range(2):
                            it = b * CPB + c2 * 2 + par
                            g0 = it * U
                            for u in range(U):
                                n, half = u // 2, u % 2
                                pool.wait_ge(Bs_ready, it * DS + n + 1)
                                pool.wait_ge(dtx_ready, 2 * it + half + 1)
                                pool.wait_ge(scan_done, done(g0 + u - NX + 1))
                                nc.gpsimd.tensor_tensor(dBx[:, u % NX, :], dtx[:, par, half, :], Bs[:, n % NS, :],
                                                        ALU.mult).then_inc(dBx_ready, 1)
                                if u == 10:
                                    add_x(it, M_OUT)
                                if u in (24, 26, 28, 30):
                                    dt_x(it + 1, 1 - par, (u - 24) // 2 % 2, (u - 24) // 4)
                add_x(NCH, 0)


def hypergraph(nc, a, x_in, pre_out, bn_stats):
    NT = L // 128
    TPC = T // 128
    with ExitStack() as ctx:
        def sb(name, shape, dt=F32):
            return ctx.enter_context(nc.sbuf_tensor("h_" + name, shape, dt))

        def ps(name, shape):
            return ctx.enter_context(nc.psum_tensor("h_" + name, shape, F32))

        sem = Semaphores(nc, "h_")
        ctx.callback(sem.clear)

        inc = sb("inc", [128, NT, L], F8)
        xn = sb("xn", [128, CPB, T])
        parts = sb("parts", [128, 2, L], F16)
        inv_b = parts[:].rearrange("p a l -> p (a l)").bitcast(F32).rearrange("p (n t) -> p n t", t=T)
        rows = sb("rows", [128, 2, NT, 128], F16)
        sq = sb("sq", [128, CPB, T])
        tmp = sb("tmp", [128, 2, T])
        ob = sb("ob", [128, 2, T])
        ident = sb("ident", [128, 128])
        ident16 = sb("ident16", [128, 128], F16)
        ones = sb("ones", [128, 128])
        halves = sb("halves", [128, 128])
        gmean = sb("gmean", [128, 128])
        wfcT = sb("wfcT", [128, 128])
        bfc = sb("bfc", [128, 1])
        st = sb("st", [128, CPB, 6])
        mv = sb("mv", [128, 2])
        tick = sb("tick", [128, 16])
        sc = sb("sc", [128, 8])
        sd = sb("sd", [128, 2, NT])
        dg = sb("dg", [128, NT, CPB])
        inv = sb("inv", [128, 3, NT])
        pG = ps("pG", [128, 4, T])
        pE = ps("pE", [128, 2, T])
        pX = ps("pX", [128, 2, T])

        s_w = sem("weights"); w_ready = sem("w_ready"); started = sem("started")
        x_loaded = [sem(f"x_loaded{j}") for j in range(CPB)]; gn = sem("gn_step")
        hi_done = sem("hi_done"); lo_done = sem("lo_done"); square_done = sem("square_done")
        sq_full = sem("sq_full"); sq_done = sem("sq_done"); diag_step = sem("diag_step")
        turned = sem("turned"); rows_hi = sem("rows_hi"); rows_lo = sem("rows_lo")
        gram_full = sem("gram_full"); inc_done = sem("inc_done"); edge_full = sem("edge_full")
        edge_out = sem("edge_out"); deg_step = sem("deg_step"); dtile = sem("dtile")
        inv_full = sem("inv_full"); inv_done = sem("inv_done"); edge_scaled = sem("edge_scaled")
        turn_full = sem("turn_full"); edge_turned = sem("edge_turned"); ehi = sem("ehi"); elo = sem("elo")
        vert_full = sem("vert_full"); vert_out = sem("vert_out")
        w_full = sem("w_full"); ob_ready = sem("ob_ready"); bn_done = sem("bn_done"); stored = [sem("stored0"), sem("stored1")]

        pe_gate = sem("pe_gate"); dve_gate = sem("dve_gate")

        LAG = 3
        GN = 21

        with nc.Block() as block:

            @block.sync
            def _(sp):
                for dst, name in ((ident, "ident"), (gmean, "gmean"), (wfcT, "W_fcT"), (bfc, "b_fc")):
                    sp.dma_start(dst[:], a[name]).then_inc(s_w, 16)
                for j in range(CPB):
                    sp.dma_start(xn[:, j, :], x_in[0, :, j * T:(j + 1) * T]).then_inc(x_loaded[j], 16)

                def outputs(b, more):
                    for j in range(CPB):
                        sp.wait_ge(ob_ready, done(b * CPB + j + 1))
                        sp.dma_start(pre_out[bass.ds(b, 1), :, j * T:(j + 1) * T].rearrange("o c t -> c (o t)"),
                                     ob[:, j % 2, :]).then_inc(stored[j % 2], 16)
                        if more:
                            sp.dma_start(xn[:, j, :], x_in[bass.ds(b + 1, 1), :, j * T:(j + 1) * T].rearrange(
                                "o c t -> c (o t)")).then_inc(x_loaded[j], 16)

                with sp.Fori(0, B - 1) as b:
                    outputs(b, True)
                outputs(B - 1, False)
                for par in range(2):
                    sp.wait_ge(stored[par], 16 * (NCH // 2 + 1))

            @block.tensor
            def _(pe):
                pe.wait_ge(s_w, 64)
                pe.wait_ge(w_ready, 3)
                pe.wait_ge(started, 1)
                with pe.Fori(0, B) as b:
                    def at(per, k):
                        return b * per + k
                    pe.wait_ge(gn, at(GN, 9))
                    nc.tensor.matmul(pX[:, 0, 0:1], gmean[:], mv[:, 0:1], start=True, stop=True).then_inc(gn, 1)
                    pe.wait_ge(gn, at(GN, 13))
                    nc.tensor.matmul(pX[:, 1, 0:1], gmean[:], sc[:, 1:2], start=True, stop=True).then_inc(gn, 1)
                    for j in range(CPB):
                        pe.wait_ge(square_done, at(CPB, j + 1))
                        pe.wait_ge(sq_done, done(at(CPB, j - 1)))
                        nc.tensor.matmul(pX[:, j % 2, :], halves[:], tmp[:, j % 2, :], start=True,
                                         stop=True).then_inc(sq_full, 1)
                        for part in range(2):
                            m = 2 * j + part
                            pe.wait_ge((hi_done, lo_done)[part], at(CPB, j + 1))
                            pe.wait_ge((rows_hi, rows_lo)[part], done(at(CPB, j - 1)))
                            dst = pG[:, m % 4, :].bitcast(F16)
                            for t in range(TPC):
                                i = j * TPC + t
                                m_ = nc.tensor.transpose(dst[:, t * 128:(t + 1) * 128],
                                                         parts[:, part, i * 128:(i + 1) * 128], ident16[:])
                            m_.then_inc(turned, 1)
                    pe.wait_ge(rows_hi, done(at(CPB, CPB)))
                    pe.wait_ge(rows_lo, done(at(CPB, CPB)))

                    def gram(k):
                        j, i = divmod(k, NT)
                        pe.wait_ge(inc_done, done(at(CPB * NT, k - 3)))
                        hi, lo = parts[:, 0, :], parts[:, 1, :]
                        me, them = slice(i * 128, (i + 1) * 128), slice(j * T, (j + 1) * T)
                        dst = pG[:, k % 4, :]
                        if i < j * TPC:
                            pe.sem_inc(pe_gate, 1)
                            for t in range(TPC):
                                m = nc.tensor.matmul(dst[:, t * 128:(t + 1) * 128], inc[:, j * TPC + t, me],
                                                     ident16[:], start=True, stop=True)
                            m.then_inc(gram_full, 1)
                            return
                        nc.tensor.matmul(dst, hi[:, me], hi[:, them], start=True, stop=False)
                        nc.tensor.matmul(dst, hi[:, me], lo[:, them], start=False, stop=False)
                        nc.tensor.matmul(dst, lo[:, me], hi[:, them], start=False, stop=True).then_inc(gram_full, 1)

                    def edge(k):
                        j, i = divmod(k, NT)
                        if i == 0:
                            pe.wait_ge(edge_out, done(at(CPB, j - 1)))
                        pe.wait_ge(inc_done, done(at(CPB * NT, k + 1)))
                        pe.sem_inc(pe_gate, 1)
                        for part in range(2):
                            m = nc.tensor.matmul(pE[:, j % 2, :], rows[:, part, i, :],
                                                 inc[:, i, j * T:(j + 1) * T],
                                                 start=(i == 0 and part == 0), stop=(i == NT - 1 and part == 1))
                        if i == NT - 1:
                            m.then_inc(edge_full, 1)

                    def turn_edges(j):
                        pe.wait_ge(edge_out, done(at(CPB, j + 1)))
                        if j >= 2:
                            pe.wait_ge(edge_turned, at(CPB, j - 1))
                        turn(nc, pX[:, j % 2, :], sq[:, j, :], ident).then_inc(turn_full, 1)

                    for k in range(LAG):
                        gram(k)
                    for k in range(CPB * NT):
                        if k + LAG < CPB * NT:
                            gram(k + LAG)
                        edge(k)
                        if k >= NT and k % NT == TPC:
                            turn_edges(k // NT - 1)
                    turn_edges(CPB - 1)

                    def spread_inv(j):
                        pe.wait_ge(dtile, at(CPB, j + 1))
                        pe.wait_ge(inv_done, done(at(CPB, j - 3)))
                        nc.tensor.matmul(pG[:, j % 4, :], ones[:], sq[:, j, :], start=True,
                                         stop=True).then_inc(inv_full, 1)

                    def fc(j):
                        pe.wait_ge(vert_out, done(at(CPB, j + 1)))
                        pe.wait_ge(ob_ready, done(at(CPB, j - 1)))
                        nc.tensor.matmul(pX[:, j % 2, :], wfcT[:], tmp[:, j % 2, :], start=True,
                                         stop=True).then_inc(w_full, 1)

                    for j in range(CPB):
                        pe.wait_ge(vert_out, done(at(CPB, j - 1)))
                        pe.sem_inc(pe_gate, 1)
                        for i in range(NT):
                            if j == 0 and i % TPC == 0:
                                pe.wait_ge(elo, done(at(CPB, i // TPC + 1)))
                                pe.sem_inc(pe_gate, 1)
                            for part in range(2):
                                m = nc.tensor.matmul(pE[:, j % 2, :], rows[:, part, i, :],
                                                     inc[:, i, j * T:(j + 1) * T],
                                                     start=(i == 0 and part == 0),
                                                     stop=(i == NT - 1 and part == 1))
                        m.then_inc(vert_full, 1)
                        if j == 0:
                            for jj in range(CPB):
                                spread_inv(jj)
                        if j >= 1:
                            fc(j - 1)
                    fc(CPB - 1)

            @block.scalar
            def _(act):
                with act.Fori(0, B) as b:
                    def at(per, k):
                        return b * per + k
                    act.wait_ge(gn, at(GN, 15))
                    nc.scalar.activation(sc[:, 4:5], sc[:, 2:3], ACT.Ln).then_inc(gn, 1)
                    act.wait_ge(gn, at(GN, 16))
                    nc.scalar.activation(sc[:, 5:6], sc[:, 4:5], ACT.Exp, scale=-0.5).then_inc(gn, 1)
                    act.wait_ge(gn, at(GN, GN))
                    for j in range(CPB):
                        nc.scalar.copy(parts[:, 0, j * T:(j + 1) * T], xn[:, j, :]).then_inc(hi_done, 1)
                        act.wait_ge(sq_full, at(CPB, j + 1))
                        nc.scalar.copy(sq[:, j, :], pX[:, j % 2, :]).then_inc(sq_done, 1)
                        act.wait_ge(turned, at(2 * CPB, 2 * j + 1))
                        nc.scalar.copy(rows[:, 0, j * TPC:(j + 1) * TPC, :].rearrange("p a b -> p (a b)"),
                                       pG[:, (2 * j) % 4, :].bitcast(F16)[:, 0:T]).then_inc(rows_hi, 1)
                    for j in range(CPB):
                        act.wait_ge(edge_full, at(CPB, j + 1))
                        nc.scalar.copy(sq[:, j, :], pE[:, j % 2, :]).then_inc(edge_out, 1)
                        act.wait_ge(turn_full, at(CPB, j + 1))
                        nc.scalar.copy(sq[:, j, :], pX[:, j % 2, :]).then_inc(edge_turned, 1)
                    for j in range(CPB):
                        act.wait_ge(edge_scaled, at(CPB, j + 1))
                        nc.scalar.copy(rows[:, 0, j * TPC:(j + 1) * TPC, :].rearrange("p a b -> p (a b)"),
                                       sq[:, j, :]).then_inc(ehi, 1)
                    for j in range(CPB):
                        act.wait_ge(inv_full, at(CPB, j + 1))
                        nc.scalar.copy(inv_b[:, j, :], pG[:, j % 4, :]).then_inc(inv_done, 1)

            @block.vector
            def _(dve):
                nc.vector.memset(ones[:], 1.0).then_inc(w_ready, 1)
                nc.vector.memset(halves[:], 0.5).then_inc(w_ready, 1)
                nc.vector.memset(tick[:, 0:1], 0.0).then_inc(sq_done, OFF)
                nc.vector.memset(tick[:, 1:2], 0.0).then_inc(rows_hi, OFF)
                nc.vector.memset(tick[:, 2:3], 0.0).then_inc(rows_lo, OFF)
                nc.vector.memset(tick[:, 3:4], 0.0).then_inc(inc_done, OFF)
                nc.vector.memset(tick[:, 4:5], 0.0).then_inc(edge_out, OFF)
                nc.vector.memset(tick[:, 5:6], 0.0).then_inc(inv_done, OFF)
                nc.vector.memset(tick[:, 6:7], 0.0).then_inc(elo, OFF)
                nc.vector.memset(tick[:, 7:8], 0.0).then_inc(vert_out, OFF)
                nc.vector.memset(tick[:, 8:9], 0.0).then_inc(ob_ready, OFF)
                nc.vector.memset(tick[:, 9:10], 0.0).then_inc(bn_done, OFF)
                nc.vector.memset(tick[:, 10:11], 0.0).then_inc(stored[0], 16)
                nc.vector.memset(tick[:, 15:16], 0.0).then_inc(stored[1], 16)
                nc.vector.memset(tick[:, 11:12], 0.0).then_inc(started, 1)
                dve.wait_ge(s_w, 64)
                nc.vector.tensor_copy(ident16[:], ident[:]).then_inc(w_ready, 1)
                with dve.Fori(0, B) as b:
                    def at(per, k):
                        return b * per + k

                    def chain(k, op):
                        dve.wait_ge(gn, at(GN, k))
                        dve.sem_inc(dve_gate, 1)
                        op().then_inc(gn, 1)

                    for j in range(CPB):
                        dve.wait_ge(x_loaded[j], 16 * (b + 1))
                        nc.vector.bn_stats(st[:, j, :], xn[:, j, :]).then_inc(gn, 1)
                    chain(8, lambda: nc.vector.bn_aggr(mv[:], st[:].rearrange("p n s -> p (n s)")))
                    chain(10, lambda: nc.vector.tensor_tensor(sc[:, 0:1], pX[:, 0, 0:1], mv[:, 0:1], ALU.subtract))
                    chain(11, lambda: nc.vector.tensor_copy(sc[:, 3:4], pX[:, 0, 0:1]))
                    chain(12, lambda: nc.vector.scalar_tensor_tensor(
                        out=sc[:, 1:2], in0=sc[:, 0:1], scalar=sc[:, 0:1], in1=mv[:, 1:2],
                        op0=ALU.mult, op1=ALU.add))
                    chain(14, lambda: nc.vector.tensor_scalar(sc[:, 2:3], pX[:, 1, 0:1], 1e-5, None, ALU.add))
                    chain(17, lambda: nc.vector.tensor_tensor(sc[:, 6:7], sc[:, 5:6], sc[:, 5:6], ALU.mult))
                    chain(18, lambda: nc.vector.scalar_tensor_tensor(
                        out=sc[:, 6:7], in0=sc[:, 6:7], scalar=-0.5, in1=sc[:, 2:3],
                        op0=ALU.mult, op1=ALU.mult))
                    chain(19, lambda: nc.vector.scalar_tensor_tensor(
                        out=sc[:, 7:8], in0=sc[:, 6:7], scalar=1.5, in1=sc[:, 5:6],
                        op0=ALU.add, op1=ALU.mult))
                    chain(20, lambda: nc.vector.tensor_scalar(
                        xn[:].rearrange("p n t -> p (n t)"), xn[:].rearrange("p n t -> p (n t)"),
                        sc[:, 3:4], sc[:, 7:8], ALU.subtract, ALU.mult))
                    for j in range(CPB):
                        dve.wait_ge(hi_done, at(CPB, j + 1))
                        nc.vector.tensor_tensor(parts[:, 1, j * T:(j + 1) * T], xn[:, j, :],
                                                parts[:, 0, j * T:(j + 1) * T], ALU.subtract).then_inc(lo_done, 1)
                        dve.wait_ge(sq_done, done(at(CPB, j + 1)))
                        if j < 2:
                            dve.wait_ge(bn_done, done(at(CPB, 0)))
                            dve.wait_ge(stored[j], 16 * (b * (CPB // 2) + 1))
                        else:
                            dve.wait_ge(diag_step, at(2 * CPB + 1, 2 * j - 2))
                        nc.vector.tensor_tensor(ob[:, j % 2, :].rearrange("p (a b) -> p a b", b=128),
                                                sq[:, j, :].rearrange("p (a b) -> p a b", b=128),
                                                ident[:].unsqueeze(1).to_broadcast([128, TPC, 128]),
                                                ALU.mult).then_inc(diag_step, 1)
                        dve.wait_ge(diag_step, at(2 * CPB + 1, 2 * j + 1))
                        nc.vector.tensor_reduce(sd[:, 0, j * TPC:(j + 1) * TPC],
                                                ob[:, j % 2, :].rearrange("p (a b) -> p a b", b=128), AX_X,
                                                ALU.add).then_inc(diag_step, 1)
                        dve.wait_ge(turned, at(2 * CPB, 2 * j + 2))
                        nc.vector.tensor_copy(rows[:, 1, j * TPC:(j + 1) * TPC, :].rearrange("p a b -> p (a b)"),
                                              pG[:, (2 * j + 1) % 4, :].bitcast(F16)[:, 0:T]).then_inc(rows_lo, 1)
                    dve.wait_ge(diag_step, at(2 * CPB + 1, 2 * CPB))
                    nc.vector.tensor_scalar(sd[:, 1, :], sd[:, 0, :], -128.0, None, ALU.add).then_inc(diag_step, 1)
                    dve.wait_ge(diag_step, at(2 * CPB + 1, 2 * CPB + 1))
                    for k in range(CPB * NT):
                        j, i = divmod(k, NT)
                        dve.wait_ge(gram_full, at(CPB * NT, k + 1))
                        dve.sem_inc(dve_gate, 1)
                        if i < j * TPC:
                            nc.vector.tensor_scalar(inc[:, i, j * T:(j + 1) * T], pG[:, k % 4, :], 1.0, 0.0,
                                                    ALU.mult, ALU.add,
                                                    accum_out=dg[:, i, j:j + 1],
                                                    saturate=False).then_inc(inc_done, 1)
                            continue
                        nc.vector.scalar_tensor_tensor(
                            out=inc[:, i, j * T:(j + 1) * T], in0=pG[:, k % 4, :], scalar=sd[:, 1, i:i + 1],
                            in1=sq[:, j, :], op0=ALU.subtract, op1=ALU.is_gt,
                            accum_out=dg[:, i, j:j + 1], saturate=False).then_inc(inc_done, 1)
                    dve.wait_ge(inc_done, done(at(CPB * NT, CPB * NT)))
                    nc.vector.tensor_reduce(inv[:, 0, :], dg[:], AX_X, ALU.add).then_inc(deg_step, 1)
                    dve.wait_ge(deg_step, at(3, 1))
                    nc.vector.tensor_scalar(inv[:, 1, :], inv[:, 0, :], 1.0, None, ALU.max).then_inc(deg_step, 1)
                    dve.wait_ge(deg_step, at(3, 2))
                    nc.vector.reciprocal(inv[:, 2, :], inv[:, 1, :]).then_inc(deg_step, 1)
                    dve.wait_ge(deg_step, at(3, 3))

                    def scale(j):
                        dve.wait_ge(edge_turned, at(CPB, j + 1))
                        nc.vector.tensor_tensor(sq[:, j, :].rearrange("p (a b) -> p a b", b=128),
                                                sq[:, j, :].rearrange("p (a b) -> p a b", b=128),
                                                inv[:, 2, j * TPC:(j + 1) * TPC].unsqueeze(2).to_broadcast(
                                                    [128, TPC, 128]), ALU.mult).then_inc(edge_scaled, 1)

                    scale(0)
                    dve.wait_ge(edge_full, at(CPB, CPB))
                    for j in range(CPB):
                        if j + 1 < CPB:
                            scale(j + 1)
                        dve.wait_ge(ehi, at(CPB, j + 1))
                        nc.vector.tensor_tensor(rows[:, 1, j * TPC:(j + 1) * TPC, :].rearrange("p a b -> p (a b)"),
                                                sq[:, j, :],
                                                rows[:, 0, j * TPC:(j + 1) * TPC, :].rearrange("p a b -> p (a b)"),
                                                ALU.subtract).then_inc(elo, 1)
                    for j in range(CPB):
                        dve.wait_ge(elo, done(at(CPB, j + 1)))
                        for t in range(TPC):
                            i = j * TPC + t
                            d = nc.vector.tensor_scalar(sq[:, j, t * 128:(t + 1) * 128], ident[:],
                                                        inv[:, 2, i:i + 1], None, ALU.mult)
                        d.then_inc(dtile, 1)
                    for j in range(CPB):
                        dve.wait_ge(vert_full, at(CPB, j + 1))
                        dve.wait_ge(inv_done, done(at(CPB, j + 1)))
                        if j >= 2:
                            dve.wait_ge(w_full, at(CPB, j - 1))
                        nc.vector.tensor_tensor(tmp[:, j % 2, :], pE[:, j % 2, :], inv_b[:, j, :],
                                                ALU.mult).then_inc(vert_out, 1)
                        dve.wait_ge(w_full, at(CPB, j + 1))
                        dve.wait_ge(stored[j % 2], 16 * (b * (CPB // 2) + j // 2 + 1))
                        nc.vector.scalar_tensor_tensor(out=ob[:, j % 2, :], in0=pX[:, j % 2, :],
                                                       scalar=bfc[:, 0:1], in1=xn[:, j, :],
                                                       op0=ALU.add, op1=ALU.add).then_inc(ob_ready, 1)
                        dve.wait_ge(ob_ready, done(at(CPB, j + 1)))
                        nc.vector.bn_stats(bn_stats[:, bass.ds(b * CPB + j, 1), :].rearrange("p o s -> p (o s)"),
                                           ob[:, j % 2, :]).then_inc(bn_done, 1)

            @block.gpsimd
            def _(pool):
                with pool.Fori(0, B) as b:
                    for j in range(CPB):
                        pool.wait_ge(gn, b * GN + GN)
                        if j >= 2:
                            pool.wait_ge(sq_full, b * CPB + j - 1)
                        nc.gpsimd.tensor_tensor(tmp[:, j % 2, :], xn[:, j, :], xn[:, j, :],
                                                ALU.mult).then_inc(square_done, 1)


class Banks:

    def __init__(self, nc, ctx, sem, prefix, names, n_banks):
        self.index = {name: k for k, name in enumerate(names)}
        assert len(names) % n_banks == 0
        self.per, self.n = len(names), n_banks
        self.psum = ctx.enter_context(nc.psum_tensor(prefix + "banks", [128, n_banks, T], F32))
        self.filled = sem(prefix + "filled")
        self.free = [sem(f"{prefix}free{k}") for k in range(n_banks)]

    def tile(self, use):
        return self.psum[:, self.index[use] % self.n, :]

    def count(self, use):
        return self.index[use] // self.n

    def wait_free(self, eng, it, use):
        k = self.index[use]
        eng.wait_ge(self.free[k % self.n], done(it * (self.per // self.n) + k // self.n))

    def wait_filled(self, eng, it, use):
        eng.wait_ge(self.filled, it * self.per + self.index[use] + 1)

    def wait_read(self, eng, it, use):
        k = self.index[use]
        eng.wait_ge(self.free[k % self.n], done(it * (self.per // self.n) + k // self.n + 1))

    def wait_to_fill(self, eng, it, use, inputs):
        for i in inputs:
            if (self.index[use] - self.index[i]) % self.n:
                self.wait_read(eng, it, i)
        self.wait_free(eng, it, use)

    def release(self, use):
        return self.free[self.index[use] % self.n]


class Norm:

    def __init__(self, nc, ctx, sem, prefix):
        def sb(name, shape):
            return ctx.enter_context(nc.sbuf_tensor(prefix + name, shape, F32))
        self.stats = sb("stats", [128, B, TPC, 6])
        self.mv = sb("mv", [128, B, TPC, 2])
        self.v = sb("v", [128, 4, B * TPC])
        self.rstd = sb("rstd", [128, B * TPC])
        self.step, self.gate = sem(prefix + "step"), sem(prefix + "gate")

    STEPS = 2 * B + 6

    def vector(self, nc, dve, banks, it, name, out):
        base = it * self.STEPS
        for b in range(B):
            banks.wait_filled(dve, it, (name, b))
            for t in range(TPC):
                i = nc.vector.bn_stats(self.stats[:, b, t, :], banks.tile((name, b))[:, t * 128:(t + 1) * 128])
            i.then_inc(self.step, 1)
        for b in range(B):
            dve.wait_ge(self.step, base + b + 1)
            dve.sem_inc(self.gate, 1)
            for t in range(TPC):
                i = nc.vector.bn_aggr(self.mv[:, b, t, :], self.stats[:, b, t, :])
            i.then_inc(self.step, 1)
        dve.wait_ge(self.step, base + 2 * B)
        nc.vector.tensor_scalar(self.v[:, 0, :], self.mv[:].rearrange("p b t s -> p (b t) s")[:, :, 1],
                                1e-5, None, ALU.add).then_inc(self.step, 1)
        dve.wait_ge(self.step, base + 2 * B + 2)
        nc.vector.reciprocal(self.v[:, 2, :], self.v[:, 1, :]).then_inc(self.step, 1)
        dve.wait_ge(self.step, base + 2 * B + 3)
        nc.vector.tensor_tensor(self.v[:, 3, :], self.v[:, 2, :], self.v[:, 2, :], ALU.mult).then_inc(self.step, 1)
        dve.wait_ge(self.step, base + 2 * B + 4)
        nc.vector.scalar_tensor_tensor(out=self.v[:, 3, :], in0=self.v[:, 3, :], scalar=-0.5,
                                       in1=self.v[:, 0, :], op0=ALU.mult, op1=ALU.mult).then_inc(self.step, 1)
        dve.wait_ge(self.step, base + 2 * B + 5)
        nc.vector.scalar_tensor_tensor(out=self.rstd[:], in0=self.v[:, 3, :], scalar=1.5,
                                       in1=self.v[:, 2, :], op0=ALU.add, op1=ALU.mult).then_inc(self.step, 1)
        dve.wait_ge(self.step, base + 2 * B + 6)
        for b in range(B):
            for t in range(TPC):
                k = b * TPC + t
                i = nc.vector.tensor_scalar(out(b, t), banks.tile((name, b))[:, t * 128:(t + 1) * 128],
                                            self.mv[:, b, t, 0:1], self.rstd[:, k:k + 1],
                                            ALU.subtract, ALU.mult)
            i.then_inc(banks.release((name, b)), 1)

    def scalar(self, nc, act, it):
        base = it * self.STEPS + 2 * B
        act.wait_ge(self.step, base + 1)
        nc.scalar.activation(self.v[:, 1, :], self.v[:, 0, :], ACT.Sqrt).then_inc(self.step, 1)


def turn(nc, dst, src, ident):
    for t in range(TPC):
        i = nc.tensor.transpose(dst[:, t * 128:(t + 1) * 128], src[:, t * 128:(t + 1) * 128], ident[:])
    return i


BACK_AND_GATE = [("back2", 0)] + [u for b in range(1, B) for u in (("back2", b), ("gate", b - 1))] + [("gate", B - 1)]


def linear_attention(nc, a, bn_stats, x_in, pre_in, x_out, xt_out, logits):
    names = ([("turn1", b) for b in range(B)] + [("back1", b) for b in range(B)]
             + [(w, b) for b in range(B) for w in ("q", "k")]
             + [("v", b) for b in range(B)] + [("kturn", b) for b in range(B)]
             + [("score", b) for b in range(B)]
             + [("kv", h, b) for h in range(2) for b in range(B)]
             + [("out", h, b) for h in range(2) for b in range(B)]
             + [("oturn", b) for b in range(B)] + [("turn2", b) for b in range(B)] + BACK_AND_GATE)
    with ExitStack() as ctx:
        def sb(name, shape, dt=F32):
            return ctx.enter_context(nc.sbuf_tensor("l_" + name, shape, dt))

        sem = Semaphores(nc, "l_")
        ctx.callback(sem.clear)

        banks = Banks(nc, ctx, sem, "l_", names, 6)
        norm1, norm2 = Norm(nc, ctx, sem, "l_n1"), Norm(nc, ctx, sem, "l_n2")
        xin, pin = sb("xin", [128, B, T]), sb("pin", [128, B, T])
        x2, x3 = sb("x2", [128, B, T]), sb("x3", [128, B, T])
        tok1, ch1 = sb("tok1", [128, B, T]), sb("ch1", [128, B, T])
        tok2, ch2 = sb("tok2", [128, B, T]), sb("ch2", [128, B, T])
        qk = sb("qk", [128, B, 2, T])
        relu = sb("relu", [128, B, 2, T])
        V = sb("V", [128, B, TPC, 129])
        kT = sb("kT", [128, B, T])
        sm = sb("sm", [128, B, T])
        o = sb("o", [128, B, T])
        S = sb("S", [128, B, TPC + 1, 129])
        rd = sb("rd", [128, 2, B, TPC])
        ident, mask = sb("ident", [128, 128]), sb("mask", [128, 128])
        wT = sb("wT", [128, 3 * C])
        bqk = sb("bqk", [128, 2])
        bv = sb("bv", [128, C])
        gwT = sb("gwT", [128, 64])
        gb = sb("gb", [128, 1])
        gamma_beta = sb("gamma_beta", [128, 2])
        mv = sb("bmv", [128, 2])
        bc = sb("bc", [128, 8])
        tick = sb("tick", [128, 32])

        s_w = sem("weights"); started = sem("started"); bn = sem("bn_step"); gate = sem("gate")
        loaded = [sem(f"loaded{b}") for b in range(B)]
        silu_done = sem("silu_done"); x2_ready = sem("x2_ready")
        exp_done = sem("exp_done"); qk_ready = sem("qk_ready"); S_step = sem("S_step")
        den_step = sem("den_step"); x_stored = [sem(f"x_stored{b}") for b in range(B)]
        t_stored = [sem(f"t_stored{b}") for b in range(B)]

        with nc.Block() as block:

            @block.sync
            def _(sp):
                for dst, name in ((ident, "ident"), (mask, "mask"), (wT, "attn2_wT"), (bqk, "attn2_bqk"),
                                  (gwT, "ffn2_gwT"), (gb, "ffn2_gb"), (gamma_beta, "gamma_beta")):
                    sp.dma_start(dst[:], a[name]).then_inc(s_w, 16)
                sp.dma_start(bv[:], a["attn2_bv"].partition_broadcast(128)).then_inc(s_w, 16)
                with sp.Fori(0, CPB) as c:
                    for b in range(B):
                        sp.wait_ge(x2_ready, done(c * B + b + 1 - B))
                        sp.dma_start(xin[:, b, :], x_in[b, :, bass.ds(c * T, T)]).then_inc(loaded[b], 16)
                        sp.dma_start(pin[:, b, :], pre_in[b, :, bass.ds(c * T, T)]).then_inc(loaded[b], 16)
                for b in range(B):
                    sp.wait_ge(loaded[b], 32 * CPB)

            @block.gpsimd
            def _(pool):
                pool.wait_ge(started, 1)
                with pool.Fori(0, CPB) as c:
                    for b in range(B):
                        pool.wait_ge(silu_done, c * B + b + 1)
                        pool.wait_ge(loaded[b], 32 * (c + 1))
                        banks.wait_read(pool, c - 1, ("oturn", b))
                        nc.gpsimd.tensor_tensor(x2[:, b, :], xin[:, b, :], pin[:, b, :],
                                                ALU.add).then_inc(x2_ready, 1)

            @block.tensor
            def _(pe):
                pe.wait_ge(started, 1)
                pe.wait_ge(s_w, 16 * 8)
                with pe.Fori(0, CPB) as c:
                    def fill(use, body, *inputs):
                        banks.wait_to_fill(pe, c, use, inputs)
                        body(banks.tile(use)).then_inc(banks.filled, 1)

                    for b in range(B):
                        pe.wait_ge(x2_ready, done(c * B + b + 1))
                        fill(("turn1", b), lambda p: turn(nc, p, x2[:, b, :], ident))
                    for b in range(B):
                        fill(("back1", b), lambda p: turn(nc, p, tok1[:, b, :], ident), ("turn1", b))
                    for b in range(B):
                        for w in range(2):
                            fill(("qk"[w], b), lambda p: nc.tensor.matmul(
                                p, wT[:, w * C:(w + 1) * C], ch1[:, b, :], start=True, stop=True), ("back1", b))
                    for b in range(B):
                        def values(p):
                            for t in range(TPC):
                                i = nc.tensor.matmul(p[:, t * 128:(t + 1) * 128], ch1[:, b, t * 128:(t + 1) * 128],
                                                     wT[:, 2 * C:], start=True, stop=True)
                            return i
                        fill(("v", b), values)
                    for b in range(B):
                        pe.wait_ge(qk_ready, c * 2 * B + 2 * b + 2)
                        fill(("kturn", b), lambda p: turn(nc, p, qk[:, b, 1, :], ident))
                    for b in range(B):
                        def scores(p):
                            for t in range(TPC):
                                s_ = slice(t * 128, (t + 1) * 128)
                                i = nc.tensor.matmul(p[:, s_], qk[:, b, 1, s_], qk[:, b, 0, s_],
                                                     start=True, stop=True)
                            return i
                        fill(("score", b), scores)
                    for h in range(2):
                        for b in range(B):
                            def state(p):
                                for t in range(2):
                                    tt = 2 * h + t
                                    i = nc.tensor.matmul(p[:, t * 129:(t + 1) * 129],
                                                         kT[:, b, tt * 128:(tt + 1) * 128],
                                                         V[:, b, tt, :], start=True, stop=True)
                                return i
                            fill(("kv", h, b), state, ("kturn", b), ("v", b))
                    for h in range(2):
                        for b in range(B):
                            def outs(p):
                                for t in range(2):
                                    tt = 2 * h + t
                                    s_ = slice(tt * 128, (tt + 1) * 128)
                                    nc.tensor.matmul(p[:, t * 129:(t + 1) * 129], sm[:, b, s_], V[:, b, tt, :],
                                                     start=True, stop=False)
                                    i = nc.tensor.matmul(p[:, t * 129:(t + 1) * 129], qk[:, b, 0, s_],
                                                         S[:, b, tt, :], start=False, stop=True)
                                return i
                            fill(("out", h, b), outs, ("score", b), ("kv", h, b))
                    for b in range(B):
                        fill(("oturn", b), lambda p: turn(nc, p, o[:, b, :], ident), ("out", 1, b))
                    for b in range(B):
                        fill(("turn2", b), lambda p: turn(nc, p, x3[:, b, :], ident), ("oturn", b))
                    for what, b in BACK_AND_GATE:
                        if what == "back2":
                            fill(("back2", b), lambda p: turn(nc, p, tok2[:, b, :], ident), ("turn2", b))
                        else:
                            r = 64 * (b % 2)
                            fill(("gate", b), lambda p: nc.tensor.matmul(p[r:r + 64, :], gwT[:], ch2[:, b, :],
                                                                         start=True, stop=True), ("back2", b))

            @block.scalar
            def _(act):
                act.wait_ge(bn, 3)
                nc.scalar.activation(bc[:, 1:2], bc[:, 0:1], ACT.Ln).then_inc(bn, 1)
                act.wait_ge(bn, 4)
                nc.scalar.activation(bc[:, 2:3], bc[:, 1:2], ACT.Exp, scale=-0.5).then_inc(bn, 1)
                act.wait_ge(bn, 10)

                def silu(c):
                    for b in range(B):
                        act.wait_ge(loaded[b], 32 * (c + 1))
                        nc.scalar.activation(pin[:, b, :], pin[:, b, :], ACT.Silu, bias=bc[:, 6:7],
                                             scale=bc[:, 4:5]).then_inc(silu_done, 1)

                def chunk(c, more):
                    norm1.scalar(nc, act, c)
                    for b in range(B):
                        banks.wait_filled(act, c, ("back1", b))
                        nc.scalar.copy(ch1[:, b, :], banks.tile(("back1", b))).then_inc(banks.release(("back1", b)), 1)
                    for b in range(B):
                        for w in range(2):
                            use = ("qk"[w], b)
                            banks.wait_filled(act, c, use)
                            nc.scalar.activation(qk[:, b, w, :], banks.tile(use), ACT.Exp,
                                                 bias=bqk[:, w:w + 1]).then_inc(exp_done, 1)
                            nc.scalar.activation(relu[:, b, w, :], banks.tile(use), ACT.Relu,
                                                 bias=bqk[:, w:w + 1]).then_inc(banks.release(use), 1)
                    for b in range(B):
                        banks.wait_filled(act, c, ("kturn", b))
                        nc.scalar.copy(kT[:, b, :], banks.tile(("kturn", b))).then_inc(banks.release(("kturn", b)), 1)
                    if more:
                        silu(c + 1)
                    for h in range(2):
                        for b in range(B):
                            act.wait_ge(den_step, (c * 2 + h) * 2 * B + B + b + 1)
                            for t in range(2):
                                tt = 2 * h + t
                                i = nc.scalar.activation(o[:, b, tt * 128:(tt + 1) * 128],
                                                         banks.tile(("out", h, b))[:, t * 129:t * 129 + 128],
                                                         ACT.Copy, scale=rd[:, 1, b, tt:tt + 1])
                            i.then_inc(banks.release(("out", h, b)), 1)
                    for b in range(B):
                        banks.wait_read(act, c, ("oturn", b))
                        act.dma_start(x_out[b, :, bass.ds(c * T, T)], x3[:, b, :]).then_inc(x_stored[b], 16)
                    norm2.scalar(nc, act, c)
                    for what, b in BACK_AND_GATE:
                        banks.wait_filled(act, c, (what, b))
                        if what == "back2":
                            nc.scalar.copy(ch2[:, b, :], banks.tile((what, b))).then_inc(banks.release((what, b)), 1)
                        else:
                            r = 64 * (b % 2)
                            nc.scalar.activation(logits[r:r + 64, b // 2, bass.ds(c * T, T)],
                                                 banks.tile((what, b))[r:r + 64, :], ACT.Identity,
                                                 bias=gb[r:r + 64, :]).then_inc(banks.release((what, b)), 1)
                    for b in range(B):
                        banks.wait_read(act, c, ("turn2", b))
                        act.dma_start(xt_out[b, bass.ds(c * T, T), :].rearrange("(t p) d -> p t d", p=128),
                                       tok2[:, b, :].rearrange("p (t d) -> p t d", d=C)).then_inc(t_stored[b], 16)

                silu(0)
                with act.Fori(0, CPB - 1) as c:
                    chunk(c, True)
                chunk(CPB - 1, False)
                for b in range(B):
                    act.wait_ge(x_stored[b], 16 * (CPB + 1))
                    act.wait_ge(t_stored[b], 16 * (CPB + 1))

            @block.vector
            def _(dve):
                k = 0
                for s in [x2_ready, S_step] + banks.free:
                    nc.vector.memset(tick[:, k:k + 1], 0.0).then_inc(s, OFF)
                    k += 1
                for s in x_stored + t_stored:
                    nc.vector.memset(tick[:, k:k + 1], 0.0).then_inc(s, 16)
                    k += 1
                nc.vector.memset(V[:, :, :, 128:129], 1.0).then_inc(S_step, 1)
                nc.vector.memset(S[:, :, TPC, :], 0.0).then_inc(S_step, 1)
                nc.vector.memset(tick[:, k:k + 1], 0.0).then_inc(started, 1)
                dve.wait_ge(s_w, 16 * 8)
                nc.vector.bn_aggr(mv[:], bn_stats[:].rearrange("p n s -> p (n s)")).then_inc(bn, 1)
                dve.wait_ge(bn, 1)
                nc.vector.tensor_scalar(bc[:, 0:1], mv[:, 1:2], 1e-5, None, ALU.add).then_inc(bn, 1)
                dve.wait_ge(bn, 2)
                nc.vector.tensor_scalar(bc[:, 7:8], mv[:, 0:1], -1.0, None, ALU.mult).then_inc(bn, 1)
                dve.wait_ge(bn, 5)
                nc.vector.tensor_tensor(bc[:, 3:4], bc[:, 2:3], bc[:, 2:3], ALU.mult).then_inc(bn, 1)
                dve.wait_ge(bn, 6)
                nc.vector.scalar_tensor_tensor(out=bc[:, 3:4], in0=bc[:, 3:4], scalar=-0.5, in1=bc[:, 0:1],
                                               op0=ALU.mult, op1=ALU.mult).then_inc(bn, 1)
                dve.wait_ge(bn, 7)
                nc.vector.scalar_tensor_tensor(out=bc[:, 5:6], in0=bc[:, 3:4], scalar=1.5, in1=bc[:, 2:3],
                                               op0=ALU.add, op1=ALU.mult).then_inc(bn, 1)
                dve.wait_ge(bn, 8)
                nc.vector.tensor_tensor(bc[:, 4:5], bc[:, 5:6], gamma_beta[:, 0:1], ALU.mult).then_inc(bn, 1)
                dve.wait_ge(bn, 9)
                nc.vector.scalar_tensor_tensor(out=bc[:, 6:7], in0=bc[:, 4:5], scalar=bc[:, 7:8],
                                               in1=gamma_beta[:, 1:2], op0=ALU.mult, op1=ALU.add).then_inc(bn, 1)
                with dve.Fori(0, CPB) as c:
                    SP_ = (TPC + 1) * B
                    for b in range(B):
                        dve.wait_ge(S_step, done(2 + c * SP_))
                        banks.wait_read(dve, c - 1, ("out", 1, b))
                        nc.vector.tensor_copy(S[:, b, 0, :], S[:, b, TPC, :]).then_inc(S_step, 1)
                    norm1.vector(nc, dve, banks, c, "turn1", lambda b, t: tok1[:, b, t * 128:(t + 1) * 128])
                    for b in range(B):
                        for w in range(2):
                            dve.wait_ge(exp_done, c * 2 * B + 2 * b + w + 1)
                            banks.wait_read(dve, c, ("qk"[w], b))
                            nc.vector.scalar_tensor_tensor(out=qk[:, b, w, :], in0=qk[:, b, w, :], scalar=1.0,
                                                           in1=relu[:, b, w, :], op0=ALU.min,
                                                           op1=ALU.add).then_inc(qk_ready, 1)
                    for b in range(B):
                        banks.wait_filled(dve, c, ("v", b))
                        nc.vector.tensor_tensor(V[:, b, :, 0:128],
                                                banks.tile(("v", b)).rearrange("p (t d) -> p t d", d=128),
                                                bv[:].unsqueeze(1).to_broadcast([128, TPC, 128]),
                                                ALU.add).then_inc(banks.release(("v", b)), 1)
                    for b in range(B):
                        banks.wait_filled(dve, c, ("score", b))
                        nc.vector.tensor_tensor(sm[:, b, :].rearrange("p (t d) -> p t d", d=128),
                                                banks.tile(("score", b)).rearrange("p (t d) -> p t d", d=128),
                                                mask[:].unsqueeze(1).to_broadcast([128, TPC, 128]),
                                                ALU.mult).then_inc(banks.release(("score", b)), 1)
                    for h in range(2):
                        for t in range(2):
                            tt = 2 * h + t
                            for b in range(B):
                                banks.wait_filled(dve, c, ("kv", h, b))
                                dve.wait_ge(S_step, done(2 + c * SP_ + tt * B + b + 1))
                                i = nc.vector.tensor_tensor(S[:, b, tt + 1, :],
                                                            banks.tile(("kv", h, b))[:, t * 129:(t + 1) * 129],
                                                            S[:, b, tt, :], ALU.add)
                                i.then_inc(S_step, 1)
                        for b in range(B):
                            dve.wait_ge(S_step, done(2 + c * SP_ + (2 * h + 2) * B + b + 1))
                            nc.vector.memset(tick[:, 20 + 4 * h + b:21 + 4 * h + b], 0.0).then_inc(
                                banks.release(("kv", h, b)), 1)
                    for h in range(2):
                        base = (c * 2 + h) * 2 * B
                        for b in range(B):
                            banks.wait_filled(dve, c, ("out", h, b))
                            nc.vector.tensor_scalar(
                                rd[:, 0, b, 2 * h:2 * h + 2], banks.tile(("out", h, b))[:, 0:258].rearrange(
                                    "p (t d) -> p t d", d=129)[:, :, 128], 1e-6, None, ALU.add).then_inc(den_step, 1)
                        for b in range(B):
                            dve.wait_ge(den_step, base + b + 1)
                            nc.vector.reciprocal(rd[:, 1, b, 2 * h:2 * h + 2], rd[:, 0, b, 2 * h:2 * h + 2]).then_inc(den_step, 1)
                    for b in range(B):
                        banks.wait_filled(dve, c, ("oturn", b))
                        dve.wait_ge(x_stored[b], 16 * (c + 1))
                        nc.vector.tensor_tensor(x3[:, b, :], banks.tile(("oturn", b)), x2[:, b, :],
                                                ALU.add).then_inc(banks.release(("oturn", b)), 1)
                    for b in range(B):
                        dve.wait_ge(t_stored[b], 16 * (c + 1))
                    norm2.vector(nc, dve, banks, c, "turn2", lambda b, t: tok2[:, b, t * 128:(t + 1) * 128])


def window_states(nc, a, x_in, q_out, states):
    names = ([("turn1", b) for b in range(B)] + [("back1", b) for b in range(B)]
             + [(w, b) for w in ("q", "k", "v") for b in range(B)]
             + [("kv", h, b) for h in range(2) for b in range(B)])
    with ExitStack() as ctx:
        def sb(name, shape, dt=F32):
            return ctx.enter_context(nc.sbuf_tensor("w_" + name, shape, dt))

        sem = Semaphores(nc, "w_")
        ctx.callback(sem.clear)

        banks = Banks(nc, ctx, sem, "w_", names, 7)
        norm = Norm(nc, ctx, sem, "w_n")
        xin = sb("xin", [128, B, T])
        tok1, ch1 = sb("tok1", [128, B, T]), sb("ch1", [128, B, T])
        q = sb("q", [128, B, T])
        k, kz, v = sb("k", [128, B, T]), sb("kz", [128, B, T]), sb("v", [128, B, T])
        half = sb("half", [128, B, 2, 128])
        ident = sb("ident", [128, 128])
        wT = sb("wT", [128, 3 * C])
        bq = sb("bq", [128, 2])
        bkv = sb("bkv", [128, 2, C])
        ends = sb("ends", [128, 2])
        tick = sb("tick", [128, 16])
        s_w = sem("weights"); started = sem("started"); prep = sem("prep")
        loaded = [sem(f"loaded{b}") for b in range(B)]
        pool_gate = sem("pool_gate"); half_ready = sem("half_ready"); q_ready = sem("q_ready"); kz_ready = sem("kz_ready")
        stored = [sem(f"stored{b}") for b in range(B)]

        with nc.Block() as block:

            @block.sync
            def _(sp):
                for dst, name in ((ident, "ident"), (wT, "attn3_wT"), (ends, "ends")):
                    sp.dma_start(dst[:], a[name]).then_inc(s_w, 16)
                sp.dma_start(bq[:, 0:1], a["attn3_bq"]).then_inc(s_w, 16)
                sp.dma_start(bkv[:], a["attn3_bkv"].partition_broadcast(128)).then_inc(s_w, 16)
                with sp.Fori(0, CPB) as c:
                    for b in range(B):
                        banks.wait_read(sp, c - 1, ("turn1", b))
                        sp.dma_start(xin[:, b, :], x_in[b, :, bass.ds(c * T, T)]).then_inc(loaded[b], 16)
                    for b in range(B):
                        sp.wait_ge(q_ready, c * B + b + 1)
                        sp.dma_start(q_out[b, :, bass.ds(c * T, T)], q[:, b, :]).then_inc(stored[b], 16)
                for b in range(B):
                    sp.wait_ge(stored[b], 16 * (CPB + 1))

            @block.gpsimd
            def _(pool):
                with pool.Fori(0, CPB) as c:
                    for b in range(B):
                        banks.wait_read(pool, c, ("k", b))
                        banks.wait_read(pool, c - 1, ("kv", 1, b))
                        pool.sem_inc(pool_gate, 1)
                        for e in range(2):
                            i = nc.gpsimd.tensor_scalar(
                                kz[:, b, :].rearrange("p (h e d) -> p h e d", e=2, d=128)[:, :, e, :],
                                k[:, b, :].rearrange("p (h e d) -> p h e d", e=2, d=128)[:, :, e, :],
                                ends[:, e:e + 1], None, ALU.mult)
                        i.then_inc(kz_ready, 1)

            @block.tensor
            def _(pe):
                pe.wait_ge(started, 1)
                pe.wait_ge(s_w, 16 * 5)
                with pe.Fori(0, CPB) as c:
                    def fill(use, body, *inputs):
                        banks.wait_to_fill(pe, c, use, inputs)
                        body(banks.tile(use)).then_inc(banks.filled, 1)

                    for b in range(B):
                        pe.wait_ge(loaded[b], 16 * (c + 1))
                        fill(("turn1", b), lambda p: turn(nc, p, xin[:, b, :], ident))
                    for b in range(B):
                        fill(("back1", b), lambda p: turn(nc, p, tok1[:, b, :], ident), ("turn1", b))
                    for b in range(B):
                        fill(("q", b), lambda p: nc.tensor.matmul(p, wT[:, 0:C], ch1[:, b, :], start=True,
                                                                  stop=True), ("back1", b))
                    for w in range(1, 3):
                        for b in range(B):
                            def by_token(p):
                                for t in range(TPC):
                                    s_ = slice(t * 128, (t + 1) * 128)
                                    i = nc.tensor.matmul(p[:, s_], ch1[:, b, s_], wT[:, w * C:(w + 1) * C],
                                                         start=True, stop=True)
                                return i
                            fill(("qkv"[w], b), by_token)
                    for h in range(2):
                        for b in range(B):
                            if h == 0:
                                pe.wait_ge(kz_ready, c * B + b + 1)
                            def state(p):
                                for n, (keys, t) in enumerate(((kz, 2 * h), (k, 2 * h), (k, 2 * h + 1), (kz, 2 * h + 1))):
                                    s_ = slice(t * 128, (t + 1) * 128)
                                    i = nc.tensor.matmul(p[:, n * 128:(n + 1) * 128], keys[:, b, s_], v[:, b, s_],
                                                         start=True, stop=True)
                                return i
                            fill(("kv", h, b), state, ("v", b))

            @block.scalar
            def _(act):
                act.wait_ge(prep, 1)
                with act.Fori(0, CPB) as c:
                    norm.scalar(nc, act, c)
                    for b in range(B):
                        banks.wait_filled(act, c, ("back1", b))
                        nc.scalar.copy(ch1[:, b, :], banks.tile(("back1", b))).then_inc(banks.release(("back1", b)), 1)
                    for b in range(B):
                        banks.wait_filled(act, c, ("q", b))
                        act.wait_ge(stored[b], 16 * (c + 1))
                        nc.scalar.activation(q[:, b, :], banks.tile(("q", b)), ACT.Identity, bias=bq[:, 1:2],
                                             scale=float(C) ** -0.5).then_inc(q_ready, 1)
                        act.wait_ge(q_ready, c * B + b + 1)
                        nc.scalar.copy(tick[:, 15:16], ident[:, 0:1]).then_inc(banks.release(("q", b)), 1)
                    for h in range(2):
                        for b in range(B):
                            banks.wait_filled(act, c, ("kv", h, b))
                            if h == 1:
                                banks.wait_read(act, c, ("kv", 0, b))
                            nc.scalar.copy(half[:, b, :, :].rearrange("p v d -> p (v d)"),
                                           banks.tile(("kv", h, b))[:, 0:256]).then_inc(half_ready, 1)

            @block.vector
            def _(dve):
                n = 0
                for s in banks.free:
                    nc.vector.memset(tick[:, n:n + 1], 0.0).then_inc(s, OFF)
                    n += 1
                for s in stored:
                    nc.vector.memset(tick[:, n:n + 1], 0.0).then_inc(s, 16)
                    n += 1
                nc.vector.memset(states[:, :, :, 0, :], 0.0).then_inc(started, 1)
                nc.vector.memset(states[:, :, :, 2 * CPB + 1, :], 0.0)
                dve.wait_ge(s_w, 16 * 5)
                nc.vector.tensor_scalar(bq[:, 1:2], bq[:, 0:1], float(C) ** -0.5, None, ALU.mult).then_inc(prep, 1)
                with dve.Fori(0, CPB) as c:
                    norm.vector(nc, dve, banks, c, "turn1", lambda b, t: tok1[:, b, t * 128:(t + 1) * 128])
                    for w, dst in ((0, k), (1, v)):
                        for b in range(B):
                            use = ("kv"[w], b)
                            banks.wait_filled(dve, c, use)
                            nc.vector.tensor_tensor(dst[:, b, :].rearrange("p (t d) -> p t d", d=128),
                                                    banks.tile(use).rearrange("p (t d) -> p t d", d=128),
                                                    bkv[:, w, :].unsqueeze(1).to_broadcast([128, TPC, 128]),
                                                    ALU.add).then_inc(banks.release(use), 1)
                    for h in range(2):
                        for b in range(B):
                            use = ("kv", h, b)
                            banks.wait_filled(dve, c, use)
                            dve.wait_ge(half_ready, c * 2 * B + h * B + b + 1)
                            kv = banks.tile(use)[:, 256:512].rearrange("p (v d) -> p v d", d=128)
                            to = states[:, b, :, bass.ds(c * 2 + h + 1, 1), :].rearrange("p v o d -> p v (o d)")
                            nc.vector.tensor_tensor(to[:, 1:3, :], half[:, b, :, :], kv, ALU.add)
                            nc.vector.tensor_tensor(to[:, 0, :], half[:, b, 1, :], kv[:, 0, :],
                                                    ALU.add).then_inc(banks.release(use), 1)


def window_attention(nc, a, x_in, q_in, states, x_out, xt_out, logits):
    names = [("att", b) for b in range(B)] + [("turn2", b) for b in range(B)] + BACK_AND_GATE
    with ExitStack() as ctx:
        def sb(name, shape, dt=F32):
            return ctx.enter_context(nc.sbuf_tensor("a_" + name, shape, dt))

        sem = Semaphores(nc, "a_")
        ctx.callback(sem.clear)

        banks = Banks(nc, ctx, sem, "a_", names, 8)
        norm = Norm(nc, ctx, sem, "a_n")
        xin, qin = sb("xin", [128, B, T]), sb("qin", [128, B, T])
        x5 = sb("x5", [128, B, T])
        tok2, ch2 = sb("tok2", [128, B, T]), sb("ch2", [128, B, T])
        W = sb("W", [128, B, 2, 2, 128])
        ident = sb("ident", [128, 128])
        gwT = sb("gwT", [128, 64])
        gb = sb("gb", [128, 1])
        tick = sb("tick", [128, 16])
        s_w = sem("weights"); started = sem("started"); W_step = sem("W_step")
        loaded = [sem(f"loaded{b}") for b in range(B)]
        x_stored = [sem(f"x_stored{b}") for b in range(B)]
        t_stored = [sem(f"t_stored{b}") for b in range(B)]

        with nc.Block() as block:

            @block.sync
            def _(sp):
                for dst, name in ((ident, "ident"), (gwT, "ffn3_gwT"), (gb, "ffn3_gb")):
                    sp.dma_start(dst[:], a[name]).then_inc(s_w, 16)
                with sp.Fori(0, CPB) as c:
                    for b in range(B):
                        banks.wait_read(sp, c - 1, ("att", b))
                        sp.dma_start(xin[:, b, :], x_in[b, :, bass.ds(c * T, T)]).then_inc(loaded[b], 16)
                        sp.dma_start(qin[:, b, :], q_in[b, :, bass.ds(c * T, T)]).then_inc(loaded[b], 16)

            @block.gpsimd
            def _(pool):
                pool.wait_ge(started, 1)
                with pool.Fori(0, CPB) as c:
                    def blocks(b, variant, first):
                        return states[:, b, variant, bass.ds(c * 2 + first, 2), :]
                    for b in range(B):
                        banks.wait_read(pool, c - 1, ("att", b))
                        nc.gpsimd.tensor_tensor(W[:, b, 0, :, :], blocks(b, 1, 0), blocks(b, 0, 1),
                                                ALU.add).then_inc(W_step, 1)
                        pool.wait_ge(W_step, (c * B + b) * 2 + 1)
                        nc.gpsimd.tensor_tensor(W[:, b, 1, :, :], W[:, b, 0, :, :], blocks(b, 2, 2),
                                                ALU.add).then_inc(W_step, 1)

            @block.tensor
            def _(pe):
                pe.wait_ge(started, 1)
                pe.wait_ge(s_w, 16 * 3)
                with pe.Fori(0, CPB) as c:
                    def fill(use, body, *inputs):
                        banks.wait_to_fill(pe, c, use, inputs)
                        body(banks.tile(use)).then_inc(banks.filled, 1)

                    for b in range(B):
                        pe.wait_ge(loaded[b], 32 * (c + 1))
                        pe.wait_ge(W_step, (c * B + b) * 2 + 2)
                        def att(p):
                            for h in range(2):
                                s_ = slice(h * 256, (h + 1) * 256)
                                i = nc.tensor.matmul(p[:, s_], W[:, b, 1, h, :], qin[:, b, s_], start=True, stop=True)
                            return i
                        fill(("att", b), att)
                    for b in range(B):
                        fill(("turn2", b), lambda p: turn(nc, p, x5[:, b, :], ident), ("att", b))
                    for what, b in BACK_AND_GATE:
                        if what == "back2":
                            fill(("back2", b), lambda p: turn(nc, p, tok2[:, b, :], ident), ("turn2", b))
                        else:
                            r = 64 * (b % 2)
                            fill(("gate", b), lambda p: nc.tensor.matmul(p[r:r + 64, :], gwT[:], ch2[:, b, :],
                                                                         start=True, stop=True), ("back2", b))

            @block.scalar
            def _(act):
                with act.Fori(0, CPB) as c:
                    for b in range(B):
                        banks.wait_read(act, c, ("att", b))
                        act.dma_start(x_out[b, :, bass.ds(c * T, T)], x5[:, b, :]).then_inc(x_stored[b], 16)
                    norm.scalar(nc, act, c)
                    for what, b in BACK_AND_GATE:
                        banks.wait_filled(act, c, (what, b))
                        if what == "back2":
                            nc.scalar.copy(ch2[:, b, :], banks.tile((what, b))).then_inc(banks.release((what, b)), 1)
                        else:
                            r = 64 * (b % 2)
                            nc.scalar.activation(logits[r:r + 64, b // 2, bass.ds(c * T, T)],
                                                 banks.tile((what, b))[r:r + 64, :], ACT.Identity,
                                                 bias=gb[r:r + 64, :]).then_inc(banks.release((what, b)), 1)
                    for b in range(B):
                        banks.wait_read(act, c, ("turn2", b))
                        act.dma_start(xt_out[b, bass.ds(c * T, T), :].rearrange("(t p) d -> p t d", p=128),
                                      tok2[:, b, :].rearrange("p (t d) -> p t d", d=C)).then_inc(t_stored[b], 16)
                for b in range(B):
                    act.wait_ge(x_stored[b], 16 * (CPB + 1))
                    act.wait_ge(t_stored[b], 16 * (CPB + 1))

            @block.vector
            def _(dve):
                n = 0
                for s in banks.free:
                    nc.vector.memset(tick[:, n:n + 1], 0.0).then_inc(s, OFF)
                    n += 1
                for s in x_stored:
                    nc.vector.memset(tick[:, n:n + 1], 0.0).then_inc(s, 16)
                    n += 1
                for s in t_stored[:3]:
                    nc.vector.memset(tick[:, n:n + 1], 0.0).then_inc(s, 16)
                    n += 1
                nc.vector.memset(tick[:, n:n + 1], 0.0).then_inc(t_stored[3], 16)
                nc.vector.memset(x5[:, 0, 0:1], 0.0).then_inc(started, 1)
                dve.wait_ge(started, 1)
                with dve.Fori(0, CPB) as c:
                    for b in range(B):
                        banks.wait_filled(dve, c, ("att", b))
                        dve.wait_ge(x_stored[b], 16 * (c + 1))
                        nc.vector.tensor_tensor(x5[:, b, :], banks.tile(("att", b)), xin[:, b, :],
                                                ALU.add).then_inc(banks.release(("att", b)), 1)
                    for b in range(B):
                        dve.wait_ge(t_stored[b], 16 * (c + 1))
                    norm.vector(nc, dve, banks, c, "turn2", lambda b, t: tok2[:, b, t * 128:(t + 1) * 128])


def experts(nc, a, tag, x_in, xt, logits, x_out):
    NE, H = 64, 512
    G = 4
    NG = NE // G
    NB = 4
    HT = H // 128
    P2 = B // 2
    w1, w2 = a[tag + "w1"], a[tag + "w2"]
    with ExitStack() as ctx:
        def sb(name, shape, dt=F32):
            return ctx.enter_context(nc.sbuf_tensor(tag + name, shape, dt))

        sem = Semaphores(nc, tag)
        ctx.callback(sem.clear)

        W1 = sb("W1", [128, NB, G, H])
        W2 = sb("W2", [128, NB, G, HT * C])
        b1 = sb("b1", [128, NE * HT])
        b2 = sb("b2", [128, NE])
        ident = sb("ident", [128, 128])
        acc = sb("acc", [128, P2, C])
        pT = sb("pT", [128, NE, B])
        oT = sb("oT", [128, B, NE])
        oE = sb("oE", [128, B, C])
        tick = sb("tick", [128, 32])
        s_w = sem("weights")
        w_loaded = [sem(f"w_loaded{i}") for i in range(NB)]

        def load_group(sp, g, buf):
            sp.dma_start(W1[:, buf, :, :], w1[bass.ds(g * G, G), 0:C, :].rearrange("e d h -> d e h")
                         ).then_inc(w_loaded[buf], 16)
            sp.dma_start(W2[:, buf, :, :], w2[bass.ds(g * G, G), 0:H, :].rearrange("e (p m) o -> p e (m o)", m=HT)
                         ).then_inc(w_loaded[buf], 16)

        names = [(w, par, p) for par in range(2) for w in ("mturn", "pool") for p in range(P2)]
        with ExitStack() as c1:
            def sb1(name, shape, dt=F32):
                return c1.enter_context(nc.sbuf_tensor(tag + name, shape, dt))

            banks = Banks(nc, c1, sem, tag + "s_", names, 8)
            rest = sb1("rest", [128, P2, L])
            xtb = sb1("xtb", [128, 2, B, T])
            ms = sb1("ms", [128, 2, P2, T])
            mT = sb1("mT", [128, 2, P2, T])
            sc = sb1("sc", [128, P2, 8])
            top = sb1("top", [128, P2, 8])
            SEL = 8
            sel = [sem(f"select_step{p}") for p in range(P2)]; acc_zero = sem("acc_zero")
            started = sem("started"); ms_ready = sem("ms_ready")
            x_loaded = [sem("x_loaded0"), sem("x_loaded1")]
            with nc.Block() as block:

                @block.sync
                def _(sp):
                    sp.dma_start(ident[:], a["ident"]).then_inc(s_w, 16)
                    sp.dma_start(b1[:], a[tag + "b1"]).then_inc(s_w, 16)
                    sp.dma_start(b2[:], a[tag + "b2"]).then_inc(s_w, 16)
                    for buf in range(NB):
                        load_group(sp, buf, buf)
                    with sp.Fori(0, CPB // 2) as c2:
                        for par in range(2):
                            for p in range(P2):
                                banks.wait_read(sp, c2 - 1, ("pool", par, p))
                            for b in range(B):
                                sp.dma_start(xtb[:, par, b, :].rearrange("p (t d) -> p t d", d=C),
                                             xt[b, bass.ds((c2 * 2 + par) * T, T), :].rearrange(
                                                 "(t p) d -> p t d", p=128)).then_inc(x_loaded[par], 16)

                @block.vector
                def _(dve):
                    n = 0
                    for s in banks.free:
                        nc.vector.memset(tick[:, n:n + 1], 0.0).then_inc(s, OFF)
                        n += 1
                    nc.vector.memset(tick[:, n:n + 1], 0.0).then_inc(ms_ready, OFF)
                    nc.vector.memset(acc[:], 0.0).then_inc(acc_zero, 1)
                    nc.vector.memset(tick[:, n + 1:n + 2], 0.0).then_inc(started, 1)

                    def step(p, k, op):
                        dve.wait_ge(sel[p], k - 1)
                        op().then_inc(sel[p], 1)

                    for p in range(P2):
                        nc.vector.reduce_max(sc[:, p, 0:1], logits[:, p, :], AX_X).then_inc(sel[p], 1)
                        step(p, 2, lambda: nc.vector.tensor_scalar(sc[:, p, 1:2], sc[:, p, 0:1], -1.0, None, ALU.mult))
                    for p in range(P2):
                        lg = logits[:, p, :]
                        step(p, 4, lambda: nc.vector.reciprocal(sc[:, p, 3:4], sc[:, p, 2:3]))
                        step(p, 5, lambda: nc.vector.tensor_scalar(lg, lg, sc[:, p, 3:4], None, ALU.mult))
                        step(p, 6, lambda: nc.vector.max(top[:, p, :], lg))
                        step(p, 7, lambda: nc.vector.match_replace(rest[:, p, :], top[:, p, :], lg, 0.0))
                        if p == P2 - 1:
                            step(p, SEL, lambda: nc.vector.tensor_tensor(lg, lg, rest[:, p, :], ALU.subtract))
                    dve.wait_ge(acc_zero, 1)
                    with dve.Fori(0, CPB // 2) as c2:
                        for par in range(2):
                            for p in range(P2):
                                banks.wait_filled(dve, c2, ("mturn", par, p))
                                nc.vector.tensor_copy(mT[:, par, p, :], banks.tile(("mturn", par, p))).then_inc(
                                    banks.release(("mturn", par, p)), 1)
                            for p in range(P2):
                                banks.wait_filled(dve, c2, ("pool", par, p))
                                banks.wait_read(dve, c2 - (par == 0), ("pool", 1 - par, p))
                                nc.vector.tensor_tensor(acc[:, p, :], acc[:, p, :],
                                                        banks.tile(("pool", par, p))[:, 0:C],
                                                        ALU.add).then_inc(banks.release(("pool", par, p)), 1)

                @block.gpsimd
                def _(pool):
                    for p in range(P2 - 1):
                        pool.wait_ge(sel[p], SEL - 1)
                        nc.gpsimd.tensor_tensor(logits[:, p, :], logits[:, p, :], rest[:, p, :],
                                                ALU.subtract).then_inc(sel[p], 1)

                @block.scalar
                def _(act):
                    for p in range(P2):
                        act.wait_ge(sel[p], 2)
                        nc.scalar.activation(logits[:, p, :], logits[:, p, :], ACT.Exp, bias=sc[:, p, 1:2],
                                             accum_out=sc[:, p, 2:3]).then_inc(sel[p], 1)
                    for p in range(P2):
                        act.wait_ge(sel[p], SEL)
                    with act.Fori(0, CPB // 2) as c2:
                        for par in range(2):
                            for p in range(P2):
                                banks.wait_read(act, c2 - 1, ("mturn", par, p))
                                nc.scalar.copy(ms[:, par, p, :], logits[:, p, bass.ds((c2 * 2 + par) * T, T)]
                                               ).then_inc(ms_ready, 1)

                @block.tensor
                def _(pe):
                    pe.wait_ge(s_w, 48)
                    pe.wait_ge(started, 1)
                    with pe.Fori(0, CPB // 2) as c2:
                        for par in range(2):
                            for p in range(P2):
                                use = ("mturn", par, p)
                                pe.wait_ge(ms_ready, done((c2 * 2 + par) * P2 + p + 1))
                                banks.wait_free(pe, c2, use)
                                turn(nc, banks.tile(use), ms[:, par, p, :], ident).then_inc(banks.filled, 1)
                            pe.wait_ge(x_loaded[par], 16 * B * (c2 + 1))
                            for p in range(P2):
                                use = ("pool", par, p)
                                banks.wait_to_fill(pe, c2, use, [("mturn", par, p)])
                                for h in range(2):
                                    for t in range(TPC):
                                        i = nc.tensor.matmul(
                                            banks.tile(use)[64 * h:64 * h + 64, 0:C],
                                            mT[:, par, p, t * 128 + 64 * h:t * 128 + 64 * h + 64],
                                            xtb[:, par, 2 * p + h, t * 128:(t + 1) * 128],
                                            start=(t == 0), stop=(t == TPC - 1))
                                i.then_inc(banks.filled, 1)

        with ExitStack() as c1:
            def sb1(name, shape, dt=F32):
                return c1.enter_context(nc.sbuf_tensor(tag + name, shape, dt))

            pP = c1.enter_context(nc.psum_tensor(tag + "pP", [128, P2, C], F32))
            pH = c1.enter_context(nc.psum_tensor(tag + "pH", [128, 2, T], F32))
            pO = c1.enter_context(nc.psum_tensor(tag + "pO", [128, 2, T], F32))
            hb = sb1("hb", [128, 2, G * HT, B])
            hg = sb1("hg", [128, 2, G * HT, B])
            pt_full = sem("pt_full"); pt_ready = sem("pt_ready"); pt_free = sem("pt_free")
            h_full = sem("h_full"); hb_ready = sem("hb_ready"); hg_ready = sem("hg_ready")
            o_full = sem("o_full"); o_ready = sem("o_ready")
            ot_full = sem("ot_full"); oe_ready = sem("oe_ready"); zero = sem("oe_zero")
            with nc.Block() as block:

                @block.sync
                def _(sp):
                    with sp.Fori(1, NG // NB) as k:
                        for buf in range(NB):
                            sp.wait_ge(o_full, (k - 1) * NB + buf + 1)
                            load_group(sp, k * NB + buf, buf)

                @block.tensor
                def _(pe):
                    for p in range(P2):
                        i = nc.tensor.transpose(pP[:, p, :], acc[:, p, :], ident[:])
                    i.then_inc(pt_full, 1)
                    pe.wait_ge(pt_ready, 1)
                    with pe.Fori(0, NG // NB) as k:
                        def hidden(buf):
                            g, par = k * NB + buf, buf % 2
                            pe.wait_ge(w_loaded[buf], 32 * (k + 1))
                            pe.wait_ge(hb_ready, done(g - 1))
                            for e in range(G):
                                for m in range(HT):
                                    j = (e * HT + m) * B
                                    i = nc.tensor.matmul(
                                        pH[:, par, j:j + B], W1[:, buf, e, m:H:HT],
                                        pT[:, bass.ds(g * G + e, 1), :].rearrange("p o b -> p (o b)"),
                                        start=True, stop=True)
                            i.then_inc(h_full, 1)

                        def output(buf):
                            g, par = k * NB + buf, buf % 2
                            pe.wait_ge(hg_ready, g + 1)
                            pe.wait_ge(o_ready, done(g - 1))
                            for e in range(G):
                                for m in range(HT):
                                    i = nc.tensor.matmul(pO[:, par, e * B:(e + 1) * B],
                                                         W2[:, buf, e, m * C:(m + 1) * C],
                                                         hg[:, par, e * HT + m, :],
                                                         start=(m == 0), stop=(m == HT - 1))
                            i.then_inc(o_full, 1)

                        hidden(0)
                        for buf in range(1, NB):
                            hidden(buf)
                            output(buf - 1)
                        output(NB - 1)
                    pe.wait_ge(o_ready, done(NG))
                    pe.wait_ge(pt_ready, 1)
                    for p in range(P2):
                        i = nc.tensor.transpose(pP[:, p, :], oT[:, 2 * p:2 * p + 2, :].rearrange("p b e -> p (b e)"),
                                                ident[:])
                    i.then_inc(ot_full, 1)

                @block.scalar
                def _(act):
                    with act.Fori(0, NG // NB) as k:
                        for buf in range(NB):
                            g, par = k * NB + buf, buf % 2
                            act.wait_ge(hb_ready, done(g + 1))
                            nc.scalar.activation(hg[:, par, :, :], hb[:, par, :, :], ACT.Gelu).then_inc(hg_ready, 1)

                @block.vector
                def _(dve):
                    nc.vector.memset(tick[:, 20:21], 0.0).then_inc(hb_ready, OFF)
                    nc.vector.memset(tick[:, 21:22], 0.0).then_inc(o_ready, OFF)
                    nc.vector.memset(oE[:], 0.0).then_inc(zero, 1)
                    dve.wait_ge(pt_full, 1)
                    nc.vector.tensor_copy(pT[:].rearrange("p e b -> p b e"),
                                          pP[:].rearrange("p a (b e) -> p (a b) e", e=NE)).then_inc(pt_ready, 1)
                    with dve.Fori(0, NG // NB) as k:
                        def hidden(buf):
                            g, par = k * NB + buf, buf % 2
                            dve.wait_ge(h_full, g + 1)
                            dve.wait_ge(o_ready, done(g - 1))
                            nc.vector.tensor_tensor(hb[:, par, :, :],
                                                    pH[:, par, 0:G * HT * B].rearrange("p (j b) -> p j b", b=B),
                                                    b1[:, bass.ds(g * (G * HT), G * HT)].unsqueeze(2).to_broadcast(
                                                        [128, G * HT, B]), ALU.add).then_inc(hb_ready, 1)

                        def output(buf):
                            g, par = k * NB + buf, buf % 2
                            dve.wait_ge(o_full, g + 1)
                            nc.vector.tensor_tensor(oT[:, :, bass.ds(g * G, G)],
                                                    pO[:, par, 0:G * B].rearrange("p (e b) -> p b e", b=B),
                                                    b2[:, bass.ds(g * G, G)].unsqueeze(1).to_broadcast([128, B, G]),
                                                    ALU.add).then_inc(o_ready, 1)

                        hidden(0)
                        for buf in range(1, NB):
                            hidden(buf)
                            output(buf - 1)
                        output(NB - 1)
                    dve.wait_ge(ot_full, 1)
                    dve.wait_ge(zero, 1)
                    for b in range(B):
                        r = 64 * (b % 2)
                        nc.vector.tensor_copy(oE[r:r + 64, b, :], pP[r:r + 64, b // 2, :]).then_inc(oe_ready, 1)

        names = [("give", b) for b in range(B)] + [("give2", b) for b in range(B)]
        with ExitStack() as c1:
            banks = Banks(nc, c1, sem, tag + "g_", names, 8)
            xin = c1.enter_context(nc.sbuf_tensor(tag + "xin", [128, 2, B, T], F32))
            xo = c1.enter_context(nc.sbuf_tensor(tag + "xo", [128, 2, B, T], F32))
            loaded = [[sem(f"gl{p}{b}") for b in range(B)] for p in range(2)]
            stored = [[sem(f"gs{p}{b}") for b in range(B)] for p in range(2)]
            go = sem("go")
            WHICH = ("give", "give2")
            with nc.Block() as block:

                @block.sync
                def _(sp):
                    sp.wait_ge(go, 1)
                    with sp.Fori(0, CPB // 2) as c2:
                        for par in range(2):
                            for b in range(B):
                                banks.wait_read(sp, c2 - 1, (WHICH[par], b))
                                sp.dma_start(xin[:, par, b, :], x_in[b, :, bass.ds((c2 * 2 + par) * T, T)]
                                             ).then_inc(loaded[par][b], 16)

                @block.tensor
                def _(pe):
                    pe.wait_ge(go, 1)
                    with pe.Fori(0, CPB // 2) as c2:
                        for par in range(2):
                            for b in range(B):
                                use = (WHICH[par], b)
                                banks.wait_free(pe, c2, use)
                                nc.tensor.matmul(banks.tile(use), oE[:, b, :],
                                                 logits[:, b // 2, bass.ds((c2 * 2 + par) * T, T)],
                                                 start=True, stop=True).then_inc(banks.filled, 1)

                @block.vector
                def _(dve):
                    n = 0
                    for s in banks.free:
                        nc.vector.memset(tick[:, n:n + 1], 0.0).then_inc(s, OFF)
                        n += 1
                    for s in stored[0] + stored[1]:
                        nc.vector.memset(tick[:, n:n + 1], 0.0).then_inc(s, 16)
                        n += 1
                    nc.vector.memset(tick[:, n:n + 1], 0.0).then_inc(go, 1)
                    with dve.Fori(0, CPB // 2) as c2:
                        for par in range(2):
                            for b in range(B):
                                use = (WHICH[par], b)
                                banks.wait_filled(dve, c2, use)
                                dve.wait_ge(loaded[par][b], 16 * (c2 + 1))
                                dve.wait_ge(stored[par][b], 16 * (c2 + 1))
                                nc.vector.tensor_tensor(xo[:, par, b, :], banks.tile(use), xin[:, par, b, :],
                                                        ALU.add).then_inc(banks.release(use), 1)

                @block.scalar
                def _(act):
                    act.wait_ge(go, 1)
                    with act.Fori(0, CPB // 2) as c2:
                        for par in range(2):
                            for b in range(B):
                                banks.wait_read(act, c2, (WHICH[par], b))
                                act.dma_start(x_out[b, :, bass.ds((c2 * 2 + par) * T, T)], xo[:, par, b, :]
                                              ).then_inc(stored[par][b], 16)
                    for par in range(2):
                        for b in range(B):
                            act.wait_ge(stored[par][b], 16 * (CPB // 2 + 1))




def build_program(nc, a, out):
    def scratch(name, shape):
        return nc.dram_tensor(name, shape, F32, kind="Internal").ap()

    x1, pre, x3, x4, x5 = (scratch(n, (B, C, L)) for n in ("x1", "pre", "x3", "x4", "x5"))
    xt, q = scratch("xt", (B, L, C)), scratch("q", (B, C, L))
    mamba(nc, a, a["x"], x1)
    with nc.sbuf_tensor("bn_stats", [C, NCH, 6], F32) as bn_stats:
        hypergraph(nc, a, x1, pre, bn_stats)
        with nc.sbuf_tensor("logits2", [128, B // 2, L], F32) as logits:
            linear_attention(nc, a, bn_stats, x1, pre, x3, xt, logits)
            experts(nc, a, "ffn2_", x3, xt, logits, x4)
    with nc.sbuf_tensor("logits3", [128, B // 2, L], F32) as logits:
        with nc.sbuf_tensor("states", [128, B, 3, 2 * CPB + 2, 128], F32) as states:
            window_states(nc, a, x4, q, states)
            window_attention(nc, a, x4, q, states, x5, xt, logits)
        experts(nc, a, "ffn3_", x5, xt, logits, out)


def kernel(**inputs):
    import numpy as np
    import concourse.bacc as bacc
    from concourse.bass_utils import run_bass_kernel_spmd

    def t(name, shape=None):
        v = np.asarray(inputs[name])
        return np.ascontiguousarray(v if shape is None else shape(v))

    xp = np.asarray(inputs["L0_conv_x_proj_w"]).T
    bc = xp[:, DR:]
    arrays = {
        "x": t("x", lambda v: v.reshape(B, C, L)),
        "ident": np.eye(128, dtype=np.float32),
        "L0_conv_proj_w": t("L0_conv_proj_w"),
        "in_projT": t("L0_conv_in_proj_w", lambda v: v.T),
        "conv_wT": t("L0_conv_conv_w", lambda v: v.reshape(DI, DK).T),
        "x_projT": np.ascontiguousarray(np.concatenate([bc, bc, bc, xp[:, :DR]], axis=1)),
        "dt_projT": t("L0_conv_dt_proj_w", lambda v: v.T),
        "out_projT": t("L0_conv_out_proj_w", lambda v: v.T),
        "conv_b": t("L0_conv_conv_b", lambda v: v.reshape(2, 128).T),
        "dt_b": t("L0_conv_dt_proj_b", lambda v: v.reshape(2, 128).T),
        "D": t("L0_conv_D", lambda v: v.reshape(2, 128).T),
        "A_log": t("L0_conv_A_log"),
        "gmean": np.kron(np.eye(C // 4, dtype=np.float32), np.full((4, 4), 0.25, np.float32)),
        "W_fcT": t("L1_conv_W_fc", lambda v: v.T),
        "gamma_beta": np.ascontiguousarray(np.stack([inputs["L1_conv_gamma"], inputs["L1_conv_beta"]], axis=1)),
        "mask": np.triu(np.ones((128, 128), np.float32)),
        "attn2_wT": t("L2_attn_W", lambda v: v.T),
        "attn2_bqk": t("L2_attn_b", lambda v: v[:2 * C].reshape(2, C).T),
        "attn2_bv": t("L2_attn_b", lambda v: v[2 * C:]),
        "attn3_wT": np.ascontiguousarray(np.concatenate([np.asarray(inputs[f"L3_attn_W{w}"]).T for w in "qkv"], axis=1)),
        "attn3_bq": t("L3_attn_bq", lambda v: v.reshape(C, 1)),
        "attn3_bkv": np.ascontiguousarray(np.stack([inputs["L3_attn_bk"], inputs["L3_attn_bv"]])),
        "ends": np.stack([np.arange(128) > 0, np.arange(128) < 127], axis=1).astype(np.float32),
        "b_fc": t("L1_conv_b_fc", lambda v: v.reshape(C, 1)),
    }
    for n in (2, 3):
        f, g = f"L{n}_ffn_", f"ffn{n}_"
        arrays[g + "gwT"] = t(f + "gate_w", lambda v: v.T)
        arrays[g + "gb"] = t(f + "gate_b", lambda v: np.concatenate([v, v]).reshape(128, 1))
        arrays[g + "w1"] = t(f + "weight1")
        arrays[g + "w2"] = t(f + "weight2")
        arrays[g + "b1"] = t(f + "weight1", lambda v: v[:, C, :].reshape(64, 128, 4).transpose(1, 0, 2).reshape(128, 256))
        arrays[g + "b2"] = t(f + "weight2", lambda v: v[:, 512, :].T)
    nc = bacc.Bacc("TRN2", target_bir_lowering=False, num_devices=1)
    a = {k: nc.dram_tensor("in_" + k, v.shape, F32, kind="ExternalInput").ap() for k, v in arrays.items()}
    out = nc.dram_tensor("out_x", (B, C, L), F32, kind="ExternalOutput").ap()
    build_program(nc, a, out)
    r = run_bass_kernel_spmd(nc, [{"in_" + k: v for k, v in arrays.items()}], core_ids=[0])
    return r.results[0]["out_x"].reshape(B, C, 64, 64)
```
